# Optimizing a Trainium2 kernel written in Bass

```python
import numpy as np
import jax
import jax.numpy as jnp

def _softmax(x, axis=-1):
    return jax.nn.softmax(x, axis=axis)

def _gelu(x):
    return jax.nn.gelu(x, approximate=True)

def _silu(x):
    return jax.nn.silu(x)

def _sigmoid(x):
    return jax.nn.sigmoid(x)

def _layernorm(x, axis=-1, eps=1e-05):
    m = jnp.mean(x, axis=axis, keepdims=True)
    v = jnp.var(x, axis=axis, keepdims=True)
    return (x - m) / jnp.sqrt(v + eps)

def _scatter_add(tgt, idx, src, axis=0):
    return tgt.at[idx].add(src)

def _segment_sum(src, seg, n):
    return jax.ops.segment_sum(src, seg, n)
kernel_name = 'mk_decoder_preln_d1_seqx_r4_8e9115'

def setup_inputs(seed: int=0):
    np.random.seed(seed)
    _w = jnp.asarray

    def _rec_inputs():
        import jax
        import jax.numpy as jnp
        _rk = jax.random.key(seed)
        x = -0.0002928 + 1 * jax.random.normal(jax.random.fold_in(_rk, 1), (2, 1024, 256), jnp.float32)
        _lenS = 1024 - jax.random.randint(jax.random.fold_in(_rk, 7), (2,), 0, max(1, 1024 // 4) + 1, jnp.int32)
        _lenS2 = 77 - jax.random.randint(jax.random.fold_in(_rk, 8), (2,), 0, max(1, 77 // 4) + 1, jnp.int32)
        _ctx_1024P = jax.random.normal(jax.random.fold_in(_rk, 11), (2, 16, 256), jnp.float32)
        _ctx_1024c = jax.random.dirichlet(jax.random.fold_in(_rk, 511), 0.3 * jnp.ones((16,), jnp.float32), (2, 77))
        _ctx_1024t = jnp.einsum('bsk,bkd->bsd', _ctx_1024c, _ctx_1024P)
        _ctx_1024t = _ctx_1024t * jax.lax.rsqrt(jnp.mean(jnp.square(_ctx_1024t)) + 1e-12) * 0.953939
        ctx_1024 = -1.39393e-06 + 0.999914 * (_ctx_1024t + 0.3 * jax.random.normal(jax.random.fold_in(_rk, 611), (2, 77, 256), jnp.float32))
        return (x, ctx_1024)
    x, ctx_1024 = _rec_inputs()

    def _L0_attn_setup():
        import jax, jax.numpy as jnp
        import numpy as np
        N_EMBD = 256
        N_HEAD = 16
        HEAD_DIM = N_EMBD // N_HEAD
        LATENT_DIM = N_EMBD // 2
        B, T = (4, 512)
        key = jax.random.key(seed)
        ks = jax.random.split(key, 5)

        def init(k, fan_in, fan_out):
            bound = 1.0 / np.sqrt(fan_in)
            return jax.random.uniform(k, (fan_in, fan_out), jnp.float32, -bound, bound)
        return {'x': jax.random.normal(ks[0], (B, T, N_EMBD), jnp.float32), 'Wc_down': init(ks[1], N_EMBD, LATENT_DIM), 'Wq_up': init(ks[2], LATENT_DIM, N_EMBD), 'Wkv_up': init(ks[3], LATENT_DIM, 2 * HEAD_DIM), 'Wc_proj': init(ks[4], N_EMBD, N_EMBD)}
    _L0_attn_all = _L0_attn_setup()
    _L0_attn_in = {k: v for k, v in _L0_attn_all.items() if k in ('Wc_down', 'Wq_up', 'Wkv_up', 'Wc_proj')}
    del _L0_attn_all

    def _L0_xattn_setup():
        import jax, jax.numpy as jnp
        import numpy as np
        DIM = 256
        HEADS = 16
        HEAD_DIM = DIM // HEADS
        SCALE = HEAD_DIM ** (-0.5)
        B, N, S = (2, 512, 512)

        def _slice_head(x, W_qkv, b_qkv, idx):
            b, l, _ = x.shape
            qkv = (x @ W_qkv + b_qkv).reshape(b, l, 3, HEADS, HEAD_DIM)
            return jnp.transpose(qkv[:, :, idx], (0, 2, 1, 3))
        key = jax.random.key(seed)
        ks = jax.random.split(key, 5)
        return {'query': jax.random.normal(ks[0], (B, N, DIM), dtype=jnp.float32), 'key': jax.random.normal(ks[1], (B, S, DIM), dtype=jnp.float32), 'value': jax.random.normal(ks[2], (B, S, DIM), dtype=jnp.float32), 'W_qkv': jax.random.normal(ks[3], (DIM, 3 * DIM), dtype=jnp.float32) * DIM ** (-0.5), 'b_qkv': jnp.zeros((3 * DIM,), dtype=jnp.float32), 'W_out': jax.random.normal(ks[4], (DIM, DIM), dtype=jnp.float32) * DIM ** (-0.5), 'b_out': jnp.zeros((DIM,), dtype=jnp.float32)}
    _L0_xattn_all = _L0_xattn_setup()
    _L0_xattn_in = {k: v for k, v in _L0_xattn_all.items() if k in ('W_qkv', 'b_qkv', 'W_out', 'b_out')}
    del _L0_xattn_all

    def _L0_ffn_setup():
        import jax, jax.numpy as jnp
        import numpy as np
        B, S, D, E, F = (2, 256, 256, 14, 512)
        key = jax.random.key(seed)
        k0, k1, k2, k3 = jax.random.split(key, 4)
        h = jax.random.normal(k0, (B, S, D), jnp.float32)
        gate_w = jax.random.normal(k1, (E, D), jnp.float32) * 0.02
        w1 = jax.random.normal(k2, (E, D, F), jnp.float32) * (1.0 / np.sqrt(D).astype(np.float32))
        b1 = jnp.zeros((E, F), jnp.float32)
        w2 = jax.random.normal(k3, (E, F, D), jnp.float32) * (1.0 / np.sqrt(F).astype(np.float32))
        b2 = jnp.zeros((E, D), jnp.float32)
        return {'h': h, 'gate_w': gate_w, 'w1': w1, 'b1': b1, 'w2': w2, 'b2': b2}
    _L0_ffn_all = _L0_ffn_setup()
    _L0_ffn_in = {k: v for k, v in _L0_ffn_all.items() if k in ('gate_w', 'w1', 'b1', 'w2', 'b2')}
    del _L0_ffn_all
    return {'x': x, 'ctx_1024': ctx_1024, 'L0_attn_Wc_down': _L0_attn_in['Wc_down'], 'L0_attn_Wq_up': _L0_attn_in['Wq_up'], 'L0_attn_Wkv_up': _L0_attn_in['Wkv_up'], 'L0_attn_Wc_proj': _L0_attn_in['Wc_proj'], 'L0_xattn_W_qkv': _L0_xattn_in['W_qkv'], 'L0_xattn_b_qkv': _L0_xattn_in['b_qkv'], 'L0_xattn_W_out': _L0_xattn_in['W_out'], 'L0_xattn_b_out': _L0_xattn_in['b_out'], 'L0_ffn_gate_w': _L0_ffn_in['gate_w'], 'L0_ffn_w1': _L0_ffn_in['w1'], 'L0_ffn_b1': _L0_ffn_in['b1'], 'L0_ffn_w2': _L0_ffn_in['w2'], 'L0_ffn_b2': _L0_ffn_in['b2']}

def reference(x, ctx_1024, L0_attn_Wc_down, L0_attn_Wq_up, L0_attn_Wkv_up, L0_attn_Wc_proj, L0_xattn_W_qkv, L0_xattn_b_qkv, L0_xattn_W_out, L0_xattn_b_out, L0_ffn_gate_w, L0_ffn_w1, L0_ffn_b1, L0_ffn_w2, L0_ffn_b2):
    import jax
    import jax.numpy as jnp

    def _L0_attn_ref(x, Wc_down, Wq_up, Wkv_up, Wc_proj):
        import jax, jax.numpy as jnp
        import numpy as np
        N_EMBD = 256
        N_HEAD = 16
        HEAD_DIM = N_EMBD // N_HEAD
        LATENT_DIM = N_EMBD // 2
        B, T = (4, 512)
        Bsz, Tlen, C = x.shape
        latent = x @ Wc_down
        q = (latent @ Wq_up).reshape(Bsz, Tlen, N_HEAD, HEAD_DIM)
        kv = latent @ Wkv_up
        k, v = (kv[..., :HEAD_DIM], kv[..., HEAD_DIM:])
        scale = 1.0 / np.sqrt(HEAD_DIM)
        att = jnp.einsum('bthd,bsd->bhts', q, k) * scale
        causal = jnp.tril(jnp.ones((Tlen, Tlen), dtype=bool))
        att = jnp.where(causal[None, None], att, -jnp.inf)
        att = jax.nn.softmax(att, axis=-1)
        y = jnp.einsum('bhts,bsd->bthd', att, v).reshape(Bsz, Tlen, C)
        return y @ Wc_proj

    def _L0_xattn_ref(query, key, value, W_qkv, b_qkv, W_out, b_out):
        import jax, jax.numpy as jnp
        import numpy as np
        DIM = 256
        HEADS = 16
        HEAD_DIM = DIM // HEADS
        SCALE = HEAD_DIM ** (-0.5)
        B, N, S = (2, 512, 512)

        def _slice_head(x, W_qkv, b_qkv, idx):
            b, l, _ = x.shape
            qkv = (x @ W_qkv + b_qkv).reshape(b, l, 3, HEADS, HEAD_DIM)
            return jnp.transpose(qkv[:, :, idx], (0, 2, 1, 3))
        q = _slice_head(query, W_qkv, b_qkv, 0)
        k = _slice_head(key, W_qkv, b_qkv, 1)
        v = _slice_head(value, W_qkv, b_qkv, 2)
        attn = jnp.einsum('bhnd,bhsd->bhns', q, k) * SCALE
        attn = jax.nn.softmax(attn, axis=-1)
        out = jnp.einsum('bhns,bhsd->bhnd', attn, v)
        out = jnp.transpose(out, (0, 2, 1, 3)).reshape(query.shape[0], query.shape[1], DIM)
        return out @ W_out + b_out

    def _L0_ffn_ref(h, gate_w, w1, b1, w2, b2):
        import jax, jax.numpy as jnp
        import numpy as np
        B, S, D, E, F = (2, 256, 256, 14, 512)
        Bb, Ss, Dd = h.shape
        x = h.reshape(Bb * Ss, Dd)
        logits = x @ gate_w.T
        probs = jax.nn.softmax(logits, axis=-1)
        top2_p, top2_i = jax.lax.top_k(probs, 2)
        w = top2_p / jnp.maximum(top2_p.sum(-1, keepdims=True), 1e-10)
        hh = jnp.einsum('nd,edf->nef', x, w1) + b1
        hh = jax.nn.gelu(hh, approximate=False)
        all_out = jnp.einsum('nef,efd->ned', hh, w2) + b2
        n = jnp.arange(x.shape[0])
        out0 = all_out[n, top2_i[:, 0]]
        out1 = all_out[n, top2_i[:, 1]]
        moe_out = w[:, 0:1] * out0 + w[:, 1:2] * out1
        result = jnp.clip(x + moe_out, -100.0, 100.0).reshape(Bb, Ss, Dd)
        return result
    x = x + _L0_attn_ref(_layernorm(x, axis=-1), L0_attn_Wc_down, L0_attn_Wq_up, L0_attn_Wkv_up, L0_attn_Wc_proj)
    x = x + _L0_xattn_ref(_layernorm(x, axis=-1), ctx_1024, ctx_1024, L0_xattn_W_qkv, L0_xattn_b_qkv, L0_xattn_W_out, L0_xattn_b_out)
    x = x + _L0_ffn_ref(_layernorm(x, axis=-1), L0_ffn_gate_w, L0_ffn_w1, L0_ffn_b1, L0_ffn_w2, L0_ffn_b2)
    return x

_drawn_inputs = setup_inputs


def setup_inputs(seed=0):
    import zlib

    import numpy as np

    out = dict(_drawn_inputs(seed))
    spreads = {'L0_xattn_b_qkv': (0.0, 0.1),
     'L0_xattn_b_out': (0.0, 0.1),
     'L0_ffn_b1': (0.0, 0.355),
     'L0_ffn_b2': (0.0, 0.1)}
    factors = {'L0_attn_Wq_up': 6.48}
    for name, (base, spread) in spreads.items():
        noise = np.random.default_rng([zlib.crc32(name.encode()), seed]).standard_normal(out[name].shape)
        drawn = base * np.exp(spread * noise) if base else spread * noise
        out[name] = jnp.asarray(drawn.astype(out[name].dtype))
    for name, factor in factors.items():
        out[name] = (out[name] * factor).astype(out[name].dtype)
    return out
```

```python
from contextlib import ExitStack

import concourse.bass as bass
from concourse import mybir

ALU = mybir.AluOpType
ACT = mybir.ActivationFunctionType
BF16 = mybir.dt.bfloat16
F32 = mybir.dt.float32
AX_X = mybir.AxisListType.X

P = 128
EPS = 1e-5
CREDIT = 1
BIG = -1.0e30
SPLIT = 6


def decoder_layer(nc, x, ctx_in, w_down, w_qup, w_kvup, w_proj, w_qkv, b_qkv, w_out, b_out,
                  gate_w, w1, b1, w2, b2, out):
    B, T, D = x.shape
    S = ctx_in.shape[1]
    E, _, F = w1.shape
    HD = w_kvup.shape[1] // 2
    H = D // HD
    LAT = w_down.shape[1]
    C = D // P
    FC = F // P
    NT = T // P
    N = B * NT
    KQ = SPLIT * HD
    KM = KQ + 3
    HV = HD + 1
    HG = 4
    G = H // HG
    SCALE = float(HD) ** -0.5
    SP = 80
    assert LAT == P and KQ <= 96 and HG * P == 512 and S <= SP

    with ExitStack() as stack:
        def sb(name, shape, dt=F32):
            return stack.enter_context(nc.sbuf_tensor(name, shape, dt))

        def sem(name):
            return stack.enter_context(nc.semaphore(name))

        ps = stack.enter_context(nc.psum_tensor("ps", [P, 8, 512], F32))

        def bank(k):
            return ps[:, k, :]

        X = sb("X", [P, N, D])
        wdown = sb("wdown", [P, C, LAT])
        wqkvup = sb("wqkvup", [P, D + 2 * HD])
        wproj = sb("wproj", [P, C, D])
        wqkv = sb("wqkv", [P, C, 3 * D])
        bqkv = sb("bqkv", [1, 3 * D])
        wout = sb("wout", [P, C, D])
        bout = sb("bout", [1, D])
        gateT = sb("gateT", [P, C, E])
        gaterow = sb("gaterow", [E, D])
        b2sb = sb("b2sb", [E, D])
        ident = sb("ident", [P, P])
        identb = sb("identb", [P, P], BF16)
        mask_ts = sb("mask_ts", [P, P], BF16)
        mask_st = sb("mask_st", [P, P], BF16)
        ones1 = sb("ones1", [1, P])
        halfneg = sb("halfneg", [P, N])
        stats = sb("stats", [P, NT, 6])
        mv = sb("mv", [P, NT, 2])
        ve = sb("ve", [P, NT])
        rstd = sb("rstd", [P, NT])
        XN = sb("XN", [P, NT, D])
        XT = sb("XT", [P, C, T])
        LT = sb("LT", [P, T])
        QF = sb("QF", [P, NT, D + 2 * HD])
        QX = sb("QX", [P, 2, H, SPLIT, HD], BF16)
        qrest = sb("qrest", [P, H, HD])
        KX = sb("KX", [P, NT, KQ + 16], BF16)
        krest = sb("krest", [P, NT, HD])
        VX = sb("VX", [P, N, 32])
        QT = sb("QT", [P, N, H, P], BF16)
        KT = sb("KT", [P, B, T], BF16)
        CX = sb("CX", [S, B, D])
        CT = sb("CT", [P, B, C, S])
        KV2 = sb("KV2", [S, B, 2 * D])
        KX2 = sb("KX2", [S, B, H, KQ + 16], BF16)
        krest2 = sb("krest2", [S, H, HD])
        V2X = sb("V2X", [S, B, H, HV])
        KT2 = sb("KT2", [P, B, H, SP], BF16)
        nmx = sb("nmx", [P, 2, 2, H])
        nm = sb("nm", [P, 2, H])
        mrest = sb("mrest", [P, H])
        MP = sb("MP", [P, 2, 3, H], BF16)
        MT = sb("MT", [3 * H, 2, P], BF16)
        PR = sb("PR", [P, 3, 2, 512])
        rinv = sb("rinv", [P, 2, H])
        YF = XT[:, 0, :].rearrange("p (a t) -> p a t", a=2)
        YN = sb("YN", [P, 2, D])
        YT = sb("YT", [P, 2, C, P])
        GT = sb("GT", [P, N, E])
        lg = sb("lg", [P, NT, E])
        scratch = sb("scratch", [P, 1])
        zerosH = sb("zerosH", [P, H])
        top = sb("top", [P, NT, 8])
        XT3 = sb("XT3", [P, B, C, T])
        mv3 = sb("mv3", [P, N, 2])
        rstd3 = sb("rstd3", [P, N])
        ex = sb("ex", [P, NT, E])
        pr = sb("pr", [P, NT, E])
        lmax = sb("lmax", [P, NT])
        lsum = sb("lsum", [P, NT])
        tix = sb("tix", [P, NT, 8], mybir.dt.uint32)
        rank = sb("rank", [P, NT, 2])
        wsum = sb("wsum", [P, NT])
        wts = sb("wts", [P, NT, 2])
        hot = sb("hot", [P, 2, NT, E])
        iotaE = sb("iotaE", [P, E])
        iotai = sb("iotai", [P, E], mybir.dt.int32)
        b1sb = sb("b1sb", [P, 2, FC])
        gT = sb("gT", [E, 2, P])
        moe = QT[:].rearrange("p n h t -> p (n h t)").bitcast(F32)
        ACC = moe[:, 0:N * D].rearrange("p (n d) -> p n d", n=N)
        at = N * D
        w1sb = moe[:, at:at + 2 * C * F].rearrange("p (a c f) -> p a c f", a=2, c=C)
        at += 2 * C * F
        w2sb = moe[:, at:at + 2 * FC * D].rearrange("p (a c f) -> p a c f", a=2, c=FC)
        at += 2 * FC * D
        HT = moe[:, at:at + 2 * FC * 512].rearrange("p (a f t) -> p a f t", a=2, f=FC)
        FINAL = XN

        names = """x_loaded w_loaded ctx_loaded consts zeros_set var_ready rstd_ready xn_ready xn_transposed
            xt_ready lat_done lat_ready qkv_done qf_ready qh_ready qx_ready qx_transposed qt_ready kx_ready kx_transposed kt_ready
            cx_transposed ct_ready kv2_done kv2_ready kx2_ready kx2_transposed kt2_ready""".split()
        s = {k: sem(k) for k in names}
        dve_chain, pool_chain = sem("dve_chain"), sem("pool_chain")
        smax_full, smax_free = sem("smax_full"), sem("smax_free")
        mt_ready = sem("mt_ready")
        nm_ready, mp_ready = sem("nm_ready"), sem("mp_ready")
        mrows = [sem("mrows_even"), sem("mrows_odd")]
        st_full, p_ready, pv_done = sem("st_full"), sem("p_ready"), sem("pv_done")
        yn_ready, yn_transposed, yt_ready = sem("yn_ready"), sem("yn_transposed"), sem("yt_ready")
        yf_ready, yf_turned = sem("yf_ready"), sem("yf_turned")
        proj_done, x1_ready = sem("proj_done"), sem("x1_ready")
        stored = sem("stored")
        s_small = sem("small_loaded")
        smallT, smallT_ready = sem("small_transposed"), sem("smallT_ready")
        v = {k: sem("x_" + k) for k in """var_ready rstd_ready xn_ready xn_transposed xt_ready q_done qf_ready qh_ready qx_ready
            qx_transposed qt_ready smax_full smax_free mp_ready mt_full mt_ready st_full p_ready pv_done yn_ready
            yn_transposed yt_ready proj_done x2_ready""".split()}
        vrows = [sem("x_mrows_even"), sem("x_mrows_odd")]
        rt = {k: sem("r_" + k) for k in """var_ready rstd_ready xn_ready xn_transposed xt_ready kept lg_done lg_ready ex_ready
            g_ready""".split()}
        e = {k: sem("e_" + k) for k in """b1_loaded w_loaded0 w_loaded1 h_done h_ready o_done o_used up_done gt_done gt_ready b2_done b2_used
            fin_ready""".split()}

        credited = [q for group in (s, v, rt, e) for name, q in group.items() if "loaded" not in name and name != "consts"]
        credited += vrows

        items = [(0, i) for i in range(NT)] + [(1, i) for i in reversed(range(NT))]
        LEAD = 2

        def max_tiles(i):
            keys = (i + 1) * P
            head = min(keys, 512)
            hb = 512 // head
            tiles = [(h, hb, 0, head, 0) for h in range(0, H, hb)]
            if keys > 512:
                hb = 512 // (keys - 512)
                tiles += [(h, hb, 512, keys - 512, 1) for h in range(0, H, hb)]
            return tiles

        def pairs(i):
            units = [(g, j) for j in range(i + 1) for g in range(G)]
            return [units[k:k + 2] for k in range(0, len(units), 2)]

        def schedule():
            order = []
            for n in range(min(LEAD, N)):
                order += [("max", n, k) for k in range(len(max_tiles(items[n][1])))] + [("mt", n, 0)]
            flat = [(n, p) for n in range(N) for p in range(len(pairs(items[n][1])))]
            order += [("st",) + flat[0]]
            for q, (n, p) in enumerate(flat):
                np_ = len(pairs(items[n][1]))
                if q + 1 < len(flat):
                    order += [("st",) + flat[q + 1]] if flat[q + 1][0] == n else []
                if n + LEAD < N:
                    m = [("max", n + LEAD, k) for k in range(len(max_tiles(items[n + LEAD][1])))]
                    lo, hi = len(m) * p // np_, len(m) * (p + 1) // np_
                    order += m[lo:hi]
                    if p == np_ - 1:
                        order += [("mt", n + LEAD, 0)]
                if q + 1 < len(flat) and flat[q + 1][0] != n:
                    order += [("st",) + flat[q + 1]]
                order += [("pv", n, p)]
                if n > 0:
                    after = [("ytr", n - 1, 0), ("yt", n - 1, 0), ("proj", n - 1, 0)]
                    order += after[p:p + 1]
                    if p == np_ - 1:
                        order += after[p + 1:]
            return order + [("ytr", N - 1, 0), ("yt", N - 1, 0), ("proj", N - 1, 0)]

        order = schedule()
        ring = [o for o in order if o[0] in ("max", "mt")]
        ring_at = {o: k for k, o in enumerate(ring)}

        def maxima_to(r):
            return sum(o[0] == "max" for o in ring[:r + 1])

        def chunks(i):
            return 2 if (i + 1) * P > 512 else 1

        pair_at = {}
        for n in range(N):
            for p in range(len(pairs(items[n][1]))):
                pair_at[(n, p)] = len(pair_at)

        block = stack.enter_context(nc.Block())

        @block.sync
        def _(sp):
            sp.dma_start(X[:, 0:NT, :], x[0].rearrange("(n p) d -> p n d", p=P)).then_inc(s["x_loaded"], 16)
            sp.dma_start(X[:, NT:N, :], x[1].rearrange("(n p) d -> p n d", p=P)).then_inc(s["x_loaded"], 16)
            for q in credited:
                sp.sem_inc(q, CREDIT)
            for b in range(B):
                sp.dma_start(CX[:, b, :], ctx_in[b]).then_inc(s["ctx_loaded"], 16)
            for n in range(N):
                sp.wait_ge(mt_ready, n + 1)
                b, i = items[n]
                for k in range(3):
                    sp.dma_start(QT[KQ + k:KQ + k + 1, b * NT + i, :, :],
                                 MT[k * H:(k + 1) * H, n % 2, :]).then_inc(mrows[n % 2], 16)
            with sp.Fori(0, B) as b:
                for i in range(NT):
                    sp.wait_ge(v["mt_ready"], CREDIT + b * NT + (i + 1))
                    for k in range(3):
                        sp.dma_start(QT[KQ + k:KQ + k + 1, bass.ds(b * NT + i, 1), :, :].rearrange("p n h t -> p (n h) t"),
                                     MT[k * H:(k + 1) * H, i % 2, :]).then_inc(vrows[i % 2], 16)
            sp.wait_ge(v["pv_done"], CREDIT + B * 2 * NT)
            with sp.Fori(0, E // 2) as u:
                for a in range(2):
                    sp.wait_ge(e["up_done"], CREDIT + u * 2 + max(a - 1, 0)) if False else None
                    sp.wait_ge(e["o_done"], CREDIT + u * 2 * N)
                    w = e["w_loaded%d" % a]
                    sp.dma_start(w1sb[:, a, :, :], w1[bass.ds(u * 2 + a, 1)].rearrange("e (c p) f -> p (e c) f", p=P)).then_inc(w, 16)
                    sp.dma_start(w2sb[:, a, :, :], w2[bass.ds(u * 2 + a, 1)].rearrange("e (p c) f -> p (e c) f", p=P)).then_inc(w, 16)
                    sp.dma_start(b1sb[:, a, :], b1[bass.ds(u * 2 + a, 1)].rearrange("e (p c) -> p (e c)", p=P)).then_inc(w, 16)
            with sp.Fori(0, N // 4) as u:
                sp.wait_ge(e["fin_ready"], CREDIT + u + 1)
                sp.dma_start(out.rearrange("b (n p) d -> (b n) p d", p=P)[bass.ds(u * 4, 4)].rearrange("n p d -> p n d"),
                             X[:, bass.ds(u * 4, 4), :]).then_inc(stored, 16)
            sp.wait_ge(stored, 16 * (N // 4))

        @block.gpsimd
        def _(pool):
            chain = [0]

            def link(ins):
                chain[0] += 1
                ins.then_inc(pool_chain, 1)
                pool.wait_ge(pool_chain, chain[0])

            def stepper(b, base, per):
                local = [0]

                def step(ins):
                    local[0] += 1
                    assert local[0] <= per
                    ins.then_inc(pool_chain, 1)
                    pool.wait_ge(pool_chain, b * per + (base + local[0]))
                return step

            link(nc.gpsimd.memset(ident[:], 0.0))
            link(nc.gpsimd.affine_select(out=ident[:], in_=ident[:], compare_op=ALU.not_equal, fill=1.0, base=0,
                                         pattern=[[-1, P]], channel_multiplier=1))
            link(nc.gpsimd.tensor_copy(identb[:], ident[:]))
            link(nc.gpsimd.memset(mask_ts[:], 0.0))
            link(nc.gpsimd.affine_select(out=mask_ts[:], in_=mask_ts[:], compare_op=ALU.is_ge, fill=BIG, base=0,
                                         pattern=[[-1, P]], channel_multiplier=1))
            link(nc.gpsimd.memset(mask_st[:], 0.0))
            link(nc.gpsimd.affine_select(out=mask_st[:], in_=mask_st[:], compare_op=ALU.is_ge, fill=BIG, base=0,
                                         pattern=[[1, P]], channel_multiplier=-1))
            link(nc.gpsimd.memset(ones1[:], 1.0))
            link(nc.gpsimd.memset(halfneg[:], -0.5))
            link(nc.gpsimd.memset(KX[:], 1.0))
            link(nc.gpsimd.memset(KX2[:], 1.0))
            link(nc.gpsimd.memset(VX[:], 0.0))
            link(nc.gpsimd.memset(VX[:, :, HD:HV], 1.0))
            link(nc.gpsimd.memset(V2X[:], 1.0))
            link(nc.gpsimd.memset(zerosH[:], 0.0))
            link(nc.gpsimd.iota(iotai[:], [[1, E]], base=0, channel_multiplier=0))
            nc.gpsimd.tensor_copy(iotaE[:], iotai[:]).then_inc(s["consts"], 1)
            for b in range(B):
                pool.wait_ge(s["kv2_ready"], CREDIT + b + 1)
                k = KV2[:, b, 0:D].rearrange("p (h d) -> p h d", h=H)
                part = [KX2[:, b, :, q * HD:(q + 1) * HD] for q in range(SPLIT)]
                for q in (3, 5):
                    nc.gpsimd.tensor_copy(part[q], k)
                link(nc.gpsimd.tensor_copy(part[0], k))
                link(nc.gpsimd.tensor_tensor(krest2[:], k, part[0], ALU.subtract))
                nc.gpsimd.tensor_copy(part[4], krest2[:])
                link(nc.gpsimd.tensor_copy(part[1], krest2[:]))
                nc.gpsimd.tensor_copy(V2X[:, b, :, 0:HD], KV2[:, b, D:2 * D].rearrange("p (h d) -> p h d", h=H))
                nc.gpsimd.tensor_tensor(part[2], krest2[:], part[1], ALU.subtract).then_inc(s["kx2_ready"], 1)
            base = chain[0]
            with pool.Fori(0, B) as b:
                pool.wait_ge(s["var_ready"], CREDIT + b + 1)
                nc.gpsimd.tensor_tensor(rstd[:, :], ve[:, :], halfneg[:, 0:NT], ALU.pow).then_inc(s["rstd_ready"], 1)
                step = stepper(b, base, NT)
                for i in range(NT):
                    q = QF[:, i, 0:D].rearrange("p (h d) -> p h d", h=H)
                    xq = QX[:, i % 2]
                    pool.wait_ge(s["qf_ready"], CREDIT + b * NT + (i + 1))
                    pool.wait_ge(s["qx_ready"], CREDIT + b * NT + i)
                    pool.wait_ge(s["qh_ready"], CREDIT + b * NT + (i + 1))
                    nc.gpsimd.tensor_tensor(qrest[:], q, xq[:, :, 0, :], ALU.subtract)
                    nc.gpsimd.tensor_tensor(xq[:, :, 3, :], q, xq[:, :, 0, :], ALU.subtract)
                    step(nc.gpsimd.tensor_tensor(xq[:, :, 4, :], q, xq[:, :, 0, :], ALU.subtract))
                    nc.gpsimd.tensor_tensor(xq[:, :, 5, :], qrest[:], xq[:, :, 3, :],
                                            ALU.subtract).then_inc(s["qx_ready"], 1)
            chain[0] += B * NT
            for n in range(N):
                if chunks(items[n][1]) == 1:
                    pool.wait_ge(smax_free, maxima_to(ring_at[("mt", n, 0)]))
                else:
                    pool.wait_ge(nm_ready, sum(chunks(i) == 2 for _, i in items[:n + 1]))
                if n >= 2:
                    pool.wait_ge(mt_ready, n - 1)
                m = nm[:, n % 2, :]
                link(nc.gpsimd.tensor_copy(MP[:, n % 2, 0, :], m))
                link(nc.gpsimd.tensor_tensor(mrest[:], m, MP[:, n % 2, 0, :], ALU.subtract))
                link(nc.gpsimd.tensor_copy(MP[:, n % 2, 1, :], mrest[:]))
                nc.gpsimd.tensor_tensor(MP[:, n % 2, 2, :], mrest[:], MP[:, n % 2, 1, :],
                                        ALU.subtract).then_inc(mp_ready, 1)

            with pool.Fori(0, B) as b:
                step = stepper(b, chain[0], NT)
                pool.wait_ge(v["var_ready"], CREDIT + b + 1)
                nc.gpsimd.tensor_tensor(rstd[:, :], ve[:, :], halfneg[:, 0:NT], ALU.pow).then_inc(v["rstd_ready"], 1)
                for i in range(NT):
                    q = QF[:, i, 0:D].rearrange("p (h d) -> p h d", h=H)
                    xq = QX[:, i % 2]
                    pool.wait_ge(v["qf_ready"], CREDIT + b * NT + (i + 1))
                    pool.wait_ge(v["qx_ready"], CREDIT + b * NT + i)
                    pool.wait_ge(v["qh_ready"], CREDIT + b * NT + (i + 1))
                    nc.gpsimd.tensor_tensor(qrest[:], q, xq[:, :, 0, :], ALU.subtract)
                    nc.gpsimd.tensor_tensor(xq[:, :, 3, :], q, xq[:, :, 0, :], ALU.subtract)
                    step(nc.gpsimd.tensor_tensor(xq[:, :, 4, :], q, xq[:, :, 0, :], ALU.subtract))
                    nc.gpsimd.tensor_tensor(xq[:, :, 5, :], qrest[:], xq[:, :, 3, :],
                                            ALU.subtract).then_inc(v["qx_ready"], 1)
            chain[0] += B * NT
            with pool.Fori(0, B) as b:
                step = stepper(b, chain[0], 2 * NT)
                for i in range(NT):
                    pool.wait_ge(v["smax_free"], CREDIT + b * NT + (i + 1))
                    pool.wait_ge(v["mt_ready"], CREDIT + b * NT + max(i - 1, 0))
                    m = nm[:, i % 2, :]
                    pool.wait_ge(v["mp_ready"], CREDIT + b * NT + i)
                    step(nc.gpsimd.tensor_tensor(MP[:, i % 2, 0, :], m, zerosH[:], ALU.add))
                    nc.gpsimd.tensor_tensor(mrest[:], m, MP[:, i % 2, 0, :], ALU.subtract)
                    step(nc.gpsimd.tensor_tensor(MP[:, i % 2, 1, :], m, MP[:, i % 2, 0, :], ALU.subtract))
                    nc.gpsimd.tensor_tensor(MP[:, i % 2, 2, :], mrest[:], MP[:, i % 2, 1, :],
                                            ALU.subtract).then_inc(v["mp_ready"], 1)
            chain[0] += B * 2 * NT
            with pool.Fori(0, B) as b:
                pool.wait_ge(rt["var_ready"], CREDIT + b + 1)
                nc.gpsimd.tensor_tensor(rstd[:, :], ve[:, :], halfneg[:, 0:NT], ALU.pow).then_inc(rt["rstd_ready"], 1)
                pool.wait_ge(rt["xt_ready"], CREDIT + b * NT + NT)
                nc.gpsimd.tensor_copy(XT3[:, bass.ds(b, 1), :, :].rearrange("p b c t -> p (b c) t"), XT[:, :, :]).then_inc(rt["kept"], 1)

        @block.scalar
        def _(act):
            def first_parts(b, i, sems):
                act.wait_ge(sems["qx_transposed"], CREDIT + b * NT + max(i - 1, 0))
                nc.scalar.copy(QX[:, i % 2, :, 0:3, :],
                               bank(3 + i % 2)[:, 0:D].rearrange("p (h d) -> p h d", h=H).unsqueeze(2)
                               .to_broadcast([P, H, 3, HD])).then_inc(sems["qh_ready"], 1)

            act.dma_start(wdown[:], w_down.rearrange("(c p) n -> p c n", p=P)).then_inc(s["w_loaded"], 16)
            act.dma_start(wqkvup[:, 0:D], w_qup).then_inc(s["w_loaded"], 16)
            act.dma_start(wqkvup[:, D:D + 2 * HD], w_kvup).then_inc(s["w_loaded"], 16)
            act.dma_start(wproj[:], w_proj.rearrange("(c p) n -> p c n", p=P)).then_inc(s["w_loaded"], 16)
            act.dma_start(wqkv[:], w_qkv.rearrange("(c p) n -> p c n", p=P)).then_inc(s_small, 16)
            act.dma_start(bqkv[:], b_qkv.rearrange("(a n) -> a n", a=1)).then_inc(s_small, 16)
            act.dma_start(wout[:], w_out.rearrange("(c p) n -> p c n", p=P)).then_inc(s_small, 16)
            act.dma_start(bout[:], b_out.rearrange("(a n) -> a n", a=1)).then_inc(s_small, 16)
            act.dma_start(gaterow[:], gate_w).then_inc(s_small, 16)
            act.dma_start(b2sb[:], b2).then_inc(s_small, 16)
            act.wait_ge(s["cx_transposed"], CREDIT + 1)
            nc.scalar.copy(CT[:], bank(0)[:, 0:B * C * S].rearrange("p (b c s) -> p b c s", b=B, c=C)).then_inc(s["ct_ready"], 1)
            nc.scalar.copy(gateT[:], bank(1)[:, 0:C * E].rearrange("p (c e) -> p c e", c=C)).then_inc(s["ct_ready"], 1)
            for b in range(B):
                act.wait_ge(s["kv2_done"], CREDIT + b + 1)
                nc.scalar.copy(KV2[:, b, :], bank(2 + b)[0:S, :]).then_inc(s["kv2_ready"], 1)
            for b in range(B):
                act.wait_ge(s["kx2_transposed"], CREDIT + b + 1)
                nc.scalar.copy(KT2[0:KM, b, :, 0:S].rearrange("p (a h) s -> p a h s", a=2),
                               ps[:, 4 + 2 * b:6 + 2 * b, :].bitcast(BF16)[0:KM, :, 0:8 * SP].rearrange("p a (h s) -> p a h s", s=SP)[:, :, :, 0:S]
                               ).then_inc(s["kt2_ready"], 1)
            with act.Fori(0, B) as b:
                for i in range(NT):
                    act.wait_ge(s["xn_transposed"], CREDIT + b * NT + (i + 1))
                    act.wait_ge(s["lat_done"], CREDIT + b * 2)
                    nc.scalar.copy(XT[:, :, i * P:(i + 1) * P],
                                   bank(i % 2)[:, 0:C * P].rearrange("p (c t) -> p c t", c=C)).then_inc(s["xt_ready"], 1)
                    if i % 4 == 3:
                        g = i // 4
                        act.wait_ge(s["lat_done"], CREDIT + b * 2 + (g + 1))
                        act.wait_ge(s["qkv_done"], CREDIT + b * NT)
                        nc.scalar.copy(LT[:, g * 512:(g + 1) * 512], bank(2)).then_inc(s["lat_ready"], 1)
                for i in range(NT):
                    act.wait_ge(s["qkv_done"], CREDIT + b * NT + (i + 1))
                    act.wait_ge(s["qx_ready"], CREDIT + b * NT)
                    act.wait_ge(s["kx_ready"], CREDIT + b)
                    nc.scalar.copy(QF[:, i, :], bank(3 + i % 2)[:, 0:D + 2 * HD]).then_inc(s["qf_ready"], 1)
                    first_parts(b, i, s)
            for kind, n, k in order:
                if kind == "mt":
                    act.wait_ge(smax_full, ring_at[(kind, n, k)] + 1)
                    if n >= 2:
                        act.wait_ge(mrows[n % 2], 48 * (n // 2))
                    r = ring_at[(kind, n, k)]
                    nc.scalar.copy(MT[:, n % 2, :], bank(4 + r % 2).bitcast(BF16)[0:3 * H, 0:P]).then_inc(mt_ready, 1)
                elif kind == "st":
                    q = pair_at[(n, k)]
                    act.wait_ge(st_full, q + 1)
                    if q >= 3:
                        act.wait_ge(pv_done, q - 2)
                    nc.scalar.activation(PR[:, q % 3, :, :], ps[:, 2 * (q % 2):2 * (q % 2) + 2, :], ACT.Exp,
                                         scale=SCALE).then_inc(p_ready, 1)
                elif kind == "ytr":
                    act.wait_ge(pv_done, pair_at[(n, len(pairs(items[n][1])) - 1)] + 1)
                    if n >= 2:
                        act.wait_ge(yf_turned, n - 1)
                    nc.scalar.copy(YF[:, n % 2, :], bank(6 + n % 2)).then_inc(yf_ready, 1)
                elif kind == "yt":
                    act.wait_ge(yn_transposed, n + 1)
                    if n >= 2:
                        act.wait_ge(proj_done, n - 1)
                    nc.scalar.copy(YT[:, n % 2, :, :],
                                   bank(6 + n % 2)[:, 0:D].rearrange("p (c t) -> p c t", c=C)).then_inc(yt_ready, 1)

            with act.Fori(0, B) as b:
                for i in range(NT):
                    act.wait_ge(v["xn_transposed"], CREDIT + b * NT + (i + 1))
                    act.wait_ge(v["q_done"], CREDIT + b * NT)
                    nc.scalar.copy(XT[:, :, i * P:(i + 1) * P],
                                   bank(i % 2)[:, 0:C * P].rearrange("p (c t) -> p c t", c=C)).then_inc(v["xt_ready"], 1)
                for i in range(NT):
                    act.wait_ge(v["q_done"], CREDIT + b * NT + (i + 1))
                    act.wait_ge(v["qx_ready"], CREDIT + b * NT)
                    nc.scalar.copy(QF[:, i, 0:D], bank(3 + i % 2)[:, 0:D]).then_inc(v["qf_ready"], 1)
                    first_parts(b, i, v)
            with act.Fori(0, B) as b:
                for i in range(NT):
                    act.wait_ge(v["mt_full"], CREDIT + b * NT + (i + 1))
                    act.wait_ge(vrows[i % 2], CREDIT + b * (48 * NT // 2) + 48 * (i // 2))
                    nc.scalar.copy(MT[:, i % 2, :], bank(4 + i % 2)[0:3 * H, 0:P]).then_inc(v["mt_ready"], 1)
            with act.Fori(0, B) as b:
                for i in range(NT + 2):
                    for q in (2 * i, 2 * i + 1):
                        if i < NT:
                            act.wait_ge(v["st_full"], CREDIT + b * (2 * NT) + (q + 1))
                            act.wait_ge(v["pv_done"], CREDIT + b * (2 * NT) + max(q - 2, 0))
                            k = 4 + 2 * (q % 2)
                            nc.scalar.activation(PR[0:S, q % 3, :, :], ps[0:S, k:k + 2, :], ACT.Exp,
                                                 scale=SCALE).then_inc(v["p_ready"], 1)
                    if i >= 2:
                        t = i - 2
                        act.wait_ge(v["yn_transposed"], CREDIT + b * NT + (t + 1))
                        act.wait_ge(v["proj_done"], CREDIT + b * NT + max(t - 1, 0))
                        nc.scalar.copy(YT[:, t % 2, :, :],
                                       bank(t % 3)[:, 0:D].rearrange("p (c t) -> p c t", c=C)).then_inc(v["yt_ready"], 1)
            with act.Fori(0, B) as b:
                act.wait_ge(rt["kept"], CREDIT + b)
                for i in range(NT):
                    act.wait_ge(rt["xn_transposed"], CREDIT + b * NT + (i + 1))
                    nc.scalar.copy(XT[:, :, i * P:(i + 1) * P],
                                   bank(i % 2)[:, 0:C * P].rearrange("p (c t) -> p c t", c=C)).then_inc(rt["xt_ready"], 1)
                act.wait_ge(rt["lg_ready"], CREDIT + b + 1)
                nc.scalar.activation(ex[:], lg[:], ACT.Exp).then_inc(rt["ex_ready"], 1)
            for u in range(N):
                act.wait_ge(e["gt_done"], CREDIT + u + 1)
                if u >= 2:
                    act.wait_ge(e["b2_done"], CREDIT + u - 1)
                nc.scalar.copy(gT[:, u % 2, :], bank(u % 2)[0:E, 0:P]).then_inc(e["gt_ready"], 1)
            with act.Fori(0, E // 2) as u:
                for a in range(2):
                    act.wait_ge(e["w_loaded%d" % a], u * 48 + 48)
                    for q in range(4):
                        for f in range(FC):
                            k = (a * 4 + q) * FC + f
                            act.wait_ge(e["h_done"], CREDIT + u * (8 * FC) + (k + 1))
                            if f == 0:
                                act.wait_ge(e["o_done"], CREDIT + u * (2 * N) + max(a * 4 + q - 1, 0) * 4)
                            nc.scalar.activation(HT[:, q % 2, f, :], bank(k % 4), ACT.Gelu,
                                                 bias=b1sb[:, a, f:f + 1]).then_inc(e["h_ready"], 1)

        @block.vector
        def _(dve):
            chain = [0]

            def link(ins):
                chain[0] += 1
                ins.then_inc(dve_chain, 1)
                dve.wait_ge(dve_chain, chain[0])

            def apart():
                nc.vector.memset(scratch[:], 0.0)

            dve.wait_ge(s["consts"], 1)
            dve.wait_ge(s["x_loaded"], 32)
            LINKS = 5
            with dve.Fori(0, B) as b:
                local = [0]

                def step(ins):
                    local[0] += 1
                    ins.then_inc(dve_chain, 1)
                    dve.wait_ge(dve_chain, b * LINKS + local[0])

                for i in range(NT):
                    ins = nc.vector.bn_stats(stats[:, i, :], X[:, bass.ds(b * NT + i, 1), :])
                step(ins)
                apart()
                for i in range(NT):
                    ins = nc.vector.bn_aggr(mv[:, i, :], stats[:, i, :])
                step(ins)
                nc.vector.tensor_scalar(ve[:, :], mv[:, :, 1], EPS, None, ALU.add).then_inc(s["var_ready"], 1)
                dve.wait_ge(s["rstd_ready"], CREDIT + b + 1)
                for i in range(NT):
                    dve.wait_ge(s["xn_transposed"], CREDIT + b * NT)
                    nc.vector.tensor_scalar(XN[:, i:i + 1, :], X[:, bass.ds(b * NT + i, 1), :], mv[:, i, 0:1], rstd[:, i:i + 1],
                                            ALU.subtract, ALU.mult).then_inc(s["xn_ready"], 1)
                for i in range(NT):
                    if i == NT - 2:
                        dve.wait_ge(s["qf_ready"], CREDIT + b * NT + NT)
                        dve.wait_ge(s["kx_transposed"], CREDIT + b)
                        k = QF[:, :, D:D + HD]
                        part = [KX[:, :, r * HD:(r + 1) * HD] for r in range(SPLIT)]
                        for r in (3, 5):
                            nc.vector.tensor_copy(part[r], k)
                        step(nc.vector.tensor_copy(part[0], k))
                        step(nc.vector.tensor_tensor(krest[:], k, part[0], ALU.subtract))
                        nc.vector.tensor_copy(part[4], krest[:])
                        step(nc.vector.tensor_copy(part[1], krest[:]))
                        nc.vector.tensor_copy(VX[:, bass.ds(b * NT, NT), 0:HD], QF[:, :, D + HD:D + 2 * HD])
                        nc.vector.tensor_tensor(part[2], krest[:], part[1], ALU.subtract).then_inc(s["kx_ready"], 1)
                    dve.wait_ge(s["qx_transposed"], CREDIT + b * NT + (i + 1))
                    nc.vector.tensor_copy(QT[0:KQ, bass.ds(b * NT + i, 1), :, :],
                                          ps[:, 6:8, :].bitcast(BF16)[0:KQ].rearrange("p a (h t) -> p (a h) t", t=P)
                                          ).then_inc(s["qt_ready"], 1)
                assert local[0] == LINKS
                dve.wait_ge(s["kx_transposed"], CREDIT + b + 1)
                nc.vector.tensor_copy(KT[0:KM, bass.ds(b, 1), :], bank(5).bitcast(BF16)[0:KM, :]).then_inc(s["kt_ready"], 1)
            chain[0] = B * LINKS

            for kind, n, k in order:
                b, i = items[n]
                if kind == "max":
                    h0, nh, s0, ns, c = max_tiles(i)[k]
                    r = ring_at[(kind, n, k)]
                    dve.wait_ge(smax_full, r + 1)
                    if k == 0 and n >= 2:
                        dve.wait_ge(mp_ready, n - 1)
                    two = chunks(i) == 2
                    last = k == len(max_tiles(i)) - 1
                    dst = nmx[:, n % 2, c, h0:h0 + nh] if two else nm[:, n % 2, h0:h0 + nh]
                    ins = nc.vector.tensor_reduce(dst, bank(4 + r % 2)[:, 0:nh * ns].rearrange("p (h s) -> p h s", h=nh),
                                                  AX_X, ALU.max, negate=True)
                    ins.then_inc(smax_free, 1)
                    if last and two:
                        dve.wait_ge(smax_free, maxima_to(r))
                        nc.vector.tensor_tensor(nm[:, n % 2, :], nmx[:, n % 2, 0, :], nmx[:, n % 2, 1, :],
                                                ALU.min).then_inc(nm_ready, 1)
                elif kind == "ytr":
                    y = bank(6 + n % 2).rearrange("p (a g v) -> p a g v", a=HG, g=G)
                    dve.wait_ge(yf_turned, n + 1)
                    if n >= 2:
                        dve.wait_ge(yn_transposed, n - 1)
                    ri = rinv[:, n % 2, :].rearrange("p (a g) -> p a g", a=HG)
                    link(nc.vector.reciprocal(ri, y[:, :, :, HD]))
                    nc.vector.tensor_tensor(YN[:, n % 2, :].rearrange("p (g a d) -> p a g d", g=G, a=HG), y[:, :, :, 0:HD],
                                            ri.unsqueeze(3).to_broadcast([P, HG, G, HD]), ALU.mult).then_inc(yn_ready, 1)
                elif kind == "proj":
                    t = b * NT + i
                    dve.wait_ge(proj_done, n + 1)
                    nc.vector.tensor_tensor(X[:, t, :], X[:, t, :], bank(6 + n % 2)[:, D:2 * D],
                                            ALU.add).then_inc(x1_ready, 1)

            def stepper(b, base, per):
                local = [0]

                def step(ins):
                    local[0] += 1
                    assert local[0] <= per
                    ins.then_inc(dve_chain, 1)
                    dve.wait_ge(dve_chain, b * per + (base + local[0]))
                return step

            def norm(b, step, sems, before):
                if True:
                    for i in range(NT):
                        ins = nc.vector.bn_stats(stats[:, i, :], X[:, bass.ds(b * NT + i, 1), :])
                    step(ins)
                    apart()
                    for i in range(NT):
                        ins = nc.vector.bn_aggr(mv[:, i, :], stats[:, i, :])
                    step(ins)
                    nc.vector.tensor_scalar(ve[:, :], mv[:, :, 1], EPS, None, ALU.add).then_inc(sems["var_ready"], 1)
                    dve.wait_ge(sems["rstd_ready"], CREDIT + b + 1)
                    dve.wait_ge(before[0], CREDIT + before[1])
                    for i in range(NT):
                        nc.vector.tensor_scalar(XN[:, i:i + 1, :], X[:, bass.ds(b * NT + i, 1), :], mv[:, i, 0:1],
                                                rstd[:, i:i + 1], ALU.subtract, ALU.mult).then_inc(sems["xn_ready"], 1)

            dve.wait_ge(x1_ready, N)
            with dve.Fori(0, B) as b:
                norm(b, stepper(b, chain[0], 2), v, (v["xn_transposed"], b * NT))
                for i in range(NT):
                    dve.wait_ge(v["qx_transposed"], CREDIT + b * NT + (i + 1))
                    nc.vector.tensor_copy(QT[0:KQ, bass.ds(b * NT + i, 1), :, :],
                                          ps[:, 6:8, :].bitcast(BF16)[0:KQ].rearrange("p a (h t) -> p (a h) t", t=P)
                                          ).then_inc(v["qt_ready"], 1)
            chain[0] += B * 2
            with dve.Fori(0, B) as b:
                for i in range(NT):
                    dve.wait_ge(v["smax_full"], CREDIT + b * NT + (i + 1))
                    dve.wait_ge(v["mp_ready"], CREDIT + b * NT + max(i - 1, 0))
                    nc.vector.tensor_reduce(nm[:, i % 2, 0:12].rearrange("p (a h) -> p a h", a=2),
                                            ps[:, 0:2, 0:6 * S].rearrange("p a (h s) -> p a h s", s=S),
                                            AX_X, ALU.max, negate=True)
                    nc.vector.tensor_reduce(nm[:, i % 2, 12:16], bank(2)[:, 0:4 * S].rearrange("p (h s) -> p h s", s=S),
                                            AX_X, ALU.max, negate=True).then_inc(v["smax_free"], 1)
            with dve.Fori(0, B) as b:
                step = stepper(b, chain[0], NT)
                for i in range(NT + 3):
                    if 1 <= i <= NT:
                        t = i - 1
                        y = bank(t % 3)[:, 0:H * HV].rearrange("p (h v) -> p h v", v=HV)
                        dve.wait_ge(v["pv_done"], CREDIT + b * (2 * NT) + (2 * t + 2))
                        dve.wait_ge(v["yn_transposed"], CREDIT + b * NT + max(t - 1, 0))
                        step(nc.vector.reciprocal(rinv[:, t % 2, :], y[:, :, HD]))
                        nc.vector.tensor_tensor(YN[:, t % 2, :].rearrange("p (h d) -> p h d", h=H), y[:, :, 0:HD],
                                                rinv[:, t % 2, :].unsqueeze(2).to_broadcast([P, H, HD]),
                                                ALU.mult).then_inc(v["yn_ready"], 1)
                    if i >= 3:
                        t = i - 3
                        dve.wait_ge(v["proj_done"], CREDIT + b * NT + (t + 1))
                        nc.vector.tensor_tensor(X[:, bass.ds(b * NT + t, 1), :], X[:, bass.ds(b * NT + t, 1), :],
                                                bank(t % 3)[:, D:2 * D].unsqueeze(1), ALU.add).then_inc(v["x2_ready"], 1)
            chain[0] += B * NT
            dve.wait_ge(v["x2_ready"], CREDIT + N)
            with dve.Fori(0, B) as b:
                step = stepper(b, chain[0], 14)
                norm(b, step, rt, (rt["xn_transposed"], b * NT))
                nc.vector.tensor_copy(mv3[:, bass.ds(b * NT, NT), :], mv[:])
                nc.vector.tensor_copy(rstd3[:, bass.ds(b * NT, NT)], rstd[:])
                dve.wait_ge(rt["lg_done"], CREDIT + b + 1)
                l3 = bank(2)[:, 0:NT * E].rearrange("p (n e) -> p n e", e=E)

                def wide(a):
                    return a.unsqueeze(2).to_broadcast([P, NT, E])

                step(nc.vector.tensor_reduce(lmax[:], l3, AX_X, ALU.max))
                nc.vector.tensor_tensor(lg[:], l3, wide(lmax[:]), ALU.subtract).then_inc(rt["lg_ready"], 1)
                dve.wait_ge(rt["ex_ready"], CREDIT + b + 1)
                step(nc.vector.tensor_reduce(lsum[:], ex[:], AX_X, ALU.add))
                step(nc.vector.reciprocal(lmax[:], lsum[:]))
                step(nc.vector.tensor_tensor(pr[:], ex[:], wide(lmax[:]), ALU.mult))
                apart()
                for i in range(NT):
                    ins = nc.vector.max(top[:, i, :], pr[:, i, :])
                step(ins)
                apart()
                for i in range(NT):
                    ins = nc.vector.max_index(tix[:, i, :], top[:, i, :], pr[:, i, :])
                step(ins)
                nc.vector.tensor_copy(rank[:], tix[:, :, 0:2])
                step(nc.vector.tensor_tensor(wsum[:], top[:, :, 0], top[:, :, 1], ALU.add))
                step(nc.vector.tensor_scalar(wsum[:], wsum[:], 1e-10, None, ALU.max))
                step(nc.vector.reciprocal(lsum[:], wsum[:]))
                step(nc.vector.tensor_tensor(wts[:], top[:, :, 0:2], lsum[:].unsqueeze(2).to_broadcast([P, NT, 2]), ALU.mult))
                for k in range(2):
                    ins = nc.vector.tensor_tensor(hot[:, k], iotaE[:].unsqueeze(1).to_broadcast([P, NT, E]),
                                                  wide(rank[:, :, k]), ALU.is_equal)
                step(ins)
                for k in range(2):
                    ins = nc.vector.tensor_tensor(hot[:, k], hot[:, k], wide(wts[:, :, k]), ALU.mult)
                step(ins)
                nc.vector.tensor_tensor(GT[:, bass.ds(b * NT, NT), :], hot[:, 0], hot[:, 1], ALU.add).then_inc(rt["g_ready"], 1)
            chain[0] += B * 14
            dve.wait_ge(v["pv_done"], CREDIT + B * 2 * NT)
            for u in range(N):
                dve.wait_ge(e["b2_done"], CREDIT + u + 1)
                nc.vector.tensor_copy(ACC[:, u, :], bank(2 + u % 2)[:, 0:D]).then_inc(e["b2_used"], 1)
            dve.wait_ge(e["b2_used"], CREDIT + N)
            with dve.Fori(0, E // 2) as u:
                for a in range(2):
                    for n in range(N):
                        k = a * N + n
                        dve.wait_ge(e["o_done"], CREDIT + u * (2 * N) + (k + 1))
                        dve.wait_ge(e["o_used"], CREDIT + u * (2 * N) + (k - n)) if n == 0 else None
                        nc.vector.scalar_tensor_tensor(out=ACC[:, n, :], in0=bank(4 + k % 4)[:, 0:D],
                                                       scalar=GT[:, n, bass.ds(u * 2 + a, 1)], in1=ACC[:, n, :],
                                                       op0=ALU.mult, op1=ALU.add).then_inc(e["o_used"], 1)
            base4 = chain[0]
            with dve.Fori(0, N // 4) as u:
                tiles = bass.ds(u * 4, 4)
                dve.wait_ge(e["o_used"], CREDIT + E * N)
                dve.wait_ge(e["fin_ready"], CREDIT + u)
                for i in range(4):
                    n = bass.ds(u * 4 + i, 1)
                    ins = nc.vector.tensor_scalar(FINAL[:, i:i + 1, :], X[:, n, :], mv3[:, n, 0], rstd3[:, n],
                                                  ALU.subtract, ALU.mult)
                ins.then_inc(dve_chain, 1)
                dve.wait_ge(dve_chain, u * 3 + (base4 + 1))
                nc.vector.tensor_tensor(FINAL[:, 0:4, :], FINAL[:, 0:4, :], ACC[:, tiles, :], ALU.add).then_inc(dve_chain, 1)
                dve.wait_ge(dve_chain, u * 3 + (base4 + 2))
                nc.vector.tensor_scalar(FINAL[:, 0:4, :], FINAL[:, 0:4, :], 100.0, -100.0, ALU.min, ALU.max).then_inc(dve_chain, 1)
                dve.wait_ge(dve_chain, u * 3 + (base4 + 3))
                nc.vector.tensor_tensor(X[:, tiles, :], FINAL[:, 0:4, :], X[:, tiles, :], ALU.add).then_inc(e["fin_ready"], 1)

        @block.tensor
        def _(pe):
            mm, tr = nc.tensor.matmul, nc.tensor.transpose
            pe.wait_ge(s["consts"], 1)
            pe.wait_ge(s["ctx_loaded"], 32)
            pe.wait_ge(s_small, 96)
            for b in range(B):
                for c in range(C):
                    tr(bank(0)[:, (b * C + c) * S:(b * C + c + 1) * S], CX[:, b, c * P:(c + 1) * P], ident[0:S, 0:S])
            for c in range(C):
                ins = tr(bank(1)[:, c * E:(c + 1) * E], gaterow[:, c * P:(c + 1) * P], ident[0:E, 0:E])
            ins.then_inc(s["cx_transposed"], 1)
            pe.wait_ge(s["ct_ready"], CREDIT + 2)
            for b in range(B):
                mm(bank(2 + b)[0:S, :], ones1[0:1, 0:S], bqkv[0:1, D:3 * D], start=True, stop=False)
                for c in range(C):
                    ins = mm(bank(2 + b)[0:S, :], CT[:, b, c, :], wqkv[:, c, D:3 * D], start=False, stop=c == C - 1)
                ins.then_inc(s["kv2_done"], 1)
            for b in range(B):
                pe.wait_ge(s["kx2_ready"], CREDIT + b + 1)
                for h in range(H):
                    ins = tr(bank(4 + 2 * b + h // 8).bitcast(BF16)[0:KM, (h % 8) * SP:(h % 8) * SP + S],
                             KX2[:, b, h, 0:KM], identb[0:S, 0:S])
                ins.then_inc(s["kx2_transposed"], 1)
            pe.wait_ge(s["w_loaded"], 64)
            pe.wait_ge(s["kt2_ready"], CREDIT + B)
            with pe.Fori(0, B) as b:
                for i in range(NT):
                    pe.wait_ge(s["xn_ready"], CREDIT + b * NT + (i + 1))
                    pe.wait_ge(s["xt_ready"], CREDIT + b * NT + max(i - 1, 0))
                    for c in range(C):
                        ins = tr(bank(i % 2)[:, c * P:(c + 1) * P], XN[:, i, c * P:(c + 1) * P], ident[:])
                    ins.then_inc(s["xn_transposed"], 1)
                    if i % 4 == 3:
                        g = i // 4
                        pe.wait_ge(s["xt_ready"], CREDIT + b * NT + (i + 1))
                        pe.wait_ge(s["lat_ready"], CREDIT + b * 2 + g)
                        for c in range(C):
                            ins = mm(bank(2), wdown[:, c, :], XT[:, c, g * 512:(g + 1) * 512], start=c == 0, stop=c == C - 1)
                        ins.then_inc(s["lat_done"], 1)
                for i in range(NT + 1):
                    if i < NT:
                        pe.wait_ge(s["lat_ready"], CREDIT + b * 2 + (i // 4 + 1))
                        pe.wait_ge(s["qh_ready"], CREDIT + b * NT + max(i - 1, 0))
                        mm(bank(3 + i % 2)[:, 0:D + 2 * HD], LT[:, i * P:(i + 1) * P], wqkvup[:], start=True,
                           stop=True).then_inc(s["qkv_done"], 1)
                    if i >= 1:
                        t = i - 1
                        pe.wait_ge(s["qx_ready"], CREDIT + b * NT + (t + 1))
                        pe.wait_ge(s["qt_ready"], CREDIT + b * NT + t)
                        for h in range(H):
                            ins = tr(bank(6 + h // 8).bitcast(BF16)[0:KQ, (h % 8) * P:(h % 8 + 1) * P],
                                     QX[:, t % 2, h, :, :].rearrange("p r d -> p (r d)"), identb[:])
                        ins.then_inc(s["qx_transposed"], 1)
                pe.wait_ge(s["kx_ready"], CREDIT + b + 1)
                pe.wait_ge(s["kt_ready"], CREDIT + b)
                for i in range(NT):
                    ins = tr(bank(5).bitcast(BF16)[0:KM, i * P:(i + 1) * P], KX[:, i, 0:KM], identb[:])
                ins.then_inc(s["kx_transposed"], 1)
            pe.wait_ge(s["qt_ready"], CREDIT + N)
            pe.wait_ge(s["kt_ready"], CREDIT + B)
            pe.wait_ge(s["qh_ready"], CREDIT + N)

            for kind, n, k in order:
                b, i = items[n]
                t = b * NT + i
                r = ring_at.get((kind, n, k))
                if r is not None and r >= 2:
                    prev = ring[r - 2]
                    if prev[0] == "max":
                        pe.wait_ge(smax_free, maxima_to(r - 2))
                    else:
                        pe.wait_ge(mt_ready, prev[1] + 1)
                if kind == "max":
                    h0, nh, s0, ns, c = max_tiles(i)[k]
                    diag = s0 + ns == (i + 1) * P
                    for a in range(nh):
                        ins = mm(bank(4 + r % 2)[:, a * ns:(a + 1) * ns], QT[0:KQ, t, h0 + a, :], KT[0:KQ, b, s0:s0 + ns],
                                 start=a == 0, stop=not diag and a == nh - 1, skip_group_check=True)
                        if diag:
                            ins = mm(bank(4 + r % 2)[:, (a + 1) * ns - P:(a + 1) * ns], identb[:], mask_ts[:],
                                     start=False, stop=a == nh - 1, skip_group_check=True)
                    ins.then_inc(smax_full, 1)
                elif kind == "mt":
                    pe.wait_ge(mp_ready, n + 1)
                    tr(bank(4 + r % 2).bitcast(BF16)[0:3 * H, 0:P], MP[:, n % 2, :, :].rearrange("p k h -> p (k h)"),
                       identb[:]).then_inc(smax_full, 1)
                elif kind == "st":
                    q = pair_at[(n, k)]
                    if k == 0:
                        pe.wait_ge(mrows[n % 2], 48 * (n // 2 + 1))
                    if q >= 2:
                        pe.wait_ge(p_ready, q - 1)
                    for u, (g, j) in enumerate(pairs(i)[k]):
                        o = bank(2 * (q % 2) + u)
                        ins = mm(o, KT[0:KM, b, j * P:(j + 1) * P], QT[0:KM, t, g * HG:(g + 1) * HG, :],
                                 start=True, stop=j < i)
                        if j == i:
                            ins = mm(o, identb[:], mask_st[:].unsqueeze(1).to_broadcast([P, HG, P]), start=False, stop=True)
                    ins.then_inc(st_full, 1)
                elif kind == "pv":
                    q = pair_at[(n, k)]
                    pe.wait_ge(p_ready, q + 1)
                    if k == 0 and n >= 2:
                        pe.wait_ge(x1_ready, n - 1)
                    for u, (g, j) in enumerate(pairs(i)[k]):
                        ins = mm(bank(6 + n % 2)[32 * g:32 * g + 32, :], VX[:, b * NT + j, :], PR[:, q % 3, u, :],
                                 start=j == 0, stop=j == i)
                    ins.then_inc(pv_done, 1)
                elif kind == "ytr":
                    pe.wait_ge(yf_ready, n + 1)
                    for a in range(HG):
                        ins = tr(bank(6 + n % 2)[:, a * P:(a + 1) * P], YF[:, n % 2, a * P:(a + 1) * P], ident[:])
                    ins.then_inc(yf_turned, 1)
                elif kind == "yt":
                    pe.wait_ge(yn_ready, n + 1)
                    for c in range(C):
                        ins = tr(bank(6 + n % 2)[:, c * P:(c + 1) * P], YN[:, n % 2, c * P:(c + 1) * P], ident[:])
                    ins.then_inc(yn_transposed, 1)
                elif kind == "proj":
                    pe.wait_ge(yt_ready, n + 1)
                    for c in range(C):
                        ins = mm(bank(6 + n % 2)[:, D:2 * D], YT[:, n % 2, c, :], wproj[:, c, :], start=c == 0, stop=c == C - 1)
                    ins.then_inc(proj_done, 1)
            pe.wait_ge(x1_ready, N)
            pe.wait_ge(p_ready, len(pair_at))
            with pe.Fori(0, B) as b:
                for i in range(NT):
                    pe.wait_ge(v["xn_ready"], CREDIT + b * NT + (i + 1))
                    pe.wait_ge(v["xt_ready"], CREDIT + b * NT + max(i - 1, 0))
                    for c in range(C):
                        ins = tr(bank(i % 2)[:, c * P:(c + 1) * P], XN[:, i, c * P:(c + 1) * P], ident[:])
                    ins.then_inc(v["xn_transposed"], 1)
                for i in range(NT + 1):
                    if i < NT:
                        pe.wait_ge(v["xt_ready"], CREDIT + b * NT + (i + 1))
                        pe.wait_ge(v["qh_ready"], CREDIT + b * NT + max(i - 1, 0))
                        mm(bank(3 + i % 2)[:, 0:D], ones1[0:1, :], bqkv[0:1, 0:D], start=True, stop=False)
                        for c in range(C):
                            ins = mm(bank(3 + i % 2)[:, 0:D], XT[:, c, i * P:(i + 1) * P], wqkv[:, c, 0:D], start=False,
                                     stop=c == C - 1)
                        ins.then_inc(v["q_done"], 1)
                    if i >= 1:
                        t = i - 1
                        pe.wait_ge(v["qx_ready"], CREDIT + b * NT + (t + 1))
                        pe.wait_ge(v["qt_ready"], CREDIT + b * NT + t)
                        for h in range(H):
                            ins = tr(bank(6 + h // 8).bitcast(BF16)[0:KQ, (h % 8) * P:(h % 8 + 1) * P],
                                     QX[:, t % 2, h, :, :].rearrange("p r d -> p (r d)"), identb[:])
                        ins.then_inc(v["qx_transposed"], 1)
            pe.wait_ge(v["xt_ready"], CREDIT + N)
            pe.wait_ge(v["qh_ready"], CREDIT + N)
            with pe.Fori(0, B) as b:
                for i in range(NT + 1):
                    if i < NT:
                        pe.wait_ge(v["qt_ready"], CREDIT + b * NT + (i + 1))
                        pe.wait_ge(v["smax_free"], CREDIT + b * NT + i)
                        for h in range(H):
                            ins = mm(bank(h // 6)[:, (h % 6) * S:(h % 6 + 1) * S],
                                     QT[0:KQ, bass.ds(b * NT + i, 1), h, :].rearrange("p n t -> p (n t)"),
                                     KT2[0:KQ, bass.ds(b, 1), h, 0:S].rearrange("p n t -> p (n t)"), start=h % 6 == 0,
                                     stop=h % 6 == 5 or h == H - 1, skip_group_check=True)
                        ins.then_inc(v["smax_full"], 1)
                    if i >= 1:
                        t = i - 1
                        pe.wait_ge(v["mp_ready"], CREDIT + b * NT + (t + 1))
                        pe.wait_ge(v["mt_ready"], CREDIT + b * NT + max(t - 1, 0))
                        mm(bank(4 + t % 2)[0:3 * H, 0:P], MP[:, t % 2, :, :].rearrange("p k h -> p (k h)"),
                           identb[:], start=True, stop=True).then_inc(v["mt_full"], 1)
            pe.wait_ge(v["mt_ready"], CREDIT + N)
            pe.wait_ge(v["smax_free"], CREDIT + N)
            with pe.Fori(0, B) as b:
                for i in range(NT + 3):
                    if i < NT:
                        pe.wait_ge(vrows[i % 2], CREDIT + b * (48 * NT // 2) + 48 * (i // 2 + 1))
                        for q in (2 * i, 2 * i + 1):
                            pe.wait_ge(v["p_ready"], CREDIT + b * (2 * NT) + max(q - 1, 0))
                            for a in range(8):
                                h = (q % 2) * 8 + a
                                ins = mm(bank(4 + 2 * (q % 2) + a // 4)[0:S, (a % 4) * P:(a % 4 + 1) * P],
                                         KT2[0:KM, bass.ds(b, 1), h, 0:S].rearrange("p n t -> p (n t)"),
                                         QT[0:KM, bass.ds(b * NT + i, 1), h, :].rearrange("p n t -> p (n t)"),
                                         start=a % 4 == 0, stop=a % 4 == 3, skip_group_check=True)
                            ins.then_inc(v["st_full"], 1)
                    if 1 <= i <= NT:
                        t = i - 1
                        pe.wait_ge(v["x2_ready"], CREDIT + b * NT + max(t - 2, 0))
                        for q in (2 * t, 2 * t + 1):
                            pe.wait_ge(v["p_ready"], CREDIT + b * (2 * NT) + (q + 1))
                            for a in range(8):
                                h = (q % 2) * 8 + a
                                ins = mm(bank(t % 3)[:, h * HV:(h + 1) * HV],
                                         PR[0:S, q % 3, a // 4, (a % 4) * P:(a % 4 + 1) * P],
                                         V2X[:, bass.ds(b, 1), h, :].rearrange("p n t -> p (n t)"), start=h == 0, stop=h == H - 1,
                                         skip_group_check=True)
                            ins.then_inc(v["pv_done"], 1)
                    if 2 <= i <= NT + 1:
                        t = i - 2
                        pe.wait_ge(v["yn_ready"], CREDIT + b * NT + (t + 1))
                        for c in range(C):
                            ins = tr(bank(t % 3)[:, c * P:(c + 1) * P], YN[:, t % 2, c * P:(c + 1) * P], ident[:])
                        ins.then_inc(v["yn_transposed"], 1)
                    if i >= 3:
                        t = i - 3
                        pe.wait_ge(v["yt_ready"], CREDIT + b * NT + (t + 1))
                        mm(bank(t % 3)[:, D:2 * D], ones1[0:1, :], bout[0:1, :], start=True, stop=False)
                        for c in range(C):
                            ins = mm(bank(t % 3)[:, D:2 * D], YT[:, t % 2, c, :], wout[:, c, :], start=False, stop=c == C - 1)
                        ins.then_inc(v["proj_done"], 1)
            pe.wait_ge(v["x2_ready"], CREDIT + N)
            with pe.Fori(0, B) as b:
                for i in range(NT):
                    pe.wait_ge(rt["xn_ready"], CREDIT + b * NT + (i + 1))
                    pe.wait_ge(rt["xt_ready"], CREDIT + b * NT + max(i - 1, 0))
                    for c in range(C):
                        ins = tr(bank(i % 2)[:, c * P:(c + 1) * P], XN[:, i, c * P:(c + 1) * P], ident[:])
                    ins.then_inc(rt["xn_transposed"], 1)
                for i in range(NT):
                    pe.wait_ge(rt["xt_ready"], CREDIT + b * NT + (i + 1))
                    for c in range(C):
                        ins = mm(bank(2)[:, i * E:(i + 1) * E], XT[:, c, i * P:(i + 1) * P], gateT[:, c, :],
                                 start=i == 0 and c == 0, stop=c == C - 1, skip_group_check=True)
                ins.then_inc(rt["lg_done"], 1)
            for u in range(N):
                pe.wait_ge(rt["g_ready"], CREDIT + B)
                if u >= 2:
                    pe.wait_ge(e["gt_ready"], CREDIT + u - 1)
                tr(bank(u % 2)[0:E, 0:P], GT[:, u, :], ident[:]).then_inc(e["gt_done"], 1)
                pe.wait_ge(e["gt_ready"], CREDIT + u + 1)
                if u >= 2:
                    pe.wait_ge(e["b2_used"], CREDIT + u - 1)
                mm(bank(2 + u % 2)[:, 0:D], gT[:, u % 2, :], b2sb[:], start=True, stop=True).then_inc(e["b2_done"], 1)
            pe.wait_ge(e["b2_used"], CREDIT + N)
            pe.wait_ge(rt["kept"], CREDIT + B)
            with pe.Fori(0, E // 2) as u:
                for a in range(2):
                    pe.wait_ge(e["w_loaded%d" % a], u * 48 + 48)
                    for q in range(4):
                        for f in range(FC):
                            k = (a * 4 + q) * FC + f
                            pe.wait_ge(e["h_ready"], CREDIT + u * (8 * FC) + max(k - 3, 0))
                            for c in range(C):
                                ins = mm(bank(k % 4), w1sb[:, a, c, f:F:FC],
                                         XT3[:, q // 2, c, (q % 2) * 512:(q % 2 + 1) * 512], start=c == 0, stop=c == C - 1)
                            ins.then_inc(e["h_done"], 1)
                        pe.wait_ge(e["h_ready"], CREDIT + u * (8 * FC) + ((a * 4 + q + 1) * FC))
                        for m in range(4):
                            k = a * N + q * 4 + m
                            pe.wait_ge(e["o_used"], CREDIT + u * (2 * N) + max(k - 3, 0))
                            for f in range(FC):
                                ins = mm(bank(4 + k % 4)[:, 0:D], HT[:, q % 2, f, m * P:(m + 1) * P], w2sb[:, a, f, :],
                                         start=f == 0, stop=f == FC - 1)
                            ins.then_inc(e["o_done"], 1)


_INS = ['x', 'ctx_1024', 'L0_attn_Wc_down', 'L0_attn_Wq_up', 'L0_attn_Wkv_up', 'L0_attn_Wc_proj', 'L0_xattn_W_qkv',
        'L0_xattn_b_qkv', 'L0_xattn_W_out', 'L0_xattn_b_out', 'L0_ffn_gate_w', 'L0_ffn_w1', 'L0_ffn_b1', 'L0_ffn_w2',
        'L0_ffn_b2']
_OUTS = [((2, 1024, 256), 'float32')]


def kernel(**inputs):
    import numpy as _np
    import concourse.bacc as _bacc
    from concourse import mybir as _mybir
    from concourse.bass_utils import run_bass_kernel_spmd as _run

    nc = _bacc.Bacc("TRN2", target_bir_lowering=False, num_devices=1)
    arrays, args = {}, []
    for name in _INS:
        a = _np.ascontiguousarray(inputs[name])
        arrays[f"in_{name}_dram"] = a
        args.append(nc.dram_tensor(f"in_{name}_dram", a.shape, _mybir.dt.from_np(a.dtype), kind="ExternalInput").ap())
    for i, (shape, dtype) in enumerate(_OUTS):
        dt = _mybir.dt.from_np(_np.dtype(dtype))
        args.append(nc.dram_tensor(f"out_{i}_dram", shape, dt, kind="ExternalOutput").ap())
    decoder_layer(nc, *args)
    r = _run(nc, [arrays], core_ids=[0])
    got = tuple(r.results[0][f"out_{i}_dram"] for i in range(len(_OUTS)))
    return got[0]
```

```python
from contextlib import ExitStack

import concourse.bass as bass
from concourse import mybir

ALU = mybir.AluOpType
ACT = mybir.ActivationFunctionType
BF16 = mybir.dt.bfloat16
F16 = mybir.dt.float16
U32 = mybir.dt.uint32
I32 = mybir.dt.int32
F32 = mybir.dt.float32
AX_X = mybir.AxisListType.X

P = 128
EPS = 1e-5
CREDIT = 1
BIG = -1.0e30
UP = 64.0
SPLIT = 6


def decoder_layer(nc, x, ctx_in, w_down, w_qup, w_kvup, w_proj, w_qkv, b_qkv, w_out, b_out,
                  gate_w, w1, b1, w2, b2, out):
    B, T, D = x.shape
    S = ctx_in.shape[1]
    E, _, F = w1.shape
    HD = w_kvup.shape[1] // 2
    H = D // HD
    LAT = w_down.shape[1]
    C = D // P
    FC = F // P
    NT = T // P
    N = B * NT
    KQ = SPLIT * HD
    KM = KQ + 3
    HV = HD + 1
    HG = 4
    G = H // HG
    SCALE = float(HD) ** -0.5
    SP = 80
    NX = (2 * T * B + E * (P - 1)) // P
    NX += (NX + 1) % 2
    LEVELS = T * B // P
    WPE = C * F
    assert LAT == P and WPE == FC * D and KQ <= 96 and HG * P == 512 and S <= SP

    ZERO = [(k, min(k + 2 * WPE // D, NX)) for k in range(0, NX, 2 * WPE // D)]

    with ExitStack() as stack:
        def sb(name, shape, dt=F32):
            return stack.enter_context(nc.sbuf_tensor(name, shape, dt))

        def sem(name):
            return stack.enter_context(nc.semaphore(name))

        ps = stack.enter_context(nc.psum_tensor("ps", [P, 8, 512], F32))

        def bank(k):
            return ps[:, k, :]

        X = sb("X", [P, N, D])
        WORDS = E * 2 * WPE
        BIGBUF = sb("BIGBUF", [P, WORDS])
        taken = [0]

        def place(shape, dt=F32, src=None):
            count = 1
            for k in shape:
                count *= k
            words = count // 2 if dt == BF16 else count
            flat = BIGBUF[:] if src is None else src[:].rearrange("p n d -> p (n d)")
            piece = flat[:, taken[0]:taken[0] + words]
            taken[0] += words
            assert taken[0] <= flat.shape[1]
            if dt == BF16:
                piece = piece.bitcast(BF16)
            axes = "abcde"[:len(shape)]
            if len(shape) == 1:
                return piece
            return piece.rearrange("p (%s) -> p %s" % (" ".join(axes), " ".join(axes)), **dict(zip(axes, shape)))

        QT = place([N, H, P], BF16)
        QF = place([NT, D + 2 * HD])
        QX = place([2, H, SPLIT, HD], BF16)
        qrest = place([H, HD])
        KX = place([NT, KQ + 16], BF16)
        KX2 = place([B, H, KQ + 16], BF16)[0:S]
        KV2 = place([B, 2 * D])[0:S]
        KT = place([B, T], BF16)
        LT = place([T])
        wdown = place([C, LAT])
        wqkvup = place([D + 2 * HD])
        wproj = place([C, D])
        wqkv = place([C, 3 * D])
        W16 = BIGBUF[:].bitcast(F16).rearrange("p (e m h x) -> p e m h x", e=E, m=2, h=2)
        XN = sb("XN", [P, NT, D])
        XT = sb("XT", [P, C, T])
        ARENA = sb("ARENA", [P, E * D])
        PR = ARENA[:, 0:3 * 2 * 512].rearrange("p (a u t) -> p a u t", a=3, u=2)
        YN = ARENA[:, 3 * 2 * 512:3 * 2 * 512 + 2 * D].rearrange("p (a d) -> p a d", a=2)
        b2all = ARENA[:].rearrange("p (e d) -> p e d", e=E)
        STG = [sb("STG", [P, 2 * WPE])[:], XN[:].rearrange("p n d -> p (n d)")]
        XN3 = sb("XN3", [P, N, D])
        taken[0] = 0
        CX = place([B, D], src=XN3)[0:S]
        CT = place([B, C, S], src=XN3)
        krest2 = place([H, HD], src=XN3)[0:S]
        krest = place([NT, HD], src=XN3)
        gaterow = place([D], src=XN3)[0:E]
        b1row = place([F], src=XN3)[0:E]
        VX = place([N, 32], src=XN3)
        V2X = place([B, H, 32], src=XN3)[0:S]
        bqkv = sb("bqkv", [1, 3 * D])
        wout = sb("wout", [P, C, D])
        bout = sb("bout", [P, D])
        gateT = sb("gateT", [P, C, E])
        b1T = sb("b1T", [P, FC, E])
        ident = sb("ident", [P, P])
        identb = sb("identb", [P, P], BF16)
        mask_ts = sb("mask_ts", [P, P], BF16)
        mask_st = sb("mask_st", [P, P], BF16)
        before = sb("before", [P, P], BF16)
        onesb = sb("onesb", [P, P], BF16)
        ones1 = sb("ones1", [1, P])
        halfneg = sb("halfneg", [P, N])
        stats = sb("stats", [P, NT, 6])
        mv = sb("mv", [P, NT, 2])
        ve = sb("ve", [P, NT])
        rstd = sb("rstd", [P, NT])
        KT2 = sb("KT2", [P, B, H, SP], BF16)
        nmx = sb("nmx", [P, 2, 2, H])
        nm = sb("nm", [P, 2, H])
        mrest = sb("mrest", [P, H])
        MP = sb("MP", [P, 2, 3, H], BF16)
        MT = sb("MT", [3 * H, 2, P], BF16)
        rinv = sb("rinv", [P, 2, H])
        YF = XT[:, 0, :].rearrange("p (a t) -> p a t", a=2)
        YT = sb("YT", [P, 2, C, P])
        lg = sb("lg", [P, NT, E])
        scratch = sb("scratch", [P, 1])
        scratch_act = sb("scratch_act", [P, 2])
        ones_act = sb("ones_act", [P, 1])
        zerosH = sb("zerosH", [P, H])
        top = sb("top", [P, NT, 8])
        ex = sb("ex", [P, NT, E])
        pr = sb("pr", [P, NT, E])
        lmax = sb("lmax", [P, NT])
        lsum = sb("lsum", [P, NT])
        tix = sb("tix", [P, NT, 8], U32)
        rank = sb("rank", [P, NT, 2])
        wsum = sb("wsum", [P, NT])
        wts = sb("wts", [P, N, 2])
        hot = sb("hot", [P, 2, N, E])
        hotb = sb("hotb", [P, N, E], BF16)
        iotai = sb("iotai", [P, NX], I32)
        iotaf = sb("iotaf", [P, NX])
        cnt = sb("cnt", [P, E])
        tiles = sb("tiles", [P, E])
        earlier = sb("earlier", [P, E, E])
        first = sb("first", [P, E])
        upto = sb("upto", [P, E])
        slotf = sb("slotf", [P, 2, N])
        slot = sb("slot", [P, 2, N], U32)
        taken[0] = 0
        levels = place([E, LEVELS], src=XT)
        place_of = place([N, E], src=XT)
        tilesum = place([NX, E], src=XT)[0:1]
        tef = sb("tef", [1, NX])
        TE = sb("TE", [1, NX], I32)
        XG = XN[:, 0:2, :]
        X16 = XN[:, 2:4, :].rearrange("p a d -> p (a d)").bitcast(F16).rearrange("p (a h c t) -> p a h c t", a=2, h=2, c=C)
        YS = XN[:, 4:6, :]
        HF = XT[:, 0, :].rearrange("p (a f) -> p a f", a=2)
        H16 = XT[:, 1, :].bitcast(F16).rearrange("p (a h f) -> p a h f", a=2, h=2)
        RET = BIGBUF[:, 0:2 * N * D].rearrange("p (k n d) -> p k n d", k=2, n=N)
        FINAL = BIGBUF[:, 2 * N * D:3 * N * D].rearrange("p (n d) -> p n d", n=N)
        XS = nc.dram_tensor("sorted_in", (NX * P, D), F32, kind="Internal").ap()
        YD = nc.dram_tensor("sorted_out", (NX * P, D), F32, kind="Internal").ap()

        names = """x_loaded w_loaded ctx_loaded consts zeros_set var_ready rstd_ready xn_ready xn_transposed
            xt_ready lat_done lat_ready qkv_done qf_ready qh_ready qx_ready qx_transposed qt_ready kx_ready kx_transposed kt_ready
            cx_transposed ct_ready kv2_done kv2_ready kx2_ready kx2_transposed kt2_ready""".split()
        s = {k: sem(k) for k in names}
        dve_chain, pool_chain = sem("dve_chain"), sem("pool_chain")
        smax_full, smax_free = sem("smax_full"), sem("smax_free")
        mt_ready = sem("mt_ready")
        nm_ready, mp_ready = sem("nm_ready"), sem("mp_ready")
        mrows = [sem("mrows_even"), sem("mrows_odd")]
        st_full, p_ready, pv_done = sem("st_full"), sem("p_ready"), sem("pv_done")
        yn_ready, yn_transposed, yt_ready = sem("yn_ready"), sem("yn_transposed"), sem("yt_ready")
        yf_ready, yf_turned = sem("yf_ready"), sem("yf_turned")
        proj_done, x1_ready = sem("proj_done"), sem("x1_ready")
        stored = sem("stored")
        s_small = sem("small_loaded")
        smallT, smallT_ready = sem("small_transposed"), sem("smallT_ready")
        v = {k: sem("x_" + k) for k in """var_ready rstd_ready xn_ready xn_transposed xt_ready q_done qf_ready qh_ready qx_ready
            qx_transposed qt_ready smax_full smax_free mp_ready mt_full mt_ready st_full p_ready pv_done yf_ready yf_turned
            yn_ready yn_transposed yt_ready proj_done x2_ready""".split()}
        vrows = [sem("x_mrows_even"), sem("x_mrows_odd")]
        rt = {k: sem("r_" + k) for k in """var_ready rstd_ready xn_ready xn_transposed xt_ready lg_done lg_ready ex_ready
            hot_ready""".split()}
        zeros_ready, zeroed, b2_loaded = sem("zeros_ready"), sem("zeroed_loaded"), sem("b2_loaded")
        ranked, slot_ready, te_ready, scattered = sem("ranked"), sem("slot_ready"), sem("te_ready"), sem("scattered")
        stg_loaded = [sem("stg_loaded_even"), sem("stg_loaded_odd")]
        w = {k: sem("w_" + k) for k in "hi_ready lo_ready".split()}
        xg_loaded = [sem("xg_loaded_even"), sem("xg_loaded_odd")]
        e = {k: sem("e_" + k) for k in """xg_transposed xh_ready xl_ready up_done act_ready hh_ready hl_ready down_done
            y_ready""".split()}
        ys_stored = [sem("ys_stored_even"), sem("ys_stored_odd")]
        returned = [sem("returned_%d" % g) for g in range(4)]
        fin_ready = sem("fin_ready")

        credited = [q for group in (s, v, rt, w, e) for name, q in group.items() if "loaded" not in name and name != "consts"]
        credited += vrows + ys_stored

        items = [(0, i) for i in range(NT)] + [(1, i) for i in reversed(range(NT))]
        LEAD = 2

        def max_tiles(i):
            keys = (i + 1) * P
            head = min(keys, 512)
            hb = 512 // head
            tiles = [(h, hb, 0, head, 0) for h in range(0, H, hb)]
            if keys > 512:
                hb = 512 // (keys - 512)
                tiles += [(h, hb, 512, keys - 512, 1) for h in range(0, H, hb)]
            return tiles

        def pairs(i):
            units = [(g, j) for j in range(i + 1) for g in range(G)]
            return [units[k:k + 2] for k in range(0, len(units), 2)]

        def schedule():
            order = []
            for n in range(min(LEAD, N)):
                order += [("max", n, k) for k in range(len(max_tiles(items[n][1])))] + [("mt", n, 0)]
            flat = [(n, p) for n in range(N) for p in range(len(pairs(items[n][1])))]
            order += [("st",) + flat[0]]
            for q, (n, p) in enumerate(flat):
                np_ = len(pairs(items[n][1]))
                if q + 1 < len(flat):
                    order += [("st",) + flat[q + 1]] if flat[q + 1][0] == n else []
                if n + LEAD < N:
                    m = [("max", n + LEAD, k) for k in range(len(max_tiles(items[n + LEAD][1])))]
                    lo, hi = len(m) * p // np_, len(m) * (p + 1) // np_
                    order += m[lo:hi]
                    if p == np_ - 1:
                        order += [("mt", n + LEAD, 0)]
                if q + 1 < len(flat) and flat[q + 1][0] != n:
                    order += [("st",) + flat[q + 1]]
                order += [("pv", n, p)]
                if n > 0:
                    after = [("ytr", n - 1, 0), ("yt", n - 1, 0), ("proj", n - 1, 0)]
                    order += after[p:p + 1]
                    if p == np_ - 1:
                        order += after[p + 1:]
            return order + [("ytr", N - 1, 0), ("yt", N - 1, 0), ("proj", N - 1, 0)]

        order = schedule()
        ring = [o for o in order if o[0] in ("max", "mt")]
        ring_at = {o: k for k, o in enumerate(ring)}

        def maxima_to(r):
            return sum(o[0] == "max" for o in ring[:r + 1])

        def chunks(i):
            return 2 if (i + 1) * P > 512 else 1

        pair_at = {}
        for n in range(N):
            for p in range(len(pairs(items[n][1]))):
                pair_at[(n, p)] = len(pair_at)

        block = stack.enter_context(nc.Block())

        @block.sync
        def _(sp):
            sp.dma_start(X[:, 0:NT, :], x[0].rearrange("(n p) d -> p n d", p=P)).then_inc(s["x_loaded"], 16)
            sp.dma_start(X[:, NT:N, :], x[1].rearrange("(n p) d -> p n d", p=P)).then_inc(s["x_loaded"], 16)
            for q in credited:
                sp.sem_inc(q, CREDIT)
            for b in range(B):
                sp.dma_start(CX[:, b, :], ctx_in[b]).then_inc(s["ctx_loaded"], 16)
            for n in range(N):
                sp.wait_ge(mt_ready, n + 1)
                b, i = items[n]
                for k in range(3):
                    sp.dma_start(QT[KQ + k:KQ + k + 1, b * NT + i, :, :],
                                 MT[k * H:(k + 1) * H, n % 2, :]).then_inc(mrows[n % 2], 16)
            with sp.Fori(0, B) as b:
                for i in range(NT):
                    sp.wait_ge(v["mt_ready"], CREDIT + b * NT + (i + 1))
                    for k in range(3):
                        sp.dma_start(QT[KQ + k:KQ + k + 1, bass.ds(b * NT + i, 1), :, :].rearrange("p n h t -> p (n h) t"),
                                     MT[k * H:(k + 1) * H, i % 2, :]).then_inc(vrows[i % 2], 16)
            sp.wait_ge(zeroed, 16 * len(ZERO))
            with sp.Fori(0, E // 2) as u:
                for a in range(2):
                    sp.wait_ge(w["hi_ready"], CREDIT + u * 2 + max(a - 1, 0))
                    sp.wait_ge(w["lo_ready"], CREDIT + u * 2 + max(a - 1, 0))
                    expert = bass.ds(u * 2 + a, 1)
                    sp.dma_start(STG[a][:, 0:WPE].rearrange("p (c f) -> p c f", c=C),
                                 w1[expert].rearrange("e (c p) f -> p (e c) f", p=P)).then_inc(stg_loaded[a], 16)
                    sp.dma_start(STG[a][:, WPE:2 * WPE].rearrange("p (c f) -> p c f", c=FC),
                                 w2[expert].rearrange("e (c p) f -> p (e c) f", p=P)).then_inc(stg_loaded[a], 16)
            sp.wait_ge(v["x2_ready"], CREDIT + N)
            sp.dma_start(b2all[:], b2.rearrange("e d -> (e d)").partition_broadcast(P).rearrange("p (e d) -> p e d", e=E)
                         ).then_inc(b2_loaded, 16)

            def load(u, c):
                if not isinstance(u, int) or u * 2 + c >= 2:
                    sp.wait_ge(e["xg_transposed"], CREDIT + u * 2 + (c - 1))
                sp.dma_start(XG[:, c % 2, :], XS[bass.ds((u * 2 + c) * P, P)]).then_inc(xg_loaded[c % 2], 16)

            def store(u, c):
                sp.wait_ge(e["y_ready"], CREDIT + u * 2 + (c + 1))
                sp.dma_start(YD[bass.ds((u * 2 + c) * P, P)], YS[:, c % 2, :]).then_inc(ys_stored[c % 2], 16)

            sp.wait_ge(w["lo_ready"], CREDIT + E)
            sp.wait_ge(scattered, 16 * 2 * N)
            for c in range(3):
                load(0, c)
            with sp.Fori(0, (NX - 3) // 2) as u:
                for c in range(2):
                    load(u, c + 3)
                    store(u, c)
            for c in range(3):
                store(0, NX - 3 + c)
            for g in range(4):
                sp.wait_ge(fin_ready, g + 1)
                sp.dma_start(out.rearrange("b (n p) d -> p (b n) d", p=P)[:, g * (N // 4):(g + 1) * (N // 4), :],
                             FINAL[:, g * (N // 4):(g + 1) * (N // 4), :]).then_inc(stored, 16)
            sp.wait_ge(stored, 16 * 4)

        @block.gpsimd
        def _(pool):
            chain = [0]

            def link(ins):
                chain[0] += 1
                ins.then_inc(pool_chain, 1)
                pool.wait_ge(pool_chain, chain[0])

            def stepper(b, base, per):
                local = [0]

                def step(ins):
                    local[0] += 1
                    assert local[0] <= per
                    ins.then_inc(pool_chain, 1)
                    pool.wait_ge(pool_chain, b * per + (base + local[0]))
                return step

            link(nc.gpsimd.memset(ident[:], 0.0))
            link(nc.gpsimd.affine_select(out=ident[:], in_=ident[:], compare_op=ALU.not_equal, fill=1.0, base=0,
                                         pattern=[[-1, P]], channel_multiplier=1))
            link(nc.gpsimd.tensor_copy(identb[:], ident[:]))
            link(nc.gpsimd.memset(mask_ts[:], 0.0))
            link(nc.gpsimd.affine_select(out=mask_ts[:], in_=mask_ts[:], compare_op=ALU.is_ge, fill=BIG, base=0,
                                         pattern=[[-1, P]], channel_multiplier=1))
            link(nc.gpsimd.memset(mask_st[:], 0.0))
            link(nc.gpsimd.affine_select(out=mask_st[:], in_=mask_st[:], compare_op=ALU.is_ge, fill=BIG, base=0,
                                         pattern=[[1, P]], channel_multiplier=-1))
            link(nc.gpsimd.memset(ones1[:], 1.0))
            link(nc.gpsimd.memset(halfneg[:], -0.5))
            link(nc.gpsimd.memset(KX[:], 1.0))
            link(nc.gpsimd.memset(KX2[:], 1.0))
            link(nc.gpsimd.memset(VX, 0.0))
            link(nc.gpsimd.memset(VX[:, :, HD:HV], 1.0))
            link(nc.gpsimd.memset(V2X, 0.0))
            link(nc.gpsimd.memset(V2X[:, :, :, HD:HV], 1.0))
            link(nc.gpsimd.memset(zerosH[:], 0.0))
            link(nc.gpsimd.iota(iotai[:], [[1, NX]], base=0, channel_multiplier=0))
            link(nc.gpsimd.memset(onesb[:], 1.0))
            link(nc.gpsimd.memset(before[:], 1.0))
            link(nc.gpsimd.affine_select(out=before[:], in_=before[:], compare_op=ALU.is_gt, fill=0.0, base=0,
                                         pattern=[[1, P]], channel_multiplier=-1))
            link(nc.gpsimd.memset(earlier[:], 1.0))
            link(nc.gpsimd.affine_select(out=earlier[:], in_=earlier[:], compare_op=ALU.is_gt, fill=0.0, base=0,
                                         pattern=[[1, E], [-1, E]], channel_multiplier=0))
            nc.gpsimd.tensor_copy(iotaf[:], iotai[:]).then_inc(s["consts"], 1)
            for b in range(B):
                pool.wait_ge(s["kv2_ready"], CREDIT + b + 1)
                k = KV2[:, b, 0:D].rearrange("p (h d) -> p h d", h=H)
                part = [KX2[:, b, :, q * HD:(q + 1) * HD] for q in range(SPLIT)]
                for q in (3, 5):
                    nc.gpsimd.tensor_copy(part[q], k)
                link(nc.gpsimd.tensor_copy(part[0], k))
                link(nc.gpsimd.tensor_tensor(krest2[:], k, part[0], ALU.subtract))
                nc.gpsimd.tensor_copy(part[4], krest2[:])
                link(nc.gpsimd.tensor_copy(part[1], krest2[:]))
                nc.gpsimd.tensor_copy(V2X[:, b, :, 0:HD], KV2[:, b, D:2 * D].rearrange("p (h d) -> p h d", h=H))
                nc.gpsimd.tensor_tensor(part[2], krest2[:], part[1], ALU.subtract).then_inc(s["kx2_ready"], 1)
            base = chain[0]
            with pool.Fori(0, B) as b:
                pool.wait_ge(s["var_ready"], CREDIT + b + 1)
                nc.gpsimd.tensor_tensor(rstd[:, :], ve[:, :], halfneg[:, 0:NT], ALU.pow).then_inc(s["rstd_ready"], 1)
                step = stepper(b, base, NT)
                for i in range(NT):
                    q = QF[:, i, 0:D].rearrange("p (h d) -> p h d", h=H)
                    xq = QX[:, i % 2]
                    pool.wait_ge(s["qf_ready"], CREDIT + b * NT + (i + 1))
                    pool.wait_ge(s["qx_ready"], CREDIT + b * NT + i)
                    pool.wait_ge(s["qh_ready"], CREDIT + b * NT + (i + 1))
                    nc.gpsimd.tensor_tensor(qrest[:], q, xq[:, :, 0, :], ALU.subtract)
                    nc.gpsimd.tensor_tensor(xq[:, :, 3, :], q, xq[:, :, 0, :], ALU.subtract)
                    step(nc.gpsimd.tensor_tensor(xq[:, :, 4, :], q, xq[:, :, 0, :], ALU.subtract))
                    nc.gpsimd.tensor_tensor(xq[:, :, 5, :], qrest[:], xq[:, :, 3, :],
                                            ALU.subtract).then_inc(s["qx_ready"], 1)
            chain[0] += B * NT
            for n in range(N):
                if chunks(items[n][1]) == 1:
                    pool.wait_ge(smax_free, maxima_to(ring_at[("mt", n, 0)]))
                else:
                    pool.wait_ge(nm_ready, sum(chunks(i) == 2 for _, i in items[:n + 1]))
                if n >= 2:
                    pool.wait_ge(mt_ready, n - 1)
                m = nm[:, n % 2, :]
                link(nc.gpsimd.tensor_copy(MP[:, n % 2, 0, :], m))
                link(nc.gpsimd.tensor_tensor(mrest[:], m, MP[:, n % 2, 0, :], ALU.subtract))
                link(nc.gpsimd.tensor_copy(MP[:, n % 2, 1, :], mrest[:]))
                nc.gpsimd.tensor_tensor(MP[:, n % 2, 2, :], mrest[:], MP[:, n % 2, 1, :],
                                        ALU.subtract).then_inc(mp_ready, 1)

            with pool.Fori(0, B) as b:
                step = stepper(b, chain[0], NT)
                pool.wait_ge(v["var_ready"], CREDIT + b + 1)
                nc.gpsimd.tensor_tensor(rstd[:, :], ve[:, :], halfneg[:, 0:NT], ALU.pow).then_inc(v["rstd_ready"], 1)
                for i in range(NT):
                    q = QF[:, i, 0:D].rearrange("p (h d) -> p h d", h=H)
                    xq = QX[:, i % 2]
                    pool.wait_ge(v["qf_ready"], CREDIT + b * NT + (i + 1))
                    pool.wait_ge(v["qx_ready"], CREDIT + b * NT + i)
                    pool.wait_ge(v["qh_ready"], CREDIT + b * NT + (i + 1))
                    nc.gpsimd.tensor_tensor(qrest[:], q, xq[:, :, 0, :], ALU.subtract)
                    nc.gpsimd.tensor_tensor(xq[:, :, 3, :], q, xq[:, :, 0, :], ALU.subtract)
                    step(nc.gpsimd.tensor_tensor(xq[:, :, 4, :], q, xq[:, :, 0, :], ALU.subtract))
                    nc.gpsimd.tensor_tensor(xq[:, :, 5, :], qrest[:], xq[:, :, 3, :],
                                            ALU.subtract).then_inc(v["qx_ready"], 1)
            chain[0] += B * NT
            with pool.Fori(0, B) as b:
                step = stepper(b, chain[0], 2 * NT)
                for i in range(NT):
                    pool.wait_ge(v["smax_free"], CREDIT + b * NT + (i + 1))
                    pool.wait_ge(v["mt_ready"], CREDIT + b * NT + max(i - 1, 0))
                    m = nm[:, i % 2, :]
                    pool.wait_ge(v["mp_ready"], CREDIT + b * NT + i)
                    step(nc.gpsimd.tensor_tensor(MP[:, i % 2, 0, :], m, zerosH[:], ALU.add))
                    nc.gpsimd.tensor_tensor(mrest[:], m, MP[:, i % 2, 0, :], ALU.subtract)
                    step(nc.gpsimd.tensor_tensor(MP[:, i % 2, 1, :], m, MP[:, i % 2, 0, :], ALU.subtract))
                    nc.gpsimd.tensor_tensor(MP[:, i % 2, 2, :], mrest[:], MP[:, i % 2, 1, :],
                                            ALU.subtract).then_inc(v["mp_ready"], 1)
            chain[0] += B * 2 * NT
            with pool.Fori(0, B) as b:
                pool.wait_ge(rt["var_ready"], CREDIT + b + 1)
                nc.gpsimd.tensor_tensor(rstd[:, :], ve[:, :], halfneg[:, 0:NT], ALU.pow).then_inc(rt["rstd_ready"], 1)
            pool.wait_ge(slot_ready, 1)
            pool.wait_ge(zeroed, 16 * len(ZERO))
            for n in range(N):
                for k in range(2):
                    nc.gpsimd.indirect_dma_start(XS, bass.IndirectOffsetOnAxis(slot[:, k, n:n + 1], 0), XN3[:, n, :],
                                                 None).then_inc(scattered, 16)
            for a in range(2):
                pool.wait_ge(ys_stored[a], CREDIT + 16 * ((NX + 1 - a) // 2))
            for n in range(N):
                for k in range(2):
                    nc.gpsimd.indirect_dma_start(RET[:, k, n, :], None, YD,
                                                 bass.IndirectOffsetOnAxis(slot[:, k, n:n + 1], 0)
                                                 ).then_inc(returned[n // (N // 4)], 16)

        @block.scalar
        def _(act):
            def apart(a):
                nc.scalar.copy(scratch_act[:, a:a + 1], ones_act[:])

            def first_parts(b, i, sems):
                act.wait_ge(sems["qx_transposed"], CREDIT + b * NT + max(i - 1, 0))
                nc.scalar.copy(QX[:, i % 2, :, 0:3, :],
                               bank(3 + i % 2)[:, 0:D].rearrange("p (h d) -> p h d", h=H).unsqueeze(2)
                               .to_broadcast([P, H, 3, HD])).then_inc(sems["qh_ready"], 1)

            act.dma_start(wdown[:], w_down.rearrange("(c p) n -> p c n", p=P)).then_inc(s["w_loaded"], 16)
            act.dma_start(wqkvup[:, 0:D], w_qup).then_inc(s["w_loaded"], 16)
            act.dma_start(wqkvup[:, D:D + 2 * HD], w_kvup).then_inc(s["w_loaded"], 16)
            act.dma_start(wproj[:], w_proj.rearrange("(c p) n -> p c n", p=P)).then_inc(s["w_loaded"], 16)
            act.dma_start(wqkv[:], w_qkv.rearrange("(c p) n -> p c n", p=P)).then_inc(s_small, 16)
            act.dma_start(bqkv[:], b_qkv.rearrange("(a n) -> a n", a=1)).then_inc(s_small, 16)
            act.dma_start(wout[:], w_out.rearrange("(c p) n -> p c n", p=P)).then_inc(s_small, 16)
            act.dma_start(bout[:], b_out.partition_broadcast(P)).then_inc(s_small, 16)
            act.dma_start(gaterow[:], gate_w).then_inc(s_small, 16)
            act.dma_start(b1row[:], b1).then_inc(s_small, 16)
            act.wait_ge(zeros_ready, 1)
            for lo, hi in ZERO:
                act.dma_start(XS[lo * P:hi * P].rearrange("(n p) d -> p n d", p=P),
                              STG[0][:, 0:(hi - lo) * D].rearrange("p (n d) -> p n d", d=D)
                              ).then_inc(zeroed, 16)
            act.wait_ge(s["cx_transposed"], CREDIT + 1)
            nc.scalar.copy(CT[:], bank(0)[:, 0:B * C * S].rearrange("p (b c s) -> p b c s", b=B, c=C)).then_inc(s["ct_ready"], 1)
            nc.scalar.copy(gateT[:], bank(1)[:, 0:C * E].rearrange("p (c e) -> p c e", c=C)).then_inc(s["ct_ready"], 1)
            nc.scalar.copy(b1T[:], bank(1)[:, C * E:(C + FC) * E].rearrange("p (c e) -> p c e", c=FC)).then_inc(s["ct_ready"], 1)
            for b in range(B):
                act.wait_ge(s["kv2_done"], CREDIT + b + 1)
                nc.scalar.copy(KV2[:, b, :], bank(2 + b)[0:S, :]).then_inc(s["kv2_ready"], 1)
            for b in range(B):
                act.wait_ge(s["kx2_transposed"], CREDIT + b + 1)
                nc.scalar.copy(KT2[0:KM, b, :, 0:S].rearrange("p (a h) s -> p a h s", a=2),
                               ps[:, 4 + 2 * b:6 + 2 * b, :].bitcast(BF16)[0:KM, :, 0:8 * SP].rearrange("p a (h s) -> p a h s", s=SP)[:, :, :, 0:S]
                               ).then_inc(s["kt2_ready"], 1)
            with act.Fori(0, B) as b:
                for i in range(NT):
                    act.wait_ge(s["xn_transposed"], CREDIT + b * NT + (i + 1))
                    act.wait_ge(s["lat_done"], CREDIT + b * 2)
                    nc.scalar.copy(XT[:, :, i * P:(i + 1) * P],
                                   bank(i % 2)[:, 0:C * P].rearrange("p (c t) -> p c t", c=C)).then_inc(s["xt_ready"], 1)
                    if i % 4 == 3:
                        g = i // 4
                        act.wait_ge(s["lat_done"], CREDIT + b * 2 + (g + 1))
                        act.wait_ge(s["qkv_done"], CREDIT + b * NT)
                        nc.scalar.copy(LT[:, g * 512:(g + 1) * 512], bank(2)).then_inc(s["lat_ready"], 1)
                for i in range(NT):
                    act.wait_ge(s["qkv_done"], CREDIT + b * NT + (i + 1))
                    act.wait_ge(s["qx_ready"], CREDIT + b * NT)
                    act.wait_ge(s["kx_ready"], CREDIT + b)
                    nc.scalar.copy(QF[:, i, :], bank(3 + i % 2)[:, 0:D + 2 * HD]).then_inc(s["qf_ready"], 1)
                    first_parts(b, i, s)
            for kind, n, k in order:
                if kind == "mt":
                    act.wait_ge(smax_full, ring_at[(kind, n, k)] + 1)
                    if n >= 2:
                        act.wait_ge(mrows[n % 2], 48 * (n // 2))
                    r = ring_at[(kind, n, k)]
                    nc.scalar.copy(MT[:, n % 2, :], bank(4 + r % 2).bitcast(BF16)[0:3 * H, 0:P]).then_inc(mt_ready, 1)
                elif kind == "st":
                    q = pair_at[(n, k)]
                    act.wait_ge(st_full, q + 1)
                    if q >= 3:
                        act.wait_ge(pv_done, q - 2)
                    nc.scalar.activation(PR[:, q % 3, :, :], ps[:, 2 * (q % 2):2 * (q % 2) + 2, :], ACT.Exp,
                                         scale=SCALE).then_inc(p_ready, 1)
                elif kind == "ytr":
                    act.wait_ge(pv_done, pair_at[(n, len(pairs(items[n][1])) - 1)] + 1)
                    if n >= 2:
                        act.wait_ge(yf_turned, n - 1)
                    nc.scalar.copy(YF[:, n % 2, :], bank(6 + n % 2)).then_inc(yf_ready, 1)
                elif kind == "yt":
                    act.wait_ge(yn_transposed, n + 1)
                    if n >= 2:
                        act.wait_ge(proj_done, n - 1)
                    nc.scalar.copy(YT[:, n % 2, :, :],
                                   bank(6 + n % 2)[:, 0:D].rearrange("p (c t) -> p c t", c=C)).then_inc(yt_ready, 1)

            with act.Fori(0, B) as b:
                for i in range(NT):
                    act.wait_ge(v["xn_transposed"], CREDIT + b * NT + (i + 1))
                    act.wait_ge(v["q_done"], CREDIT + b * NT)
                    nc.scalar.copy(XT[:, :, i * P:(i + 1) * P],
                                   bank(i % 2)[:, 0:C * P].rearrange("p (c t) -> p c t", c=C)).then_inc(v["xt_ready"], 1)
                for i in range(NT):
                    act.wait_ge(v["q_done"], CREDIT + b * NT + (i + 1))
                    act.wait_ge(v["qx_ready"], CREDIT + b * NT)
                    nc.scalar.copy(QF[:, i, 0:D], bank(3 + i % 2)[:, 0:D]).then_inc(v["qf_ready"], 1)
                    first_parts(b, i, v)
            with act.Fori(0, B) as b:
                for i in range(NT):
                    act.wait_ge(v["mt_full"], CREDIT + b * NT + (i + 1))
                    act.wait_ge(vrows[i % 2], CREDIT + b * (48 * NT // 2) + 48 * (i // 2))
                    nc.scalar.copy(MT[:, i % 2, :], bank(6 + i % 2)[0:3 * H, 0:P]).then_inc(v["mt_ready"], 1)
            for i in range(N + 3):
                if i < N:
                    for q in (2 * i, 2 * i + 1):
                        act.wait_ge(v["st_full"], CREDIT + q + 1)
                        if q >= 3:
                            act.wait_ge(v["pv_done"], CREDIT + q - 2)
                        k = 4 + 2 * (q % 2)
                        nc.scalar.activation(PR[0:S, q % 3, :, :], ps[0:S, k:k + 2, :], ACT.Exp,
                                             scale=SCALE).then_inc(v["p_ready"], 1)
                if 1 <= i <= N:
                    t = i - 1
                    act.wait_ge(v["pv_done"], CREDIT + 2 * t + 2)
                    if t >= 2:
                        act.wait_ge(v["yf_turned"], CREDIT + t - 1)
                    nc.scalar.copy(YF[:, t % 2, :], bank(t % 4)).then_inc(v["yf_ready"], 1)
                if i >= 3:
                    t = i - 3
                    act.wait_ge(v["yn_transposed"], CREDIT + t + 1)
                    if t >= 2:
                        act.wait_ge(v["proj_done"], CREDIT + t - 1)
                    nc.scalar.copy(YT[:, t % 2, :, :],
                                   bank(t % 4)[:, 0:D].rearrange("p (c t) -> p c t", c=C)).then_inc(v["yt_ready"], 1)
            with act.Fori(0, B) as b:
                act.wait_ge(rt["lg_done"], CREDIT + b)
                for i in range(NT):
                    act.wait_ge(rt["xn_transposed"], CREDIT + b * NT + (i + 1))
                    nc.scalar.copy(XT[:, :, i * P:(i + 1) * P],
                                   bank(i % 2)[:, 0:C * P].rearrange("p (c t) -> p c t", c=C)).then_inc(rt["xt_ready"], 1)
                act.wait_ge(rt["lg_ready"], CREDIT + b + 1)
                nc.scalar.activation(ex[:], lg[:], ACT.Exp).then_inc(rt["ex_ready"], 1)
            with act.Fori(0, E // 2) as u:
                for a in range(2):
                    act.wait_ge(stg_loaded[a], u * 32 + 32)
                    apart(a)
                    nc.scalar.activation(W16[:, bass.ds(u * 2 + a, 1), :, 0, :].rearrange("p e m x -> p (e m) x"),
                                         STG[a].rearrange("p (m x) -> p m x", m=2), ACT.Copy,
                                         scale=UP).then_inc(w["hi_ready"], 1)

            def turn(u, c):
                act.wait_ge(e["xg_transposed"], CREDIT + u * 2 + (c + 1))
                if not isinstance(u, int) or u * 2 + c >= 2:
                    act.wait_ge(e["up_done"], CREDIT + u * 2 + (c - 1))
                nc.scalar.activation(X16[:, c % 2, 0, :, :], bank(c % 2)[:, 0:D].rearrange("p (c t) -> p c t", c=C), ACT.Copy,
                                     scale=UP).then_inc(e["xh_ready"], 1)

            def hidden(u, c):
                ex_ = act.value_load(TE[0:1, bass.ds(u * 2 + c, 1)], min_val=0, max_val=E - 1)
                act.wait_ge(e["up_done"], CREDIT + u * 2 + (c + 1))
                if not isinstance(u, int) or u * 2 + c >= 2:
                    act.wait_ge(e["hl_ready"], CREDIT + u * 2 + (c - 1))
                    act.wait_ge(e["down_done"], CREDIT + u * 2 + (c - 1))
                apart(c % 2)
                for f in range(FC):
                    ins = nc.scalar.activation(HF[:, c % 2, f * P:(f + 1) * P], bank(2 + c % 2)[:, f * P:(f + 1) * P], ACT.Gelu,
                                               bias=b1T[:, f, bass.ds(ex_, 1)], scale=1.0 / (UP * UP))
                ins.then_inc(e["act_ready"], 1)
                act.wait_ge(e["act_ready"], CREDIT + u * 2 + (c + 1))
                nc.scalar.activation(H16[:, c % 2, 0, :], HF[:, c % 2, :], ACT.Copy, scale=UP).then_inc(e["hh_ready"], 1)

            act.wait_ge(te_ready, 1)
            turn(0, 0)
            turn(0, 1)
            hidden(0, 0)
            with act.Fori(0, (NX - 3) // 2) as u:
                for c in (1, 2):
                    turn(u, c + 1)
                    hidden(u, c)
            turn(0, NX - 1)
            hidden(0, NX - 2)
            hidden(0, NX - 1)

        @block.vector
        def _(dve):
            chain = [0]

            def link(ins):
                chain[0] += 1
                ins.then_inc(dve_chain, 1)
                dve.wait_ge(dve_chain, chain[0])

            def apart():
                nc.vector.memset(scratch[:], 0.0)

            nc.vector.memset(ones_act[:], 1.0)
            nc.vector.memset(STG[0], 0.0).then_inc(zeros_ready, 1)
            dve.wait_ge(s["consts"], 1)
            dve.wait_ge(s["x_loaded"], 32)
            LINKS = 5
            with dve.Fori(0, B) as b:
                local = [0]

                def step(ins):
                    local[0] += 1
                    ins.then_inc(dve_chain, 1)
                    dve.wait_ge(dve_chain, b * LINKS + local[0])

                for i in range(NT):
                    ins = nc.vector.bn_stats(stats[:, i, :], X[:, bass.ds(b * NT + i, 1), :])
                step(ins)
                apart()
                for i in range(NT):
                    ins = nc.vector.bn_aggr(mv[:, i, :], stats[:, i, :])
                step(ins)
                nc.vector.tensor_scalar(ve[:, :], mv[:, :, 1], EPS, None, ALU.add).then_inc(s["var_ready"], 1)
                dve.wait_ge(s["rstd_ready"], CREDIT + b + 1)
                for i in range(NT):
                    dve.wait_ge(s["xn_transposed"], CREDIT + b * NT)
                    nc.vector.tensor_scalar(XN[:, i:i + 1, :], X[:, bass.ds(b * NT + i, 1), :], mv[:, i, 0:1], rstd[:, i:i + 1],
                                            ALU.subtract, ALU.mult).then_inc(s["xn_ready"], 1)
                for i in range(NT):
                    if i == NT - 2:
                        dve.wait_ge(s["qf_ready"], CREDIT + b * NT + NT)
                        dve.wait_ge(s["kx_transposed"], CREDIT + b)
                        k = QF[:, :, D:D + HD]
                        part = [KX[:, :, r * HD:(r + 1) * HD] for r in range(SPLIT)]
                        for r in (3, 5):
                            nc.vector.tensor_copy(part[r], k)
                        step(nc.vector.tensor_copy(part[0], k))
                        step(nc.vector.tensor_tensor(krest[:], k, part[0], ALU.subtract))
                        nc.vector.tensor_copy(part[4], krest[:])
                        step(nc.vector.tensor_copy(part[1], krest[:]))
                        nc.vector.tensor_copy(VX[:, bass.ds(b * NT, NT), 0:HD], QF[:, :, D + HD:D + 2 * HD])
                        nc.vector.tensor_tensor(part[2], krest[:], part[1], ALU.subtract).then_inc(s["kx_ready"], 1)
                    dve.wait_ge(s["qx_transposed"], CREDIT + b * NT + (i + 1))
                    nc.vector.tensor_copy(QT[0:KQ, bass.ds(b * NT + i, 1), :, :],
                                          ps[:, 6:8, :].bitcast(BF16)[0:KQ].rearrange("p a (h t) -> p (a h) t", t=P)
                                          ).then_inc(s["qt_ready"], 1)
                assert local[0] == LINKS
                dve.wait_ge(s["kx_transposed"], CREDIT + b + 1)
                nc.vector.tensor_copy(KT[0:KM, bass.ds(b, 1), :], bank(5).bitcast(BF16)[0:KM, :]).then_inc(s["kt_ready"], 1)
            chain[0] = B * LINKS

            for kind, n, k in order:
                b, i = items[n]
                if kind == "max":
                    h0, nh, s0, ns, c = max_tiles(i)[k]
                    r = ring_at[(kind, n, k)]
                    dve.wait_ge(smax_full, r + 1)
                    if k == 0 and n >= 2:
                        dve.wait_ge(mp_ready, n - 1)
                    two = chunks(i) == 2
                    last = k == len(max_tiles(i)) - 1
                    dst = nmx[:, n % 2, c, h0:h0 + nh] if two else nm[:, n % 2, h0:h0 + nh]
                    ins = nc.vector.tensor_reduce(dst, bank(4 + r % 2)[:, 0:nh * ns].rearrange("p (h s) -> p h s", h=nh),
                                                  AX_X, ALU.max, negate=True)
                    ins.then_inc(smax_free, 1)
                    if last and two:
                        dve.wait_ge(smax_free, maxima_to(r))
                        nc.vector.tensor_tensor(nm[:, n % 2, :], nmx[:, n % 2, 0, :], nmx[:, n % 2, 1, :],
                                                ALU.min).then_inc(nm_ready, 1)
                elif kind == "ytr":
                    y = bank(6 + n % 2).rearrange("p (a g v) -> p a g v", a=HG, g=G)
                    dve.wait_ge(yf_turned, n + 1)
                    if n >= 2:
                        dve.wait_ge(yn_transposed, n - 1)
                    ri = rinv[:, n % 2, :].rearrange("p (a g) -> p a g", a=HG)
                    link(nc.vector.reciprocal(ri, y[:, :, :, HD]))
                    nc.vector.tensor_tensor(YN[:, n % 2, :].rearrange("p (g a d) -> p a g d", g=G, a=HG), y[:, :, :, 0:HD],
                                            ri.unsqueeze(3).to_broadcast([P, HG, G, HD]), ALU.mult).then_inc(yn_ready, 1)
                elif kind == "proj":
                    t = b * NT + i
                    dve.wait_ge(proj_done, n + 1)
                    nc.vector.tensor_tensor(X[:, t, :], X[:, t, :], bank(6 + n % 2)[:, D:2 * D],
                                            ALU.add).then_inc(x1_ready, 1)

            def stepper(b, base, per):
                local = [0]

                def step(ins):
                    local[0] += 1
                    assert local[0] <= per
                    ins.then_inc(dve_chain, 1)
                    dve.wait_ge(dve_chain, b * per + (base + local[0]))
                return step

            def norm(b, step, sems, before, to):
                if True:
                    for i in range(NT):
                        ins = nc.vector.bn_stats(stats[:, i, :], X[:, bass.ds(b * NT + i, 1), :])
                    step(ins)
                    apart()
                    for i in range(NT):
                        ins = nc.vector.bn_aggr(mv[:, i, :], stats[:, i, :])
                    step(ins)
                    nc.vector.tensor_scalar(ve[:, :], mv[:, :, 1], EPS, None, ALU.add).then_inc(sems["var_ready"], 1)
                    dve.wait_ge(sems["rstd_ready"], CREDIT + b + 1)
                    dve.wait_ge(before[0], CREDIT + before[1])
                    for i in range(NT):
                        nc.vector.tensor_scalar(to(b, i), X[:, bass.ds(b * NT + i, 1), :], mv[:, i, 0:1],
                                                rstd[:, i:i + 1], ALU.subtract, ALU.mult).then_inc(sems["xn_ready"], 1)

            dve.wait_ge(x1_ready, N)
            with dve.Fori(0, B) as b:
                norm(b, stepper(b, chain[0], 2), v, (v["xn_transposed"], b * NT), lambda b, i: XN[:, i:i + 1, :])
                for i in range(NT):
                    dve.wait_ge(v["qx_transposed"], CREDIT + b * NT + (i + 1))
                    nc.vector.tensor_copy(QT[0:KQ, bass.ds(b * NT + i, 1), :, :],
                                          ps[:, 6:8, :].bitcast(BF16)[0:KQ].rearrange("p a (h t) -> p (a h) t", t=P)
                                          ).then_inc(v["qt_ready"], 1)
            chain[0] += B * 2
            with dve.Fori(0, B) as b:
                for i in range(NT):
                    dve.wait_ge(v["smax_full"], CREDIT + b * NT + (i + 1))
                    dve.wait_ge(v["mp_ready"], CREDIT + b * NT + max(i - 1, 0))
                    nc.vector.tensor_reduce(nm[:, i % 2, 0:12].rearrange("p (a h) -> p a h", a=2),
                                            ps[:, 3 * (i % 2):3 * (i % 2) + 2, 0:6 * S].rearrange("p a (h s) -> p a h s", s=S),
                                            AX_X, ALU.max, negate=True)
                    nc.vector.tensor_reduce(nm[:, i % 2, 12:16], bank(3 * (i % 2) + 2)[:, 0:4 * S].rearrange("p (h s) -> p h s", s=S),
                                            AX_X, ALU.max, negate=True).then_inc(v["smax_free"], 1)
            for i in range(N + 4):
                if i < N:
                    nc.vector.tensor_tensor(X[:, i, :], X[:, i, :], bout[:], ALU.add)
                if 2 <= i <= N + 1:
                    t = i - 2
                    y = bank(t % 4).rearrange("p (a g v) -> p a g v", a=HG, g=G)
                    dve.wait_ge(v["yf_turned"], CREDIT + t + 1)
                    if t >= 2:
                        dve.wait_ge(v["yn_transposed"], CREDIT + t - 1)
                    ri = rinv[:, t % 2, :].rearrange("p (a g) -> p a g", a=HG)
                    link(nc.vector.reciprocal(ri, y[:, :, :, HD]))
                    nc.vector.tensor_tensor(YN[:, t % 2, :].rearrange("p (a g d) -> p a g d", g=G, a=HG), y[:, :, :, 0:HD],
                                            ri.unsqueeze(3).to_broadcast([P, HG, G, HD]), ALU.mult).then_inc(v["yn_ready"], 1)
                if i >= 4:
                    t = i - 4
                    dve.wait_ge(v["proj_done"], CREDIT + t + 1)
                    nc.vector.tensor_tensor(X[:, t, :], X[:, t, :], bank(t % 4)[:, D:2 * D],
                                            ALU.add).then_inc(v["x2_ready"], 1)
            dve.wait_ge(v["x2_ready"], CREDIT + N)
            with dve.Fori(0, B) as b:
                step = stepper(b, chain[0], 12)
                norm(b, step, rt, (rt["xn_transposed"], b * NT), lambda b, i: XN3[:, bass.ds(b * NT + i, 1), :])
                dve.wait_ge(rt["lg_done"], CREDIT + b + 1)
                l3 = bank(2)[:, 0:NT * E].rearrange("p (n e) -> p n e", e=E)

                def wide(a):
                    return a.unsqueeze(2).to_broadcast([P, NT, E])

                step(nc.vector.tensor_reduce(lmax[:], l3, AX_X, ALU.max))
                nc.vector.tensor_tensor(lg[:], l3, wide(lmax[:]), ALU.subtract).then_inc(rt["lg_ready"], 1)
                dve.wait_ge(rt["ex_ready"], CREDIT + b + 1)
                step(nc.vector.tensor_reduce(lsum[:], ex[:], AX_X, ALU.add))
                step(nc.vector.reciprocal(lmax[:], lsum[:]))
                step(nc.vector.tensor_tensor(pr[:], ex[:], wide(lmax[:]), ALU.mult))
                apart()
                for i in range(NT):
                    ins = nc.vector.max(top[:, i, :], pr[:, i, :])
                step(ins)
                apart()
                for i in range(NT):
                    ins = nc.vector.max_index(tix[:, i, :], top[:, i, :], pr[:, i, :])
                step(ins)
                nc.vector.tensor_copy(rank[:], tix[:, :, 0:2])
                step(nc.vector.tensor_tensor(wsum[:], top[:, :, 0], top[:, :, 1], ALU.add))
                step(nc.vector.tensor_scalar(wsum[:], wsum[:], 1e-10, None, ALU.max))
                step(nc.vector.reciprocal(lsum[:], wsum[:]))
                tiles_b = bass.ds(b * NT, NT)
                nc.vector.tensor_tensor(wts[:, tiles_b, :], top[:, :, 0:2], lsum[:].unsqueeze(2).to_broadcast([P, NT, 2]),
                                        ALU.mult)
                for k in range(2):
                    ins = nc.vector.tensor_tensor(hot[:, k, tiles_b, :], iotaf[:, 0:E].unsqueeze(1).to_broadcast([P, NT, E]),
                                                  wide(rank[:, :, k]), ALU.is_equal)
                step(ins)
                nc.vector.tensor_tensor(hotb[:, tiles_b, :], hot[:, 0, tiles_b, :], hot[:, 1, tiles_b, :],
                                        ALU.add).then_inc(rt["hot_ready"], 1)
            chain[0] += B * 12
            dve.wait_ge(ranked, 1)
            link(nc.vector.tensor_copy(cnt[:], bank(4)[:, 0:E]))
            link(nc.vector.scalar_tensor_tensor(out=levels, in0=iotaf[:, 0:LEVELS].unsqueeze(1).to_broadcast([P, E, LEVELS]),
                                                scalar=float(P), in1=cnt[:].unsqueeze(2).to_broadcast([P, E, LEVELS]),
                                                op0=ALU.mult, op1=ALU.is_lt))
            link(nc.vector.tensor_reduce(tiles[:], levels, AX_X, ALU.add))
            link(nc.vector.tensor_tensor(earlier[:], earlier[:], tiles[:].unsqueeze(1).to_broadcast([P, E, E]), ALU.mult))
            link(nc.vector.tensor_reduce(first[:], earlier[:], AX_X, ALU.add))
            nc.vector.tensor_tensor(upto[:], first[:], tiles[:], ALU.add)
            link(nc.vector.scalar_tensor_tensor(out=place_of, in0=first[:].unsqueeze(1).to_broadcast([P, N, E]),
                                                scalar=float(P), in1=bank(3)[:, 0:N * E].rearrange("p (n e) -> p n e", e=E),
                                                op0=ALU.mult, op1=ALU.add))
            for k in range(2):
                ins = nc.vector.tensor_tensor(hot[:, k], hot[:, k], place_of, ALU.mult)
            link(ins)
            link(nc.vector.tensor_reduce(slotf[:], hot[:], AX_X, ALU.add))
            nc.vector.tensor_copy(slot[:], slotf[:]).then_inc(slot_ready, 1)
            link(nc.vector.tensor_tensor(tilesum, iotaf[0:1, :].unsqueeze(2).to_broadcast([1, NX, E]),
                                         upto[0:1, :].unsqueeze(1).to_broadcast([1, NX, E]), ALU.is_ge))
            link(nc.vector.tensor_reduce(tef[:], tilesum, AX_X, ALU.add))
            nc.vector.tensor_scalar(TE[:], tef[:], float(E - 1), None, ALU.min).then_inc(te_ready, 1)
            with dve.Fori(0, E // 2) as u:
                for a in range(2):
                    dve.wait_ge(w["hi_ready"], CREDIT + u * 2 + (a + 1))
                    expert = bass.ds(u * 2 + a, 1)
                    nc.vector.scalar_tensor_tensor(out=W16[:, expert, :, 1, :].rearrange("p e m x -> p (e m) x"),
                                                   in0=STG[a].rearrange("p (m x) -> p m x", m=2), scalar=UP,
                                                   in1=W16[:, expert, :, 0, :].rearrange("p e m x -> p (e m) x"),
                                                   op0=ALU.mult, op1=ALU.subtract).then_inc(w["lo_ready"], 1)

            def turn(u, c):
                dve.wait_ge(e["xh_ready"], CREDIT + u * 2 + (c + 1))
                nc.vector.scalar_tensor_tensor(out=X16[:, c % 2, 1, :, :], in0=bank(c % 2)[:, 0:D].rearrange("p (c t) -> p c t", c=C),
                                               scalar=UP, in1=X16[:, c % 2, 0, :, :], op0=ALU.mult,
                                               op1=ALU.subtract).then_inc(e["xl_ready"], 1)

            def hidden(u, c):
                dve.wait_ge(e["hh_ready"], CREDIT + u * 2 + (c + 1))
                nc.vector.scalar_tensor_tensor(out=H16[:, c % 2, 1, :], in0=HF[:, c % 2, :], scalar=UP, in1=H16[:, c % 2, 0, :],
                                               op0=ALU.mult, op1=ALU.subtract).then_inc(e["hl_ready"], 1)

            def give(u, c):
                ex_ = dve.value_load(TE[0:1, bass.ds(u * 2 + c, 1)], min_val=0, max_val=E - 1)
                dve.wait_ge(e["down_done"], CREDIT + u * 2 + (c + 1))
                if not isinstance(u, int) or u * 2 + c >= 2:
                    dve.wait_ge(ys_stored[c % 2], CREDIT + u * 16 + 16 * (c // 2))
                nc.vector.scalar_tensor_tensor(out=YS[:, c % 2:c % 2 + 1, :], in0=bank(4 + c % 2)[:, 0:D].unsqueeze(1),
                                               scalar=1.0 / (UP * UP), in1=b2all[:, bass.ds(ex_, 1), :],
                                               op0=ALU.mult, op1=ALU.add).then_inc(e["y_ready"], 1)

            dve.wait_ge(te_ready, 1)
            dve.wait_ge(b2_loaded, 16)
            turn(0, 0)
            turn(0, 1)
            hidden(0, 0)
            with dve.Fori(0, (NX - 3) // 2) as u:
                for c in (1, 2):
                    turn(u, c + 1)
                    hidden(u, c)
                    give(u, c - 1)
            turn(0, NX - 1)
            hidden(0, NX - 2)
            give(0, NX - 3)
            hidden(0, NX - 1)
            give(0, NX - 2)
            give(0, NX - 1)

            for g in range(4):
                dve.wait_ge(returned[g], 16 * 2 * (N // 4))
                group = slice(g * (N // 4), (g + 1) * (N // 4))
                for k, into in ((0, XN3), (1, FINAL)):
                    for n in range(N)[group]:
                        ins = nc.vector.scalar_tensor_tensor(out=FINAL[:, n, :], in0=RET[:, k, n, :], scalar=wts[:, n, k:k + 1],
                                                             in1=into[:, n, :], op0=ALU.mult, op1=ALU.add)
                    link(ins)
                link(nc.vector.tensor_scalar(FINAL[:, group, :], FINAL[:, group, :], 100.0, -100.0, ALU.min, ALU.max))
                nc.vector.tensor_tensor(FINAL[:, group, :], FINAL[:, group, :], X[:, group, :], ALU.add).then_inc(fin_ready, 1)

        @block.tensor
        def _(pe):
            mm, tr = nc.tensor.matmul, nc.tensor.transpose
            pe.wait_ge(s["consts"], 1)
            pe.wait_ge(s["ctx_loaded"], 32)
            pe.wait_ge(s_small, 96)
            for b in range(B):
                for c in range(C):
                    tr(bank(0)[:, (b * C + c) * S:(b * C + c + 1) * S], CX[:, b, c * P:(c + 1) * P], ident[0:S, 0:S])
            for c in range(C):
                ins = tr(bank(1)[:, c * E:(c + 1) * E], gaterow[:, c * P:(c + 1) * P], ident[0:E, 0:E])
            for c in range(FC):
                ins = tr(bank(1)[:, (C + c) * E:(C + c + 1) * E], b1row[:, c * P:(c + 1) * P], ident[0:E, 0:E])
            ins.then_inc(s["cx_transposed"], 1)
            pe.wait_ge(s["ct_ready"], CREDIT + 3)
            for b in range(B):
                mm(bank(2 + b)[0:S, :], ones1[0:1, 0:S], bqkv[0:1, D:3 * D], start=True, stop=False)
                for c in range(C):
                    ins = mm(bank(2 + b)[0:S, :], CT[:, b, c, :], wqkv[:, c, D:3 * D], start=False, stop=c == C - 1)
                ins.then_inc(s["kv2_done"], 1)
            for b in range(B):
                pe.wait_ge(s["kx2_ready"], CREDIT + b + 1)
                for h in range(H):
                    ins = tr(bank(4 + 2 * b + h // 8).bitcast(BF16)[0:KM, (h % 8) * SP:(h % 8) * SP + S],
                             KX2[:, b, h, 0:KM], identb[0:S, 0:S])
                ins.then_inc(s["kx2_transposed"], 1)
            pe.wait_ge(s["w_loaded"], 64)
            pe.wait_ge(s["kt2_ready"], CREDIT + B)
            with pe.Fori(0, B) as b:
                for i in range(NT):
                    pe.wait_ge(s["xn_ready"], CREDIT + b * NT + (i + 1))
                    pe.wait_ge(s["xt_ready"], CREDIT + b * NT + max(i - 1, 0))
                    for c in range(C):
                        ins = tr(bank(i % 2)[:, c * P:(c + 1) * P], XN[:, i, c * P:(c + 1) * P], ident[:])
                    ins.then_inc(s["xn_transposed"], 1)
                    if i % 4 == 3:
                        g = i // 4
                        pe.wait_ge(s["xt_ready"], CREDIT + b * NT + (i + 1))
                        pe.wait_ge(s["lat_ready"], CREDIT + b * 2 + g)
                        for c in range(C):
                            ins = mm(bank(2), wdown[:, c, :], XT[:, c, g * 512:(g + 1) * 512], start=c == 0, stop=c == C - 1)
                        ins.then_inc(s["lat_done"], 1)
                for i in range(NT + 1):
                    if i < NT:
                        pe.wait_ge(s["lat_ready"], CREDIT + b * 2 + (i // 4 + 1))
                        pe.wait_ge(s["qh_ready"], CREDIT + b * NT + max(i - 1, 0))
                        mm(bank(3 + i % 2)[:, 0:D + 2 * HD], LT[:, i * P:(i + 1) * P], wqkvup[:], start=True,
                           stop=True).then_inc(s["qkv_done"], 1)
                    if i >= 1:
                        t = i - 1
                        pe.wait_ge(s["qx_ready"], CREDIT + b * NT + (t + 1))
                        pe.wait_ge(s["qt_ready"], CREDIT + b * NT + t)
                        for h in range(H):
                            ins = tr(bank(6 + h // 8).bitcast(BF16)[0:KQ, (h % 8) * P:(h % 8 + 1) * P],
                                     QX[:, t % 2, h, :, :].rearrange("p r d -> p (r d)"), identb[:])
                        ins.then_inc(s["qx_transposed"], 1)
                pe.wait_ge(s["kx_ready"], CREDIT + b + 1)
                pe.wait_ge(s["kt_ready"], CREDIT + b)
                for i in range(NT):
                    ins = tr(bank(5).bitcast(BF16)[0:KM, i * P:(i + 1) * P], KX[:, i, 0:KM], identb[:])
                ins.then_inc(s["kx_transposed"], 1)
            pe.wait_ge(s["qt_ready"], CREDIT + N)
            pe.wait_ge(s["kt_ready"], CREDIT + B)
            pe.wait_ge(s["qh_ready"], CREDIT + N)

            for kind, n, k in order:
                b, i = items[n]
                t = b * NT + i
                r = ring_at.get((kind, n, k))
                if r is not None and r >= 2:
                    prev = ring[r - 2]
                    if prev[0] == "max":
                        pe.wait_ge(smax_free, maxima_to(r - 2))
                    else:
                        pe.wait_ge(mt_ready, prev[1] + 1)
                if kind == "max":
                    h0, nh, s0, ns, c = max_tiles(i)[k]
                    diag = s0 + ns == (i + 1) * P
                    for a in range(nh):
                        ins = mm(bank(4 + r % 2)[:, a * ns:(a + 1) * ns], QT[0:KQ, t, h0 + a, :], KT[0:KQ, b, s0:s0 + ns],
                                 start=a == 0, stop=not diag and a == nh - 1, skip_group_check=True)
                        if diag:
                            ins = mm(bank(4 + r % 2)[:, (a + 1) * ns - P:(a + 1) * ns], identb[:], mask_ts[:],
                                     start=False, stop=a == nh - 1, skip_group_check=True)
                    ins.then_inc(smax_full, 1)
                elif kind == "mt":
                    pe.wait_ge(mp_ready, n + 1)
                    tr(bank(4 + r % 2).bitcast(BF16)[0:3 * H, 0:P], MP[:, n % 2, :, :].rearrange("p k h -> p (k h)"),
                       identb[:]).then_inc(smax_full, 1)
                elif kind == "st":
                    q = pair_at[(n, k)]
                    if k == 0:
                        pe.wait_ge(mrows[n % 2], 48 * (n // 2 + 1))
                    if q >= 2:
                        pe.wait_ge(p_ready, q - 1)
                    for u, (g, j) in enumerate(pairs(i)[k]):
                        o = bank(2 * (q % 2) + u)
                        ins = mm(o, KT[0:KM, b, j * P:(j + 1) * P], QT[0:KM, t, g * HG:(g + 1) * HG, :],
                                 start=True, stop=j < i)
                        if j == i:
                            ins = mm(o, identb[:], mask_st[:].unsqueeze(1).to_broadcast([P, HG, P]), start=False, stop=True)
                    ins.then_inc(st_full, 1)
                elif kind == "pv":
                    q = pair_at[(n, k)]
                    pe.wait_ge(p_ready, q + 1)
                    if k == 0 and n >= 2:
                        pe.wait_ge(x1_ready, n - 1)
                    for u, (g, j) in enumerate(pairs(i)[k]):
                        ins = mm(bank(6 + n % 2)[32 * g:32 * g + 32, :], VX[:, b * NT + j, :], PR[:, q % 3, u, :],
                                 start=j == 0, stop=j == i)
                    ins.then_inc(pv_done, 1)
                elif kind == "ytr":
                    pe.wait_ge(yf_ready, n + 1)
                    for a in range(HG):
                        ins = tr(bank(6 + n % 2)[:, a * P:(a + 1) * P], YF[:, n % 2, a * P:(a + 1) * P], ident[:])
                    ins.then_inc(yf_turned, 1)
                elif kind == "yt":
                    pe.wait_ge(yn_ready, n + 1)
                    for c in range(C):
                        ins = tr(bank(6 + n % 2)[:, c * P:(c + 1) * P], YN[:, n % 2, c * P:(c + 1) * P], ident[:])
                    ins.then_inc(yn_transposed, 1)
                elif kind == "proj":
                    pe.wait_ge(yt_ready, n + 1)
                    for c in range(C):
                        ins = mm(bank(6 + n % 2)[:, D:2 * D], YT[:, n % 2, c, :], wproj[:, c, :], start=c == 0, stop=c == C - 1)
                    ins.then_inc(proj_done, 1)
            pe.wait_ge(x1_ready, N)
            pe.wait_ge(p_ready, len(pair_at))
            with pe.Fori(0, B) as b:
                for i in range(NT):
                    pe.wait_ge(v["xn_ready"], CREDIT + b * NT + (i + 1))
                    pe.wait_ge(v["xt_ready"], CREDIT + b * NT + max(i - 1, 0))
                    for c in range(C):
                        ins = tr(bank(i % 2)[:, c * P:(c + 1) * P], XN[:, i, c * P:(c + 1) * P], ident[:])
                    ins.then_inc(v["xn_transposed"], 1)
                for i in range(NT + 1):
                    if i < NT:
                        pe.wait_ge(v["xt_ready"], CREDIT + b * NT + (i + 1))
                        pe.wait_ge(v["qh_ready"], CREDIT + b * NT + max(i - 1, 0))
                        mm(bank(3 + i % 2)[:, 0:D], ones1[0:1, :], bqkv[0:1, 0:D], start=True, stop=False)
                        for c in range(C):
                            ins = mm(bank(3 + i % 2)[:, 0:D], XT[:, c, i * P:(i + 1) * P], wqkv[:, c, 0:D], start=False,
                                     stop=c == C - 1)
                        ins.then_inc(v["q_done"], 1)
                    if i >= 1:
                        t = i - 1
                        pe.wait_ge(v["qx_ready"], CREDIT + b * NT + (t + 1))
                        pe.wait_ge(v["qt_ready"], CREDIT + b * NT + t)
                        for h in range(H):
                            ins = tr(bank(6 + h // 8).bitcast(BF16)[0:KQ, (h % 8) * P:(h % 8 + 1) * P],
                                     QX[:, t % 2, h, :, :].rearrange("p r d -> p (r d)"), identb[:])
                        ins.then_inc(v["qx_transposed"], 1)
            pe.wait_ge(v["xt_ready"], CREDIT + N)
            pe.wait_ge(v["qh_ready"], CREDIT + N)
            with pe.Fori(0, B) as b:
                for i in range(NT + 1):
                    if i < NT:
                        pe.wait_ge(v["qt_ready"], CREDIT + b * NT + (i + 1))
                        pe.wait_ge(v["smax_free"], CREDIT + b * NT + max(i - 1, 0))
                        for h in range(H):
                            ins = mm(bank(3 * (i % 2) + h // 6)[:, (h % 6) * S:(h % 6 + 1) * S],
                                     QT[0:KQ, bass.ds(b * NT + i, 1), h, :].rearrange("p n t -> p (n t)"),
                                     KT2[0:KQ, bass.ds(b, 1), h, 0:S].rearrange("p n t -> p (n t)"), start=h % 6 == 0,
                                     stop=h % 6 == 5 or h == H - 1, skip_group_check=True)
                        ins.then_inc(v["smax_full"], 1)
                    if i >= 1:
                        t = i - 1
                        pe.wait_ge(v["mp_ready"], CREDIT + b * NT + (t + 1))
                        pe.wait_ge(v["mt_ready"], CREDIT + b * NT + max(t - 1, 0))
                        mm(bank(6 + t % 2)[0:3 * H, 0:P], MP[:, t % 2, :, :].rearrange("p k h -> p (k h)"),
                           identb[:], start=True, stop=True).then_inc(v["mt_full"], 1)
            pe.wait_ge(v["mt_ready"], CREDIT + N)
            pe.wait_ge(v["smax_free"], CREDIT + N)
            for i in range(N + 4):
                if i < N:
                    b = i // NT
                    pe.wait_ge(vrows[i % 2], CREDIT + 48 * (i // 2 + 1))
                    for q in (2 * i, 2 * i + 1):
                        if q >= 2:
                            pe.wait_ge(v["p_ready"], CREDIT + q - 1)
                        for a in range(8):
                            h = (q % 2) * 8 + a
                            ins = mm(bank(4 + 2 * (q % 2) + a // 4)[0:S, (a % 4) * P:(a % 4 + 1) * P], KT2[0:KM, b, h, 0:S],
                                     QT[0:KM, i, h, :], start=a % 4 == 0, stop=a % 4 == 3, skip_group_check=True)
                        ins.then_inc(v["st_full"], 1)
                if 1 <= i <= N:
                    t = i - 1
                    b = t // NT
                    if t >= 4:
                        pe.wait_ge(v["x2_ready"], CREDIT + t - 3)
                    for q in (2 * t, 2 * t + 1):
                        pe.wait_ge(v["p_ready"], CREDIT + q + 1)
                        for a in range(8):
                            h = (q % 2) * 8 + a
                            g, k = h % 4, h // 4
                            ins = mm(bank(t % 4)[32 * g:32 * g + 32, k * P:(k + 1) * P], V2X[:, b, h, :],
                                     PR[0:S, q % 3, a // 4, (a % 4) * P:(a % 4 + 1) * P], start=k == 0, stop=k == 3,
                                     skip_group_check=True)
                        ins.then_inc(v["pv_done"], 1)
                if 2 <= i <= N + 1:
                    t = i - 2
                    pe.wait_ge(v["yf_ready"], CREDIT + t + 1)
                    for a in range(HG):
                        ins = tr(bank(t % 4)[:, a * P:(a + 1) * P], YF[:, t % 2, a * P:(a + 1) * P], ident[:])
                    ins.then_inc(v["yf_turned"], 1)
                if 3 <= i <= N + 2:
                    t = i - 3
                    pe.wait_ge(v["yn_ready"], CREDIT + t + 1)
                    for c in range(C):
                        ins = tr(bank(t % 4)[:, c * P:(c + 1) * P], YN[:, t % 2, c * P:(c + 1) * P], ident[:])
                    ins.then_inc(v["yn_transposed"], 1)
                if i >= 4:
                    t = i - 4
                    pe.wait_ge(v["yt_ready"], CREDIT + t + 1)
                    for c in range(C):
                        ins = mm(bank(t % 4)[:, D:2 * D], YT[:, t % 2, c, :], wout[:, c, :], start=c == 0, stop=c == C - 1)
                    ins.then_inc(v["proj_done"], 1)
            pe.wait_ge(v["x2_ready"], CREDIT + N)
            for b in range(B):
                for i in range(NT):
                    pe.wait_ge(rt["xn_ready"], CREDIT + b * NT + (i + 1))
                    pe.wait_ge(rt["xt_ready"], CREDIT + b * NT + max(i - 1, 0))
                    for c in range(C):
                        ins = tr(bank(i % 2)[:, c * P:(c + 1) * P],
                                 XN3[:, b * NT + i, c * P:(c + 1) * P], ident[:])
                    ins.then_inc(rt["xn_transposed"], 1)
                for i in range(NT):
                    pe.wait_ge(rt["xt_ready"], CREDIT + b * NT + (i + 1))
                    for c in range(C):
                        ins = mm(bank(2)[:, i * E:(i + 1) * E], XT[:, c, i * P:(i + 1) * P], gateT[:, c, :],
                                 start=i == 0 and c == 0, stop=c == C - 1, skip_group_check=True)
                ins.then_inc(rt["lg_done"], 1)
            pe.wait_ge(rt["hot_ready"], CREDIT + B)
            for n in range(N - 1):
                mm(bank(3)[:, (n + 1) * E:N * E].rearrange("p (n e) -> p n e", e=E), onesb[:],
                   hotb[:, n:n + 1, :].to_broadcast([P, N - 1 - n, E]), start=n == 0, stop=False, skip_group_check=True)
            mm(bank(3)[:, 0:N * E], before[:], hotb[:].rearrange("p n e -> p (n e)"), start=False, stop=True,
               skip_group_check=True)
            for n in range(N):
                ins = mm(bank(4)[:, 0:E], onesb[:], hotb[:, n, :], start=n == 0, stop=n == N - 1)
            ins.then_inc(ranked, 1)

            def turn(u, c):
                pe.wait_ge(xg_loaded[c % 2], u * 16 + 16 * (c // 2 + 1))
                if not isinstance(u, int) or u * 2 + c >= 2:
                    pe.wait_ge(e["xl_ready"], CREDIT + u * 2 + (c - 1))
                for k in range(C):
                    ins = tr(bank(c % 2)[:, k * P:(k + 1) * P], XG[:, c % 2, k * P:(k + 1) * P], ident[:])
                ins.then_inc(e["xg_transposed"], 1)

            PARTS = ((0, 0), (0, 1), (1, 0))

            def expert(u, c):
                return pe.value_load(TE[0:1, bass.ds(u * 2 + c, 1)], min_val=0, max_val=E - 1)

            def hidden(u, c, ex_):
                pe.wait_ge(e["xl_ready"], CREDIT + u * 2 + (c + 1))
                if not isinstance(u, int) or u * 2 + c >= 2:
                    pe.wait_ge(e["act_ready"], CREDIT + u * 2 + (c - 1))
                for f in range(FC):
                    for q, (a, b) in enumerate(PARTS):
                        for k in range(C):
                            ins = mm(bank(2 + c % 2)[:, f * P:(f + 1) * P],
                                     W16[:, bass.ds(ex_, 1), 0, a, k * F + f * P:k * F + (f + 1) * P].rearrange("p e x -> p (e x)"),
                                     X16[:, c % 2, b, k, :], start=f == 0 and q == 0 and k == 0,
                                     stop=q == 2 and k == C - 1, skip_group_check=True)
                ins.then_inc(e["up_done"], 1)

            def give(u, c, ex_):
                pe.wait_ge(e["hl_ready"], CREDIT + u * 2 + (c + 1))
                if not isinstance(u, int) or u * 2 + c >= 2:
                    pe.wait_ge(e["y_ready"], CREDIT + u * 2 + (c - 1))
                for f in range(FC):
                    for q, (a, b) in enumerate(PARTS):
                        ins = mm(bank(4 + c % 2)[:, 0:D], H16[:, c % 2, a, f * P:(f + 1) * P],
                                 W16[:, bass.ds(ex_, 1), 1, b, f * D:(f + 1) * D].rearrange("p e x -> p (e x)"),
                                 start=f == 0 and q == 0, stop=f == FC - 1 and q == 2)
                ins.then_inc(e["down_done"], 1)

            pe.wait_ge(te_ready, 1)
            pe.wait_ge(w["lo_ready"], CREDIT + E)
            turn(0, 0)
            turn(0, 1)
            hidden(0, 0, expert(0, 0))
            with pe.Fori(0, (NX - 3) // 2) as u:
                of = [expert(u, c) for c in range(3)]
                for c in (1, 2):
                    turn(u, c + 1)
                    hidden(u, c, of[c])
                    give(u, c - 1, of[c - 1])
            turn(0, NX - 1)
            of = [expert(0, NX - 3 + c) for c in range(3)]
            hidden(0, NX - 2, of[1])
            give(0, NX - 3, of[0])
            hidden(0, NX - 1, of[2])
            give(0, NX - 2, of[1])
            give(0, NX - 1, of[2])


_INS = ['x', 'ctx_1024', 'L0_attn_Wc_down', 'L0_attn_Wq_up', 'L0_attn_Wkv_up', 'L0_attn_Wc_proj', 'L0_xattn_W_qkv',
        'L0_xattn_b_qkv', 'L0_xattn_W_out', 'L0_xattn_b_out', 'L0_ffn_gate_w', 'L0_ffn_w1', 'L0_ffn_b1', 'L0_ffn_w2',
        'L0_ffn_b2']
_OUTS = [((2, 1024, 256), 'float32')]


def kernel(**inputs):
    import numpy as _np
    import concourse.bacc as _bacc
    from concourse import mybir as _mybir
    from concourse.bass_utils import run_bass_kernel_spmd as _run

    nc = _bacc.Bacc("TRN2", target_bir_lowering=False, num_devices=1)
    arrays, args = {}, []
    for name in _INS:
        a = _np.ascontiguousarray(inputs[name])
        arrays[f"in_{name}_dram"] = a
        args.append(nc.dram_tensor(f"in_{name}_dram", a.shape, _mybir.dt.from_np(a.dtype), kind="ExternalInput").ap())
    for i, (shape, dtype) in enumerate(_OUTS):
        dt = _mybir.dt.from_np(_np.dtype(dtype))
        args.append(nc.dram_tensor(f"out_{i}_dram", shape, dt, kind="ExternalOutput").ap())
    decoder_layer(nc, *args)
    r = _run(nc, [arrays], core_ids=[0])
    got = tuple(r.results[0][f"out_{i}_dram"] for i in range(len(_OUTS)))
    return got[0]
```

```python
from contextlib import ExitStack

import concourse.bass as bass
from concourse import mybir

ALU = mybir.AluOpType
ACT = mybir.ActivationFunctionType
BF16 = mybir.dt.bfloat16
F16 = mybir.dt.float16
U32 = mybir.dt.uint32
I32 = mybir.dt.int32
F32 = mybir.dt.float32
AX_X = mybir.AxisListType.X

P = 128
EPS = 1e-5
CREDIT = 1
BIG = -1.0e30
UP = 64.0
SPLIT = 6


def decoder_layer(nc, x, ctx_in, w_down, w_qup, w_kvup, w_proj, w_qkv, b_qkv, w_out, b_out,
                  gate_w, w1, b1, w2, b2, out):
    B, T, D = x.shape
    S = ctx_in.shape[1]
    E, _, F = w1.shape
    HD = w_kvup.shape[1] // 2
    H = D // HD
    LAT = w_down.shape[1]
    C = D // P
    FC = F // P
    NT = T // P
    N = B * NT
    KQ = SPLIT * HD
    KM = KQ + 3
    HV = HD + 1
    HG = 4
    G = H // HG
    SCALE = float(HD) ** -0.5
    SP = 80
    NX = (2 * T * B + E * (P - 1)) // P
    NX += (3 - NX) % 6
    LEVELS = T * B // P
    WPE = C * F
    assert LAT == P and WPE == FC * D and KQ <= 96 and HG * P == 512 and S <= SP

    HIGH_AT = (0, 1, 2, 3, 11, 12, 14, 15)
    MIDDLE = len(HIGH_AT) // 2
    EARLY = 8
    assert T * B <= 2048

    with ExitStack() as stack:
        def sb(name, shape, dt=F32):
            return stack.enter_context(nc.sbuf_tensor(name, shape, dt))

        def sem(name):
            return stack.enter_context(nc.semaphore(name))

        ps = stack.enter_context(nc.psum_tensor("ps", [P, 8, 512], F32))

        def bank(k):
            return ps[:, k, :]

        X = sb("X", [P, N, D])
        WORDS = E * 2 * WPE
        BIGBUF = sb("BIGBUF", [P, WORDS])
        taken = [0]

        def place(shape, dt=F32, src=None):
            count = 1
            for k in shape:
                count *= k
            words = count // 2 if dt == BF16 else count
            flat = BIGBUF[:] if src is None else src[:].rearrange("p n d -> p (n d)")
            piece = flat[:, taken[0]:taken[0] + words]
            taken[0] += words
            assert taken[0] <= flat.shape[1]
            if dt == BF16:
                piece = piece.bitcast(BF16)
            axes = "abcde"[:len(shape)]
            if len(shape) == 1:
                return piece
            return piece.rearrange("p (%s) -> p %s" % (" ".join(axes), " ".join(axes)), **dict(zip(axes, shape)))

        QT = place([N, H, P], BF16)
        QF = place([NT, D + 2 * HD])
        QX = place([2, H, SPLIT, HD], BF16)
        qrest = place([H, HD])
        KX = place([NT, KQ + 16], BF16)
        KX2 = place([B, H, KQ + 16], BF16)[0:S]
        KV2 = place([B, 2 * D])[0:S]
        KT = place([B, T], BF16)
        LT = place([T])
        wdown = place([C, LAT])
        wqkvup = place([D + 2 * HD])
        wproj = place([C, D])
        wqkv = place([C, 3 * D])
        W16 = BIGBUF[:].bitcast(F16).rearrange("p (e m h x) -> p e m h x", e=E, m=2, h=2)
        XN = sb("XN", [P, NT, D])
        XT = sb("XT", [P, C, T])
        ARENA = sb("ARENA", [P, E * D])
        PR = ARENA[:, 0:3 * 2 * 512].rearrange("p (a u t) -> p a u t", a=3, u=2)
        YN = ARENA[:, 3 * 2 * 512:3 * 2 * 512 + 2 * D].rearrange("p (a d) -> p a d", a=2)
        b2all = ARENA[:].rearrange("p (e d) -> p e d", e=E)
        STG = [sb("STG", [P, 2 * WPE])[:], XN[:].rearrange("p n d -> p (n d)")]
        XN3 = sb("XN3", [P, N, D])
        taken[0] = 0
        CX = place([B, D], src=XN3)[0:S]
        CT = place([B, C, S], src=XN3)
        krest2 = place([H, HD], src=XN3)[0:S]
        krest = place([NT, HD], src=XN3)
        gaterow = place([D], src=XN3)[0:E]
        b1row = place([F], src=XN3)[0:E]
        VX = place([N, 32], src=XN3)
        V2X = place([B, H, 32], src=XN3)[0:S]
        bqkv = sb("bqkv", [1, 3 * D])
        wout = sb("wout", [P, C, D])
        bout = sb("bout", [P, D])
        gateT = sb("gateT", [P, C, E])
        b1T = sb("b1T", [P, FC, E])
        ident = sb("ident", [P, P])
        identb = sb("identb", [P, P], BF16)
        mask_ts = sb("mask_ts", [P, P], BF16)
        mask_st = sb("mask_st", [P, P], BF16)
        before = sb("before", [P, P], BF16)
        onesb = sb("onesb", [P, P], BF16)
        ones1 = sb("ones1", [1, P])
        halfneg = sb("halfneg", [P, N])
        stats = sb("stats", [P, NT, 6])
        mv = sb("mv", [P, NT, 2])
        ve = sb("ve", [P, NT])
        rstd = sb("rstd", [P, NT])
        KTBUF = sb("KTBUF", [P, 1, B * H * SP // 2])
        taken[0] = 0
        KT2 = place([B, H, SP], BF16, src=KTBUF)
        nmx = sb("nmx", [P, 2, 2, H])
        nm = sb("nm", [P, 2, H])
        mrest = sb("mrest", [P, H])
        MP = sb("MP", [P, 2, 3, H], BF16)
        MT = sb("MT", [3 * H, 2, P], BF16)
        rinv = sb("rinv", [P, 2, H])
        YF = XT[:, 0, :].rearrange("p (a t) -> p a t", a=2)
        YT = sb("YT", [P, 2, C, P])
        scratch = sb("scratch", [P, 1])
        scratch_act = sb("scratch_act", [P, 2])
        ones_act = sb("ones_act", [P, 1])
        zerosH = sb("zerosH", [P, H])
        stats3 = sb("stats3", [P, N, 6])
        mv3 = sb("mv3", [P, N, 2])
        ve3 = sb("ve3", [P, N])
        rstd3 = sb("rstd3", [P, N])
        lmax = sb("lmax", [P, N])
        lsum = sb("lsum", [P, N])
        tix = sb("tix", [P, N, 8], U32)
        wsum = sb("wsum", [P, N])
        taken[0] = 0
        lg = place([N, E], src=KTBUF)
        ex = place([N, E], src=KTBUF)
        pr = place([N, E], src=KTBUF)
        top = place([N, 8], src=KTBUF)
        rank = place([N, 2], src=KTBUF)
        wts = sb("wts", [P, N, 2])
        hot = sb("hot", [P, 2, N, E])
        hotb = sb("hotb", [P, N, E], BF16)
        iotai = sb("iotai", [P, P], I32)
        iotaf = sb("iotaf", [P, P])
        tokeni = sb("tokeni", [P, N], I32)
        token = sb("token", [P, N])
        cnt = sb("cnt", [P, E])
        tiles = sb("tiles", [P, E])
        earlier = sb("earlier", [P, E, E])
        first = sb("first", [P, E])
        upto = sb("upto", [P, E])
        slotf = sb("slotf", [P, 2, N])
        slot = sb("slot", [P, 2, N], U32)
        taken[0] = 0
        place_of = place([N, E], src=XT)
        levels = place([E, LEVELS], src=XT)
        taken[0] = N * E
        tilesum = place([NX, E], src=XT)[0:1]
        slotq = sb("slotq", [P, 2, N], U32)
        slotqf = sb("slotqf", [P, 2, N])
        slotr = sb("slotr", [P, 2, N])
        index = sb("index", [P, NX], U32)
        inv = ARENA[:].bitcast(F16)
        is_row = inv[:, 0:2 * N * P].rearrange("p (m r) -> p m r", r=P)
        is_tile = inv[:, 2 * N * P:2 * N * (P + NX)].rearrange("p (m j) -> p m j", j=NX)
        token_at = inv[:, 2 * N * (P + NX):2 * N * (P + 2 * NX)].rearrange("p (m j) -> p m j", j=NX)
        tef = sb("tef", [1, NX])
        TE = sb("TE", [1, NX], I32)
        teh = sb("teh", [1, NX])
        TE4 = sb("TE4", [1, NX], I32)
        XG = XN[:, 0:2, :]
        X16 = XN[:, 2:4, :].rearrange("p a d -> p (a d)").bitcast(F16).rearrange("p (a h c t) -> p a h c t", a=2, h=2, c=C)
        YS = XN[:, 4:6, :]
        HF = XT[:, 0, :].rearrange("p (a f) -> p a f", a=2)
        H16 = XT[:, 1, :].bitcast(F16).rearrange("p (a h f) -> p a h f", a=2, h=2)
        RET = BIGBUF[:, 0:2 * N * D].rearrange("p (k n d) -> p k n d", k=2, n=N)
        FINAL = BIGBUF[:, 2 * N * D:3 * N * D].rearrange("p (n d) -> p n d", n=N)
        XD = nc.dram_tensor("by_token", (N * P, D), F32, kind="Internal").ap()
        YD = nc.dram_tensor("sorted_out", (NX * P, D), F32, kind="Internal").ap()

        names = """w_loaded ctx_loaded consts var_ready rstd_ready xn_ready xn_transposed
            xt_ready lat_done lat_ready qkv_done qf_ready qh_ready qm_ready qx_ready qx_transposed qt_ready kx_ready kx_transposed kt_ready
            cx_transposed ct_ready kv2_done kv2_ready kx2_ready kx2_transposed kt2_ready""".split()
        s = {k: sem(k) for k in names}
        x_loaded = [sem("x0_loaded"), sem("x1_loaded")]
        dve_chain, pool_chain = sem("dve_chain"), sem("pool_chain")
        smax_full, smax_free = sem("smax_full"), sem("smax_free")
        mt_ready = sem("mt_ready")
        nm_ready, mp_ready = sem("nm_ready"), sem("mp_ready")
        mrows = [sem("mrows_even"), sem("mrows_odd")]
        st_full, p_ready, pv_done = sem("st_full"), sem("p_ready"), sem("pv_done")
        yn_ready, yn_transposed, yt_ready = sem("yn_ready"), sem("yn_transposed"), sem("yt_ready")
        yf_ready, yf_turned = sem("yf_ready"), sem("yf_turned")
        proj_done, x1_ready = sem("proj_done"), sem("x1_ready")
        stored = sem("stored")
        s_small = sem("small_loaded")
        v = {k: sem("x_" + k) for k in """var_ready rstd_ready xn_ready xn_transposed xt_ready q_done qf_ready qh_ready qm_ready qx_ready
            qx_transposed qt_ready smax_full smax_free mp_ready mt_full mt_ready st_full p_ready pv_done yf_ready yf_turned
            yn_ready yn_transposed yt_ready proj_done x2_ready""".split()}
        vrows = [sem("x_mrows_even"), sem("x_mrows_odd")]
        rt = {k: sem("r_" + k) for k in """var_ready rstd_ready xn_ready xn_transposed xt_ready lg_done lg_ready ex_ready
            hot_ready""".split()}
        GROUPS = N
        b2_loaded, x3_stored = sem("b2_loaded"), sem("x3_stored")
        ranked, slot_ready, te_ready = sem("ranked"), sem("slot_ready"), sem("te_ready")
        inverse_ready, inverted, index_ready = sem("inverse_ready"), sem("inverted"), sem("index_ready")
        stg_loaded = [sem("stg_loaded_even"), sem("stg_loaded_odd")]
        w = {k: sem("w_" + k) for k in "hi_ready lo_ready".split()}
        xg_loaded = [sem("xg_loaded_even"), sem("xg_loaded_odd")]
        e = {k: sem("e_" + k) for k in """xg_transposed xh_ready xl_ready up_done act_ready hh_ready hl_ready down_done
            y_ready""".split()}
        ys_stored = [sem("ys_stored_even"), sem("ys_stored_odd")]
        returned = [sem("returned_%d" % g) for g in range(GROUPS)]
        fin_ready = sem("fin_ready")

        credited = [q for group in (s, v, rt, w, e) for name, q in group.items() if "loaded" not in name and name != "consts"]
        credited += vrows + ys_stored

        items = [divmod(k, NT) for k in (0, 1, 3, 5, 7, 15, 6, 14, 13, 4, 12, 11, 2, 10, 9, 8)]
        assert sorted(items) == [(b, i) for b in range(B) for i in range(NT)]
        LEAD = 2

        def max_tiles(i):
            keys = (i + 1) * P
            head = min(keys, 512)
            hb = 512 // head
            tiles = [(h, hb, 0, head, 0) for h in range(0, H, hb)]
            if keys > 512:
                hb = 512 // (keys - 512)
                tiles += [(h, hb, 512, keys - 512, 1) for h in range(0, H, hb)]
            return tiles

        def pairs(i):
            units = [(g, j) for j in range(i + 1) for g in range(G)]
            return [units[k:k + 2] for k in range(0, len(units), 2)]

        def schedule():
            order = []
            for n in range(min(LEAD, N)):
                order += [("max", n, k) for k in range(len(max_tiles(items[n][1])))] + [("mt", n, 0)]
            flat = [(n, p) for n in range(N) for p in range(len(pairs(items[n][1])))]
            order += [("st",) + flat[0]]
            for q, (n, p) in enumerate(flat):
                np_ = len(pairs(items[n][1]))
                maxima = []
                if n + LEAD < N:
                    m = [("max", n + LEAD, k) for k in range(len(max_tiles(items[n + LEAD][1])))]
                    maxima = m[len(m) * p // np_:len(m) * (p + 1) // np_]
                if n > 0 and p == 0:
                    order += [("yf", n - 1, 0)]
                order += maxima[:1]
                if q + 1 < len(flat) and flat[q + 1][0] == n:
                    order += [("st",) + flat[q + 1]]
                order += maxima[1:]
                if q + 1 < len(flat) and flat[q + 1][0] != n:
                    order += [("st",) + flat[q + 1]]
                order += [("pv", n, p)]
                if n > 0 and p == 0 and n - 1 + LEAD < N:
                    order += [("mt", n - 1 + LEAD, 0)]
                if n > 0:
                    after = [("ytr", n - 1, 0), ("yt", n - 1, 0), ("proj", n - 1, 0)]
                    if p > 0:
                        order += after[p - 1:p]
                    if p == np_ - 1:
                        order += after[p:]
            return order + [("yf", N - 1, 0), ("ytr", N - 1, 0), ("yt", N - 1, 0), ("proj", N - 1, 0)]

        order = schedule()
        ring = [o for o in order if o[0] in ("max", "mt")]
        ring_at = {o: k for k, o in enumerate(ring)}

        def maxima_to(r):
            return sum(o[0] == "max" for o in ring[:r + 1])

        def chunks(i):
            return 2 if (i + 1) * P > 512 else 1

        pair_at = {}
        for n in range(N):
            for p in range(len(pairs(items[n][1]))):
                pair_at[(n, p)] = len(pair_at)

        block = stack.enter_context(nc.Block())

        @block.sync
        def _(sp):
            sp.dma_start(X[:, 0:NT, :], x[0].rearrange("(n p) d -> p n d", p=P)).then_inc(x_loaded[0], 16)
            sp.dma_start(X[:, NT:N, :], x[1].rearrange("(n p) d -> p n d", p=P)).then_inc(x_loaded[1], 16)
            for q in credited:
                sp.sem_inc(q, CREDIT)
            for b in range(B):
                sp.dma_start(CX[:, b, :], ctx_in[b]).then_inc(s["ctx_loaded"], 16)
            for n in range(N):
                sp.wait_ge(mt_ready, n + 1)
                b, i = items[n]
                for k in range(3):
                    sp.dma_start(QT[KQ + k:KQ + k + 1, b * NT + i, :, :],
                                 MT[k * H:(k + 1) * H, n % 2, :]).then_inc(mrows[n % 2], 16)
            sp.wait_ge(v["xn_transposed"], CREDIT + N)
            for a in range(2):
                sp.dma_start(STG[a][:, 0:WPE].rearrange("p (c f) -> p c f", c=C),
                             w1[EARLY + a].rearrange("(c p) f -> p c f", p=P)).then_inc(stg_loaded[a], 16)
                sp.dma_start(STG[a][:, WPE:2 * WPE].rearrange("p (c f) -> p c f", c=FC),
                             w2[EARLY + a].rearrange("(c p) f -> p c f", p=P)).then_inc(stg_loaded[a], 16)
            with sp.Fori(0, B) as b:
                for i in range(NT):
                    sp.wait_ge(v["mt_ready"], CREDIT + b * NT + (i + 1))
                    for k in range(3):
                        sp.dma_start(QT[KQ + k:KQ + k + 1, bass.ds(b * NT + i, 1), :, :].rearrange("p n h t -> p (n h) t"),
                                     MT[k * H:(k + 1) * H, i % 2, :]).then_inc(vrows[i % 2], 16)
            for first_expert, done, turns in ((EARLY + 2, 2, (E - EARLY - 2) // 2), (0, E - EARLY, EARLY // 2)):
                with sp.Fori(0, turns) as u:
                    for a in range(2):
                        sp.wait_ge(w["hi_ready"], CREDIT + u * 2 + max(done + a - 1, 0))
                        sp.wait_ge(w["lo_ready"], CREDIT + u * 2 + max(done + a - 1, 0))
                        expert = bass.ds(u * 2 + (first_expert + a), 1)
                        sp.dma_start(STG[a][:, 0:WPE].rearrange("p (c f) -> p c f", c=C),
                                     w1[expert].rearrange("e (c p) f -> p (e c) f", p=P)).then_inc(stg_loaded[a], 16)
                        sp.dma_start(STG[a][:, WPE:2 * WPE].rearrange("p (c f) -> p c f", c=FC),
                                     w2[expert].rearrange("e (c p) f -> p (e c) f", p=P)).then_inc(stg_loaded[a], 16)
            sp.wait_ge(inverted, 1)
            sp.dma_start(b2all[:], b2.rearrange("e d -> (e d)").partition_broadcast(P).rearrange("p (e d) -> p e d", e=E)
                         ).then_inc(b2_loaded, 16)

            def store(u, c):
                sp.wait_ge(e["y_ready"], CREDIT + u * 2 + (c + 1))
                sp.dma_start(YD[bass.ds((u * 2 + c) * P, P)], YS[:, c % 2, :]).then_inc(ys_stored[c % 2], 16)

            with sp.Fori(0, (NX - 1) // 2) as u:
                for c in range(2):
                    store(u, c)
            store(0, NX - 1)
            for g in range(GROUPS):
                sp.wait_ge(fin_ready, g + 1)
                sp.dma_start(out.rearrange("b (n p) d -> p (b n) d", p=P)[:, g * (N // GROUPS):(g + 1) * (N // GROUPS), :],
                             FINAL[:, g * (N // GROUPS):(g + 1) * (N // GROUPS), :]).then_inc(stored, 16)
            sp.wait_ge(stored, 16 * GROUPS)

        @block.gpsimd
        def _(pool):
            chain = [0]

            def link(ins):
                chain[0] += 1
                ins.then_inc(pool_chain, 1)
                pool.wait_ge(pool_chain, chain[0])

            def stepper(b, base, per):
                local = [0]

                def step(ins):
                    local[0] += 1
                    assert local[0] <= per
                    ins.then_inc(pool_chain, 1)
                    pool.wait_ge(pool_chain, b * per + (base + local[0]))
                return step

            link(nc.gpsimd.memset(ident[:], 0.0))
            link(nc.gpsimd.affine_select(out=ident[:], in_=ident[:], compare_op=ALU.not_equal, fill=1.0, base=0,
                                         pattern=[[-1, P]], channel_multiplier=1))
            link(nc.gpsimd.tensor_copy(identb[:], ident[:]))
            link(nc.gpsimd.memset(mask_ts[:], 0.0))
            link(nc.gpsimd.affine_select(out=mask_ts[:], in_=mask_ts[:], compare_op=ALU.is_ge, fill=BIG, base=0,
                                         pattern=[[-1, P]], channel_multiplier=1))
            link(nc.gpsimd.memset(mask_st[:], 0.0))
            link(nc.gpsimd.affine_select(out=mask_st[:], in_=mask_st[:], compare_op=ALU.is_ge, fill=BIG, base=0,
                                         pattern=[[1, P]], channel_multiplier=-1))
            link(nc.gpsimd.memset(ones1[:], 1.0))
            link(nc.gpsimd.memset(halfneg[:], -0.5))
            link(nc.gpsimd.memset(KX[:], 1.0))
            link(nc.gpsimd.memset(KX2[:], 1.0))
            link(nc.gpsimd.memset(VX, 0.0))
            link(nc.gpsimd.memset(VX[:, :, HD:HV], 1.0))
            link(nc.gpsimd.memset(V2X, 0.0))
            link(nc.gpsimd.memset(V2X[:, :, :, HD:HV], 1.0))
            link(nc.gpsimd.memset(zerosH[:], 0.0))
            link(nc.gpsimd.iota(iotai[:], [[1, P]], base=0, channel_multiplier=0))
            link(nc.gpsimd.iota(tokeni[:], [[P, N]], base=0, channel_multiplier=1))
            link(nc.gpsimd.tensor_copy(token[:], tokeni[:]))
            link(nc.gpsimd.memset(onesb[:], 1.0))
            link(nc.gpsimd.memset(before[:], 1.0))
            link(nc.gpsimd.affine_select(out=before[:], in_=before[:], compare_op=ALU.is_gt, fill=0.0, base=0,
                                         pattern=[[1, P]], channel_multiplier=-1))
            link(nc.gpsimd.memset(earlier[:], 1.0))
            link(nc.gpsimd.affine_select(out=earlier[:], in_=earlier[:], compare_op=ALU.is_gt, fill=0.0, base=0,
                                         pattern=[[1, E], [-1, E]], channel_multiplier=0))
            nc.gpsimd.tensor_copy(iotaf[:], iotai[:]).then_inc(s["consts"], 1)
            base = chain[0]
            with pool.Fori(0, B) as b:
                pool.wait_ge(s["var_ready"], CREDIT + b + 1)
                nc.gpsimd.tensor_tensor(rstd[:, :], ve[:, :], halfneg[:, 0:NT], ALU.pow).then_inc(s["rstd_ready"], 1)
                step = stepper(b, base, NT)
                for i in range(NT):
                    q = QF[:, i, 0:D].rearrange("p (h d) -> p h d", h=H)
                    xq = QX[:, i % 2]
                    pool.wait_ge(s["qf_ready"], CREDIT + b * NT + (i + 1))
                    pool.wait_ge(s["qx_ready"], CREDIT + b * NT + i)
                    pool.wait_ge(s["qh_ready"], CREDIT + b * NT + (i + 1))
                    step(nc.gpsimd.tensor_tensor(qrest[:], q, xq[:, :, 0, :], ALU.subtract))
                    pool.wait_ge(s["qm_ready"], CREDIT + b * NT + (i + 1))
                    nc.gpsimd.tensor_tensor(xq[:, :, 5, :], qrest[:], xq[:, :, 3, :],
                                            ALU.subtract).then_inc(s["qx_ready"], 1)
            chain[0] += B * NT
            def context_parts(b):
                pool.wait_ge(s["kv2_ready"], CREDIT + b + 1)
                k = KV2[:, b, 0:D].rearrange("p (h d) -> p h d", h=H)
                part = [KX2[:, b, :, q * HD:(q + 1) * HD] for q in range(SPLIT)]
                for q in (3, 5):
                    nc.gpsimd.tensor_copy(part[q], k)
                link(nc.gpsimd.tensor_copy(part[0], k))
                link(nc.gpsimd.tensor_tensor(krest2[:], k, part[0], ALU.subtract))
                nc.gpsimd.tensor_copy(part[4], krest2[:])
                link(nc.gpsimd.tensor_copy(part[1], krest2[:]))
                nc.gpsimd.tensor_copy(V2X[:, b, :, 0:HD], KV2[:, b, D:2 * D].rearrange("p (h d) -> p h d", h=H))
                nc.gpsimd.tensor_tensor(part[2], krest2[:], part[1], ALU.subtract).then_inc(s["kx2_ready"], 1)

            for n in range(N):
                if chunks(items[n][1]) == 1:
                    pool.wait_ge(smax_free, maxima_to(ring_at[("max", n, len(max_tiles(items[n][1])) - 1)]))
                else:
                    pool.wait_ge(nm_ready, sum(chunks(i) == 2 for _, i in items[:n + 1]))
                if n >= 2:
                    pool.wait_ge(mt_ready, n - 1)
                m = nm[:, n % 2, :]
                link(nc.gpsimd.tensor_copy(MP[:, n % 2, 0, :], m))
                link(nc.gpsimd.tensor_tensor(mrest[:], m, MP[:, n % 2, 0, :], ALU.subtract))
                link(nc.gpsimd.tensor_copy(MP[:, n % 2, 1, :], mrest[:]))
                nc.gpsimd.tensor_tensor(MP[:, n % 2, 2, :], mrest[:], MP[:, n % 2, 1, :],
                                        ALU.subtract).then_inc(mp_ready, 1)
                if n in (4, 6):
                    context_parts((n - 4) // 2)

            def deviations(b, sems):
                row = slice(b * NT, (b + 1) * NT)
                pool.wait_ge(sems["var_ready"], CREDIT + b + 1)
                nc.gpsimd.tensor_tensor(rstd3[:, row], ve3[:, row], halfneg[:, 0:NT], ALU.pow).then_inc(sems["rstd_ready"], 1)

            for b in range(B):
                deviations(b, v)
            with pool.Fori(0, B) as b:
                step = stepper(b, chain[0], NT)
                for i in range(NT):
                    q = QF[:, i, 0:D].rearrange("p (h d) -> p h d", h=H)
                    xq = QX[:, i % 2]
                    pool.wait_ge(v["qf_ready"], CREDIT + b * NT + (i + 1))
                    pool.wait_ge(v["qx_ready"], CREDIT + b * NT + i)
                    pool.wait_ge(v["qh_ready"], CREDIT + b * NT + (i + 1))
                    step(nc.gpsimd.tensor_tensor(qrest[:], q, xq[:, :, 0, :], ALU.subtract))
                    pool.wait_ge(v["qm_ready"], CREDIT + b * NT + (i + 1))
                    nc.gpsimd.tensor_tensor(xq[:, :, 5, :], qrest[:], xq[:, :, 3, :],
                                            ALU.subtract).then_inc(v["qx_ready"], 1)
            chain[0] += B * NT
            with pool.Fori(0, B) as b:
                step = stepper(b, chain[0], 2 * NT)
                for i in range(NT):
                    pool.wait_ge(v["smax_free"], CREDIT + b * NT + (i + 1))
                    pool.wait_ge(v["mt_ready"], CREDIT + b * NT + max(i - 1, 0))
                    m = nm[:, i % 2, :]
                    pool.wait_ge(v["mp_ready"], CREDIT + b * NT + i)
                    step(nc.gpsimd.tensor_tensor(MP[:, i % 2, 0, :], m, zerosH[:], ALU.add))
                    nc.gpsimd.tensor_tensor(mrest[:], m, MP[:, i % 2, 0, :], ALU.subtract)
                    step(nc.gpsimd.tensor_tensor(MP[:, i % 2, 1, :], m, MP[:, i % 2, 0, :], ALU.subtract))
                    nc.gpsimd.tensor_tensor(MP[:, i % 2, 2, :], mrest[:], MP[:, i % 2, 1, :],
                                            ALU.subtract).then_inc(v["mp_ready"], 1)
            chain[0] += B * 2 * NT
            pool.wait_ge(v["qt_ready"], CREDIT + N)
            for k in range(E - EARLY):
                pool.wait_ge(stg_loaded[k % 2], 32 * (k // 2 + 1))
                nc.gpsimd.tensor_scalar(W16[:, EARLY + k, :, 0, :], STG[k % 2].rearrange("p (m x) -> p m x", m=2), UP, None,
                                        ALU.mult).then_inc(w["hi_ready"], 1)
            for b in range(B):
                deviations(b, rt)
            pool.wait_ge(index_ready, 1)
            pool.wait_ge(x3_stored, 16 * 4)
            pool.wait_ge(w["lo_ready"], CREDIT + E)
            for j in range(NX):
                if j >= 2:
                    pool.wait_ge(e["xg_transposed"], CREDIT + j - 1)
                nc.gpsimd.indirect_dma_start(XG[:, j % 2, :], None, XD,
                                             bass.IndirectOffsetOnAxis(index[:, j:j + 1], 0)).then_inc(xg_loaded[j % 2], 16)
            for a in range(2):
                pool.wait_ge(ys_stored[a], CREDIT + 16 * ((NX + 1 - a) // 2))
            for n in range(N):
                for k in range(2):
                    nc.gpsimd.indirect_dma_start(RET[:, k, n, :], None, YD,
                                                 bass.IndirectOffsetOnAxis(slot[:, k, n:n + 1], 0)
                                                 ).then_inc(returned[n // (N // GROUPS)], 16)

        @block.scalar
        def _(act):
            def apart(a):
                nc.scalar.copy(scratch_act[:, a:a + 1], ones_act[:])

            def first_parts(b, i, sems):
                act.wait_ge(sems["qx_transposed"], CREDIT + b * NT + max(i - 1, 0))
                nc.scalar.copy(QX[:, i % 2, :, 0:3, :],
                               bank(3 + i % 2)[:, 0:D].rearrange("p (h d) -> p h d", h=H).unsqueeze(2)
                               .to_broadcast([P, H, 3, HD])).then_inc(sems["qh_ready"], 1)

            act.dma_start(wdown[:], w_down.rearrange("(c p) n -> p c n", p=P)).then_inc(s["w_loaded"], 16)
            act.dma_start(wqkvup[:, 0:D], w_qup).then_inc(s["w_loaded"], 16)
            act.dma_start(wqkvup[:, D:D + 2 * HD], w_kvup).then_inc(s["w_loaded"], 16)
            act.dma_start(wproj[:], w_proj.rearrange("(c p) n -> p c n", p=P)).then_inc(s["w_loaded"], 16)
            act.dma_start(wqkv[:], w_qkv.rearrange("(c p) n -> p c n", p=P)).then_inc(s_small, 16)
            act.dma_start(bqkv[:], b_qkv.rearrange("(a n) -> a n", a=1)).then_inc(s_small, 16)
            act.dma_start(wout[:], w_out.rearrange("(c p) n -> p c n", p=P)).then_inc(s_small, 16)
            act.dma_start(bout[:], b_out.partition_broadcast(P)).then_inc(s_small, 16)
            act.dma_start(gaterow[:], gate_w).then_inc(s_small, 16)
            act.dma_start(b1row[:], b1).then_inc(s_small, 16)
            act.wait_ge(s["cx_transposed"], CREDIT + 1)
            nc.scalar.copy(CT[:], bank(0)[:, 0:B * C * S].rearrange("p (b c s) -> p b c s", b=B, c=C)).then_inc(s["ct_ready"], 1)
            nc.scalar.copy(gateT[:], bank(1)[:, 0:C * E].rearrange("p (c e) -> p c e", c=C)).then_inc(s["ct_ready"], 1)
            nc.scalar.copy(b1T[:], bank(1)[:, C * E:(C + FC) * E].rearrange("p (c e) -> p c e", c=FC)).then_inc(s["ct_ready"], 1)
            with act.Fori(0, B) as b:
                for i in range(NT):
                    act.wait_ge(s["xn_transposed"], CREDIT + b * NT + (i + 1))
                    act.wait_ge(s["lat_done"], CREDIT + b * 2)
                    nc.scalar.copy(XT[:, :, i * P:(i + 1) * P],
                                   bank(i % 2)[:, 0:C * P].rearrange("p (c t) -> p c t", c=C)).then_inc(s["xt_ready"], 1)
                    if i % 4 == 3:
                        g = i // 4
                        act.wait_ge(s["lat_done"], CREDIT + b * 2 + (g + 1))
                        act.wait_ge(s["qkv_done"], CREDIT + b * NT)
                        nc.scalar.copy(LT[:, g * 512:(g + 1) * 512], bank(2)).then_inc(s["lat_ready"], 1)
                for i in range(NT):
                    act.wait_ge(s["qkv_done"], CREDIT + b * NT + (i + 1))
                    act.wait_ge(s["qx_ready"], CREDIT + b * NT)
                    act.wait_ge(s["kx_ready"], CREDIT + b)
                    nc.scalar.copy(QF[:, i, :], bank(3 + i % 2)[:, 0:D + 2 * HD]).then_inc(s["qf_ready"], 1)
                    first_parts(b, i, s)
            for b in range(B):
                act.wait_ge(s["kv2_done"], CREDIT + b + 1)
                nc.scalar.copy(KV2[:, b, :], bank(b)[0:S, :]).then_inc(s["kv2_ready"], 1)
            for kind, n, k in order:
                if kind == "mt":
                    act.wait_ge(smax_full, ring_at[(kind, n, k)] + 1)
                    if n >= 2:
                        act.wait_ge(mrows[n % 2], 48 * (n // 2))
                    r = ring_at[(kind, n, k)]
                    nc.scalar.copy(MT[:, n % 2, :], bank(4 + r % 2).bitcast(BF16)[0:3 * H, 0:P]).then_inc(mt_ready, 1)
                elif kind == "st":
                    q = pair_at[(n, k)]
                    act.wait_ge(st_full, q + 1)
                    if q >= 3:
                        act.wait_ge(pv_done, q - 2)
                    nc.scalar.activation(PR[:, q % 3, :, :], ps[:, 2 * (q % 2):2 * (q % 2) + 2, :], ACT.Exp,
                                         scale=SCALE).then_inc(p_ready, 1)
                elif kind == "yf":
                    act.wait_ge(pv_done, pair_at[(n, len(pairs(items[n][1])) - 1)] + 1)
                    if n >= 2:
                        act.wait_ge(yf_turned, n - 1)
                    nc.scalar.copy(YF[:, n % 2, :], bank(6 + n % 2)).then_inc(yf_ready, 1)
                elif kind == "yt":
                    act.wait_ge(yn_transposed, n + 1)
                    if n >= 2:
                        act.wait_ge(proj_done, n - 1)
                    nc.scalar.copy(YT[:, n % 2, :, :],
                                   bank(6 + n % 2)[:, 0:D].rearrange("p (c t) -> p c t", c=C)).then_inc(yt_ready, 1)

            for b in range(B):
                act.wait_ge(s["kx2_transposed"], CREDIT + b + 1)
                nc.scalar.copy(KT2[0:KM, b, :, 0:S].rearrange("p (a h) s -> p a h s", a=2),
                               ps[:, 4 + 2 * b:6 + 2 * b, :].bitcast(BF16)[0:KM, :, 0:8 * SP].rearrange("p a (h s) -> p a h s", s=SP)[:, :, :, 0:S]
                               ).then_inc(s["kt2_ready"], 1)
            with act.Fori(0, B) as b:
                for i in range(NT):
                    act.wait_ge(v["xn_transposed"], CREDIT + b * NT + (i + 1))
                    act.wait_ge(v["q_done"], CREDIT + b * NT)
                    nc.scalar.copy(XT[:, :, i * P:(i + 1) * P],
                                   bank(i % 2)[:, 0:C * P].rearrange("p (c t) -> p c t", c=C)).then_inc(v["xt_ready"], 1)
                for i in range(NT):
                    act.wait_ge(v["q_done"], CREDIT + b * NT + (i + 1))
                    act.wait_ge(v["qx_ready"], CREDIT + b * NT)
                    nc.scalar.copy(QF[:, i, 0:D], bank(3 + i % 2)[:, 0:D]).then_inc(v["qf_ready"], 1)
                    first_parts(b, i, v)
            with act.Fori(0, B) as b:
                for i in range(NT):
                    act.wait_ge(v["mt_full"], CREDIT + b * NT + (i + 1))
                    act.wait_ge(vrows[i % 2], CREDIT + b * (48 * NT // 2) + 48 * (i // 2))
                    nc.scalar.copy(MT[:, i % 2, :], bank(6 + i % 2)[0:3 * H, 0:P]).then_inc(v["mt_ready"], 1)
            for i in range(N + 3):
                if i < N:
                    for q in (2 * i, 2 * i + 1):
                        act.wait_ge(v["st_full"], CREDIT + q + 1)
                        if q >= 3:
                            act.wait_ge(v["pv_done"], CREDIT + q - 2)
                        k = 4 + 2 * (q % 2)
                        nc.scalar.activation(PR[0:S, q % 3, :, :], ps[0:S, k:k + 2, :], ACT.Exp,
                                             scale=SCALE).then_inc(v["p_ready"], 1)
                if 1 <= i <= N:
                    t = i - 1
                    act.wait_ge(v["pv_done"], CREDIT + 2 * t + 2)
                    if t >= 2:
                        act.wait_ge(v["yf_turned"], CREDIT + t - 1)
                    nc.scalar.copy(YF[:, t % 2, :], bank(t % 4)).then_inc(v["yf_ready"], 1)
                if i >= 3:
                    t = i - 3
                    act.wait_ge(v["yn_transposed"], CREDIT + t + 1)
                    if t >= 2:
                        act.wait_ge(v["proj_done"], CREDIT + t - 1)
                    nc.scalar.copy(YT[:, t % 2, :, :],
                                   bank(t % 4)[:, 0:D].rearrange("p (c t) -> p c t", c=C)).then_inc(v["yt_ready"], 1)
            for t in range(N):
                act.wait_ge(rt["xn_transposed"], CREDIT + t + 1)
                if t >= NT:
                    act.wait_ge(rt["lg_done"], CREDIT + t - NT + 1)
                nc.scalar.copy(XT[:, :, (t % NT) * P:(t % NT + 1) * P],
                               bank(4 + t % 4)[:, 0:C * P].rearrange("p (c t) -> p c t", c=C)).then_inc(rt["xt_ready"], 1)
                if t % 4 == 3:
                    act.wait_ge(rt["xn_ready"], CREDIT + t + 1)
                    act.dma_start(XD[(t - 3) * P:(t + 1) * P].rearrange("(n p) d -> p n d", p=P),
                                  XN3[:, t - 3:t + 1, :]).then_inc(x3_stored, 16)
                if t in HIGH_AT:
                    k, m = divmod(HIGH_AT.index(t), 2)
                    act.wait_ge(stg_loaded[k % 2], 32 * ((E - EARLY + k) // 2 + 1))
                    ins = nc.scalar.activation(W16[:, k, m, 0, :], STG[k % 2].rearrange("p (m x) -> p m x", m=2)[:, m, :],
                                               ACT.Copy, scale=UP)
                    if m == 1:
                        ins.then_inc(w["hi_ready"], 1)
            act.wait_ge(rt["lg_ready"], CREDIT + 1)
            nc.scalar.activation(ex[:], lg[:], ACT.Exp).then_inc(rt["ex_ready"], 1)
            with act.Fori(0, (EARLY - MIDDLE) // 2) as u:
                for a in range(2):
                    act.wait_ge(stg_loaded[a], u * 32 + 32 * ((E - EARLY + MIDDLE) // 2 + 1))
                    apart(a)
                    nc.scalar.activation(W16[:, bass.ds(u * 2 + (MIDDLE + a), 1), :, 0, :].rearrange("p e m x -> p (e m) x"),
                                         STG[a].rearrange("p (m x) -> p m x", m=2), ACT.Copy,
                                         scale=UP).then_inc(w["hi_ready"], 1)

            def turn(u, c):
                act.wait_ge(e["xg_transposed"], CREDIT + u * 2 + (c + 1))
                if not isinstance(u, int) or u * 2 + c >= 2:
                    act.wait_ge(e["up_done"], CREDIT + u * 2 + (c - 1))
                nc.scalar.activation(X16[:, c % 2, 0, :, :], bank(c % 2)[:, 0:D].rearrange("p (c t) -> p c t", c=C), ACT.Copy,
                                     scale=UP).then_inc(e["xh_ready"], 1)

            def hidden(u, c):
                ex_ = act.value_load(TE[0:1, bass.ds(u * 2 + c, 1)], min_val=0, max_val=E - 1)
                act.wait_ge(e["up_done"], CREDIT + u * 2 + (c + 1))
                if not isinstance(u, int) or u * 2 + c >= 2:
                    act.wait_ge(e["hl_ready"], CREDIT + u * 2 + (c - 1))
                    act.wait_ge(e["down_done"], CREDIT + u * 2 + (c - 1))
                apart(c % 2)
                for f in range(FC):
                    ins = nc.scalar.activation(HF[:, c % 2, f * P:(f + 1) * P], bank(2 + c % 2)[:, f * P:(f + 1) * P], ACT.Gelu,
                                               bias=b1T[:, f, bass.ds(ex_, 1)], scale=1.0 / (UP * UP))
                ins.then_inc(e["act_ready"], 1)
                act.wait_ge(e["act_ready"], CREDIT + u * 2 + (c + 1))
                nc.scalar.activation(H16[:, c % 2, 0, :], HF[:, c % 2, :], ACT.Copy, scale=UP).then_inc(e["hh_ready"], 1)

            act.wait_ge(te_ready, 1)
            turn(0, 0)
            turn(0, 1)
            hidden(0, 0)
            with act.Fori(0, (NX - 3) // 2) as u:
                for c in (1, 2):
                    turn(u, c + 1)
                    hidden(u, c)
            turn(0, NX - 1)
            hidden(0, NX - 2)
            hidden(0, NX - 1)

        @block.vector
        def _(dve):
            chain = [0]

            def link(ins):
                chain[0] += 1
                ins.then_inc(dve_chain, 1)
                dve.wait_ge(dve_chain, chain[0])

            def apart():
                nc.vector.memset(scratch[:], 0.0)

            nc.vector.memset(ones_act[:], 1.0)
            def middle_parts(b, i, sems):
                dve.wait_ge(sems["qh_ready"], CREDIT + b * NT + (i + 1))
                nc.vector.tensor_tensor(QX[:, i % 2, :, 3:5, :],
                                        QF[:, i, 0:D].rearrange("p (h d) -> p h d", h=H).unsqueeze(2).to_broadcast([P, H, 2, HD]),
                                        QX[:, i % 2, :, 0:2, :], ALU.subtract).then_inc(sems["qm_ready"], 1)

            dve.wait_ge(s["consts"], 1)
            dve.wait_ge(x_loaded[0], 16)
            LINKS = 5
            with dve.Fori(0, B) as b:
                local = [0]

                def step(ins):
                    local[0] += 1
                    ins.then_inc(dve_chain, 1)
                    dve.wait_ge(dve_chain, b * LINKS + local[0])

                for i in range(NT):
                    ins = nc.vector.bn_stats(stats[:, i, :], X[:, bass.ds(b * NT + i, 1), :])
                step(ins)
                apart()
                for i in range(NT):
                    ins = nc.vector.bn_aggr(mv[:, i, :], stats[:, i, :])
                step(ins)
                nc.vector.tensor_scalar(ve[:, :], mv[:, :, 1], EPS, None, ALU.add).then_inc(s["var_ready"], 1)
                dve.wait_ge(s["rstd_ready"], CREDIT + b + 1)
                for i in range(NT):
                    dve.wait_ge(s["xn_transposed"], CREDIT + b * NT)
                    nc.vector.tensor_scalar(XN[:, i:i + 1, :], X[:, bass.ds(b * NT + i, 1), :], mv[:, i, 0:1], rstd[:, i:i + 1],
                                            ALU.subtract, ALU.mult).then_inc(s["xn_ready"], 1)
                middle_parts(b, 0, s)
                for i in range(NT):
                    if i + 1 < NT:
                        middle_parts(b, i + 1, s)
                    if i == NT - 2:
                        dve.wait_ge(s["qf_ready"], CREDIT + b * NT + NT)
                        dve.wait_ge(s["kx_transposed"], CREDIT + b)
                        k = QF[:, :, D:D + HD]
                        part = [KX[:, :, r * HD:(r + 1) * HD] for r in range(SPLIT)]
                        for r in (3, 5):
                            nc.vector.tensor_copy(part[r], k)
                        step(nc.vector.tensor_copy(part[0], k))
                        step(nc.vector.tensor_tensor(krest[:], k, part[0], ALU.subtract))
                        nc.vector.tensor_copy(part[4], krest[:])
                        step(nc.vector.tensor_copy(part[1], krest[:]))
                        nc.vector.tensor_copy(VX[:, bass.ds(b * NT, NT), 0:HD], QF[:, :, D + HD:D + 2 * HD])
                        nc.vector.tensor_tensor(part[2], krest[:], part[1], ALU.subtract).then_inc(s["kx_ready"], 1)
                    dve.wait_ge(s["qx_transposed"], CREDIT + b * NT + (i + 1))
                    nc.vector.tensor_copy(QT[0:KQ, bass.ds(b * NT + i, 1), :, :],
                                          ps[:, (6, 0)[i % 2]:(8, 2)[i % 2], :].bitcast(BF16)[0:KQ].rearrange("p a (h t) -> p (a h) t", t=P)
                                          ).then_inc(s["qt_ready"], 1)
                assert local[0] == LINKS
                dve.wait_ge(x_loaded[1], 16)
                dve.wait_ge(s["kx_transposed"], CREDIT + b + 1)
                nc.vector.tensor_copy(KT[0:KM, bass.ds(b, 1), :], bank(5).bitcast(BF16)[0:KM, :]).then_inc(s["kt_ready"], 1)
            chain[0] = B * LINKS

            def variances(b, sems):
                for t in range(b * NT, (b + 1) * NT):
                    ins = nc.vector.bn_aggr(mv3[:, t, :], stats3[:, t, :])
                link(ins)
                row = slice(b * NT, (b + 1) * NT)
                nc.vector.tensor_scalar(ve3[:, row], mv3[:, row, 1], EPS, None, ALU.add).then_inc(sems["var_ready"], 1)

            last_of_first_row = max(n for n, (b, _) in enumerate(items) if b == 0)

            for kind, n, k in order:
                b, i = items[n]
                if kind == "max":
                    h0, nh, s0, ns, c = max_tiles(i)[k]
                    r = ring_at[(kind, n, k)]
                    dve.wait_ge(smax_full, r + 1)
                    if k == 0 and n >= 2:
                        dve.wait_ge(mp_ready, n - 1)
                    two = chunks(i) == 2
                    last = k == len(max_tiles(i)) - 1
                    dst = nmx[:, n % 2, c, h0:h0 + nh] if two else nm[:, n % 2, h0:h0 + nh]
                    ins = nc.vector.tensor_reduce(dst, bank(4 + r % 2)[:, 0:nh * ns].rearrange("p (h s) -> p h s", h=nh),
                                                  AX_X, ALU.max, negate=True)
                    ins.then_inc(smax_free, 1)
                    if last and two:
                        dve.wait_ge(smax_free, maxima_to(r))
                        nc.vector.tensor_tensor(nm[:, n % 2, :], nmx[:, n % 2, 0, :], nmx[:, n % 2, 1, :],
                                                ALU.min).then_inc(nm_ready, 1)
                elif kind == "ytr":
                    y = bank(6 + n % 2).rearrange("p (a g v) -> p a g v", a=HG, g=G)
                    dve.wait_ge(yf_turned, n + 1)
                    if n >= 2:
                        dve.wait_ge(yn_transposed, n - 1)
                    ri = rinv[:, n % 2, :].rearrange("p (a g) -> p a g", a=HG)
                    link(nc.vector.reciprocal(ri, y[:, :, :, HD]))
                    nc.vector.tensor_tensor(YN[:, n % 2, :].rearrange("p (g a d) -> p a g d", g=G, a=HG), y[:, :, :, 0:HD],
                                            ri.unsqueeze(3).to_broadcast([P, HG, G, HD]), ALU.mult).then_inc(yn_ready, 1)
                elif kind == "proj":
                    t = b * NT + i
                    dve.wait_ge(proj_done, n + 1)
                    nc.vector.tensor_tensor(X[:, t, :], X[:, t, :], bank(6 + n % 2)[:, D:2 * D],
                                            ALU.add).then_inc(x1_ready, 1)
                    if n > 0:
                        dve.wait_ge(x1_ready, n)
                        pb, pi = items[n - 1]
                        ins = nc.vector.bn_stats(stats3[:, pb * NT + pi, :], X[:, pb * NT + pi, :])
                        if n - 1 == last_of_first_row:
                            link(ins)
                            variances(0, v)

            def stepper(b, base, per):
                local = [0]

                def step(ins):
                    local[0] += 1
                    assert local[0] <= per
                    ins.then_inc(dve_chain, 1)
                    dve.wait_ge(dve_chain, b * per + (base + local[0]))
                return step

            dve.wait_ge(x1_ready, N)
            pb, pi = items[N - 1]
            link(nc.vector.bn_stats(stats3[:, pb * NT + pi, :], X[:, pb * NT + pi, :]))
            variances(1, v)
            with dve.Fori(0, B) as b:
                dve.wait_ge(v["rstd_ready"], CREDIT + b + 1)
                dve.wait_ge(v["xn_transposed"], CREDIT + b * NT)
                for i in range(NT):
                    t = bass.ds(b * NT + i, 1)
                    nc.vector.tensor_scalar(XN[:, i:i + 1, :], X[:, t, :], mv3[:, t, 0], rstd3[:, t],
                                            ALU.subtract, ALU.mult).then_inc(v["xn_ready"], 1)
                middle_parts(b, 0, v)
                for i in range(NT):
                    if i + 1 < NT:
                        middle_parts(b, i + 1, v)
                    dve.wait_ge(v["qx_transposed"], CREDIT + b * NT + (i + 1))
                    nc.vector.tensor_copy(QT[0:KQ, bass.ds(b * NT + i, 1), :, :],
                                          ps[:, (6, 0)[i % 2]:(8, 2)[i % 2], :].bitcast(BF16)[0:KQ].rearrange("p a (h t) -> p (a h) t", t=P)
                                          ).then_inc(v["qt_ready"], 1)
            with dve.Fori(0, B) as b:
                for i in range(NT):
                    dve.wait_ge(v["smax_full"], CREDIT + b * NT + (i + 1))
                    dve.wait_ge(v["mp_ready"], CREDIT + b * NT + max(i - 1, 0))
                    nc.vector.tensor_reduce(nm[:, i % 2, 0:12].rearrange("p (a h) -> p a h", a=2),
                                            ps[:, 3 * (i % 2):3 * (i % 2) + 2, 0:6 * S].rearrange("p a (h s) -> p a h s", s=S),
                                            AX_X, ALU.max, negate=True)
                    nc.vector.tensor_reduce(nm[:, i % 2, 12:16], bank(3 * (i % 2) + 2)[:, 0:4 * S].rearrange("p (h s) -> p h s", s=S),
                                            AX_X, ALU.max, negate=True).then_inc(v["smax_free"], 1)
            for i in range(N + 4):
                if i < N:
                    nc.vector.tensor_tensor(X[:, i, :], X[:, i, :], bout[:], ALU.add)
                if 2 <= i <= N + 1:
                    t = i - 2
                    y = bank(t % 4).rearrange("p (a g v) -> p a g v", a=HG, g=G)
                    dve.wait_ge(v["yf_turned"], CREDIT + t + 1)
                    if t >= 2:
                        dve.wait_ge(v["yn_transposed"], CREDIT + t - 1)
                    ri = rinv[:, t % 2, :].rearrange("p (a g) -> p a g", a=HG)
                    link(nc.vector.reciprocal(ri, y[:, :, :, HD]))
                    nc.vector.tensor_tensor(YN[:, t % 2, :].rearrange("p (a g d) -> p a g d", g=G, a=HG), y[:, :, :, 0:HD],
                                            ri.unsqueeze(3).to_broadcast([P, HG, G, HD]), ALU.mult).then_inc(v["yn_ready"], 1)
                if i >= 4:
                    t = i - 4
                    dve.wait_ge(v["proj_done"], CREDIT + t + 1)
                    nc.vector.tensor_tensor(X[:, t, :], X[:, t, :], bank(t % 4)[:, D:2 * D],
                                            ALU.add).then_inc(v["x2_ready"], 1)
                if i >= 5:
                    t = i - 5
                    dve.wait_ge(v["x2_ready"], CREDIT + t + 1)
                    ins = nc.vector.bn_stats(stats3[:, t, :], X[:, t, :])
                    if t == NT - 1:
                        link(ins)
                        variances(0, rt)
                if 4 <= i < 4 + 2 * (E - EARLY):
                    k, m = divmod(i - 4, 2)
                    dve.wait_ge(w["hi_ready"], CREDIT + k + 1)
                    ins = nc.vector.scalar_tensor_tensor(out=W16[:, EARLY + k, m, 1, :],
                                                         in0=STG[k % 2].rearrange("p (m x) -> p m x", m=2)[:, m, :],
                                                         scalar=UP, in1=W16[:, EARLY + k, m, 0, :], op0=ALU.mult,
                                                         op1=ALU.subtract)
                    if m == 1:
                        ins.then_inc(w["lo_ready"], 1)
            dve.wait_ge(v["x2_ready"], CREDIT + N)
            link(nc.vector.bn_stats(stats3[:, N - 1, :], X[:, N - 1, :]))
            variances(1, rt)
            for t in range(N):
                if t % NT == 0:
                    dve.wait_ge(rt["rstd_ready"], CREDIT + t // NT + 1)
                nc.vector.tensor_scalar(XN3[:, t, :], X[:, t, :], mv3[:, t, 0:1], rstd3[:, t:t + 1],
                                        ALU.subtract, ALU.mult).then_inc(rt["xn_ready"], 1)

            def low_parts(k):
                dve.wait_ge(w["hi_ready"], CREDIT + E - EARLY + k + 1)
                nc.vector.scalar_tensor_tensor(out=W16[:, k, :, 1, :], in0=STG[k % 2].rearrange("p (m x) -> p m x", m=2),
                                               scalar=UP, in1=W16[:, k, :, 0, :], op0=ALU.mult,
                                               op1=ALU.subtract).then_inc(w["lo_ready"], 1)

            for k in range(MIDDLE):
                low_parts(k)

            def wide(a):
                return a.unsqueeze(2).to_broadcast([P, N, E])

            l3 = bank(2)[:, 0:N * E].rearrange("p (n e) -> p n e", e=E)
            dve.wait_ge(rt["lg_done"], CREDIT + N)
            link(nc.vector.tensor_reduce(lmax[:], l3, AX_X, ALU.max))
            nc.vector.tensor_tensor(lg[:], l3, wide(lmax[:]), ALU.subtract).then_inc(rt["lg_ready"], 1)
            dve.wait_ge(rt["ex_ready"], CREDIT + 1)
            link(nc.vector.tensor_reduce(lsum[:], ex[:], AX_X, ALU.add))
            link(nc.vector.reciprocal(lmax[:], lsum[:]))
            link(nc.vector.tensor_tensor(pr[:], ex[:], wide(lmax[:]), ALU.mult))
            for t in range(N):
                ins = nc.vector.max(top[:, t, :], pr[:, t, :])
            link(ins)
            for t in range(N):
                ins = nc.vector.max_index(tix[:, t, :], top[:, t, :], pr[:, t, :])
            link(ins)
            nc.vector.tensor_copy(rank[:], tix[:, :, 0:2])
            link(nc.vector.tensor_tensor(wsum[:], top[:, :, 0], top[:, :, 1], ALU.add))
            link(nc.vector.tensor_scalar(wsum[:], wsum[:], 1e-10, None, ALU.max))
            link(nc.vector.reciprocal(lsum[:], wsum[:]))
            nc.vector.tensor_tensor(wts[:], top[:, :, 0:2], lsum[:].unsqueeze(2).to_broadcast([P, N, 2]), ALU.mult)
            for k in range(2):
                ins = nc.vector.tensor_tensor(hot[:, k], iotaf[:, 0:E].unsqueeze(1).to_broadcast([P, N, E]),
                                              wide(rank[:, :, k]), ALU.is_equal)
            link(ins)
            nc.vector.tensor_tensor(hotb[:], hot[:, 0], hot[:, 1], ALU.add).then_inc(rt["hot_ready"], 1)
            low_parts(MIDDLE)
            dve.wait_ge(ranked, 1)
            link(nc.vector.tensor_copy(cnt[:], bank(4)[:, 0:E]))
            link(nc.vector.scalar_tensor_tensor(out=levels, in0=iotaf[:, 0:LEVELS].unsqueeze(1).to_broadcast([P, E, LEVELS]),
                                                scalar=float(P), in1=cnt[:].unsqueeze(2).to_broadcast([P, E, LEVELS]),
                                                op0=ALU.mult, op1=ALU.is_lt))
            link(nc.vector.tensor_reduce(tiles[:], levels, AX_X, ALU.add))
            link(nc.vector.tensor_tensor(earlier[:], earlier[:], tiles[:].unsqueeze(1).to_broadcast([P, E, E]), ALU.mult))
            link(nc.vector.tensor_reduce(first[:], earlier[:], AX_X, ALU.add))
            nc.vector.tensor_tensor(upto[:], first[:], tiles[:], ALU.add)
            link(nc.vector.scalar_tensor_tensor(out=place_of, in0=first[:].unsqueeze(1).to_broadcast([P, N, E]),
                                                scalar=float(P), in1=bank(3)[:, 0:N * E].rearrange("p (n e) -> p n e", e=E),
                                                op0=ALU.mult, op1=ALU.add))
            for k in range(2):
                ins = nc.vector.tensor_tensor(hot[:, k], hot[:, k], place_of, ALU.mult)
            link(ins)
            link(nc.vector.tensor_reduce(slotf[:], hot[:], AX_X, ALU.add))
            link(nc.vector.tensor_copy(slot[:], slotf[:]))
            link(nc.vector.tensor_scalar(slotq[:], slot[:], P.bit_length() - 1, None, ALU.logical_shift_right))
            link(nc.vector.tensor_copy(slotqf[:], slotq[:]))
            nc.vector.scalar_tensor_tensor(out=slotr[:], in0=slotqf[:], scalar=-float(P), in1=slotf[:], op0=ALU.mult,
                                           op1=ALU.add).then_inc(slot_ready, 1)
            low_parts(MIDDLE + 1)
            dve.wait_ge(slot_ready, 1)
            link(nc.vector.tensor_tensor(is_tile, iotaf[:, 0:NX].unsqueeze(1).to_broadcast([P, 2 * N, NX]),
                                         slotqf[:].rearrange("p k n -> p (k n)").unsqueeze(2).to_broadcast([P, 2 * N, NX]),
                                         ALU.is_equal))
            for k in range(2):
                nc.vector.tensor_tensor(token_at[:, k * N:(k + 1) * N, :], is_tile[:, k * N:(k + 1) * N, :],
                                        token[:].unsqueeze(2).to_broadcast([P, N, NX]), ALU.mult)
            nc.vector.tensor_tensor(is_row, iotaf[:].unsqueeze(1).to_broadcast([P, 2 * N, P]),
                                    slotr[:].rearrange("p k n -> p (k n)").unsqueeze(2).to_broadcast([P, 2 * N, P]),
                                    ALU.is_equal).then_inc(inverse_ready, 1)
            link(nc.vector.tensor_tensor(tilesum, iotaf[0:1, 0:NX].unsqueeze(2).to_broadcast([1, NX, E]),
                                         upto[0:1, :].unsqueeze(1).to_broadcast([1, NX, E]), ALU.is_ge))
            link(nc.vector.tensor_reduce(tef[:], tilesum, AX_X, ALU.add))
            link(nc.vector.tensor_scalar(tef[:], tef[:], float(E - 1), None, ALU.min))
            nc.vector.tensor_copy(TE[:], tef[:])
            link(nc.vector.scalar_tensor_tensor(out=teh[:, 0:NX - 1], in0=tef[:, 1:NX], scalar=float(E), in1=tef[:, 0:NX - 1],
                                                op0=ALU.mult, op1=ALU.add))
            nc.vector.scalar_tensor_tensor(out=TE4[:, 0:NX - 3], in0=teh[:, 2:NX - 1], scalar=float(E * E), in1=teh[:, 0:NX - 3],
                                           op0=ALU.mult, op1=ALU.add).then_inc(te_ready, 1)
            dve.wait_ge(inverted, 1)
            nc.vector.tensor_scalar(index[:], bank(5)[:, 0:NX], float(N * P - 1), None, ALU.min).then_inc(index_ready, 1)
            for k in range(MIDDLE + 2, EARLY):
                low_parts(k)

            def turn(u, c):
                dve.wait_ge(e["xh_ready"], CREDIT + u * 2 + (c + 1))
                nc.vector.scalar_tensor_tensor(out=X16[:, c % 2, 1, :, :], in0=bank(c % 2)[:, 0:D].rearrange("p (c t) -> p c t", c=C),
                                               scalar=UP, in1=X16[:, c % 2, 0, :, :], op0=ALU.mult,
                                               op1=ALU.subtract).then_inc(e["xl_ready"], 1)

            def hidden(u, c):
                dve.wait_ge(e["hh_ready"], CREDIT + u * 2 + (c + 1))
                nc.vector.scalar_tensor_tensor(out=H16[:, c % 2, 1, :], in0=HF[:, c % 2, :], scalar=UP, in1=H16[:, c % 2, 0, :],
                                               op0=ALU.mult, op1=ALU.subtract).then_inc(e["hl_ready"], 1)

            def give(u, c):
                ex_ = dve.value_load(TE[0:1, bass.ds(u * 2 + c, 1)], min_val=0, max_val=E - 1)
                dve.wait_ge(e["down_done"], CREDIT + u * 2 + (c + 1))
                if not isinstance(u, int) or u * 2 + c >= 2:
                    dve.wait_ge(ys_stored[c % 2], CREDIT + u * 16 + 16 * (c // 2))
                nc.vector.scalar_tensor_tensor(out=YS[:, c % 2:c % 2 + 1, :], in0=bank(4 + c % 2)[:, 0:D].unsqueeze(1),
                                               scalar=1.0 / (UP * UP), in1=b2all[:, bass.ds(ex_, 1), :],
                                               op0=ALU.mult, op1=ALU.add).then_inc(e["y_ready"], 1)

            dve.wait_ge(te_ready, 1)
            dve.wait_ge(b2_loaded, 16)
            turn(0, 0)
            turn(0, 1)
            hidden(0, 0)
            with dve.Fori(0, (NX - 3) // 2) as u:
                for c in (1, 2):
                    turn(u, c + 1)
                    hidden(u, c)
                    give(u, c - 1)
            turn(0, NX - 1)
            hidden(0, NX - 2)
            give(0, NX - 3)
            hidden(0, NX - 1)
            give(0, NX - 2)
            give(0, NX - 1)

            for g in range(GROUPS):
                dve.wait_ge(returned[g], 16 * 2 * (N // GROUPS))
                group = slice(g * (N // GROUPS), (g + 1) * (N // GROUPS))
                for k, into in ((0, XN3), (1, FINAL)):
                    for n in range(N)[group]:
                        ins = nc.vector.scalar_tensor_tensor(out=FINAL[:, n, :], in0=RET[:, k, n, :], scalar=wts[:, n, k:k + 1],
                                                             in1=into[:, n, :], op0=ALU.mult, op1=ALU.add)
                    link(ins)
                link(nc.vector.tensor_scalar(FINAL[:, group, :], FINAL[:, group, :], 100.0, -100.0, ALU.min, ALU.max))
                nc.vector.tensor_tensor(FINAL[:, group, :], FINAL[:, group, :], X[:, group, :], ALU.add).then_inc(fin_ready, 1)

        @block.tensor
        def _(pe):
            mm, tr = nc.tensor.matmul, nc.tensor.transpose
            pe.wait_ge(s["consts"], 1)
            pe.wait_ge(s["ctx_loaded"], 32)
            pe.wait_ge(s_small, 96)
            for b in range(B):
                for c in range(C):
                    tr(bank(0)[:, (b * C + c) * S:(b * C + c + 1) * S], CX[:, b, c * P:(c + 1) * P], ident[0:S, 0:S])
            for c in range(C):
                ins = tr(bank(1)[:, c * E:(c + 1) * E], gaterow[:, c * P:(c + 1) * P], ident[0:E, 0:E])
            for c in range(FC):
                ins = tr(bank(1)[:, (C + c) * E:(C + c + 1) * E], b1row[:, c * P:(c + 1) * P], ident[0:E, 0:E])
            ins.then_inc(s["cx_transposed"], 1)
            pe.wait_ge(s["w_loaded"], 64)
            pe.wait_ge(s["ct_ready"], CREDIT + 3)
            with pe.Fori(0, B) as b:
                for i in range(NT):
                    pe.wait_ge(s["xn_ready"], CREDIT + b * NT + (i + 1))
                    pe.wait_ge(s["xt_ready"], CREDIT + b * NT + max(i - 1, 0))
                    if i == 0:
                        pe.wait_ge(s["qt_ready"], CREDIT + b * NT)
                    for c in range(C):
                        ins = tr(bank(i % 2)[:, c * P:(c + 1) * P], XN[:, i, c * P:(c + 1) * P], ident[:])
                    ins.then_inc(s["xn_transposed"], 1)
                    if i % 4 == 3:
                        g = i // 4
                        pe.wait_ge(s["xt_ready"], CREDIT + b * NT + (i + 1))
                        pe.wait_ge(s["lat_ready"], CREDIT + b * 2 + g)
                        for c in range(C):
                            ins = mm(bank(2), wdown[:, c, :], XT[:, c, g * 512:(g + 1) * 512], start=c == 0, stop=c == C - 1)
                        ins.then_inc(s["lat_done"], 1)
                for i in range(NT + 1):
                    if i < NT:
                        pe.wait_ge(s["lat_ready"], CREDIT + b * 2 + (i // 4 + 1))
                        pe.wait_ge(s["qh_ready"], CREDIT + b * NT + max(i - 1, 0))
                        mm(bank(3 + i % 2)[:, 0:D + 2 * HD], LT[:, i * P:(i + 1) * P], wqkvup[:], start=True,
                           stop=True).then_inc(s["qkv_done"], 1)
                    if i >= 1:
                        t = i - 1
                        pe.wait_ge(s["qx_ready"], CREDIT + b * NT + (t + 1))
                        pe.wait_ge(s["qt_ready"], CREDIT + b * NT + max(t - 1, 0))
                        if t == 1:
                            pe.wait_ge(s["xt_ready"], CREDIT + b * NT + NT)
                        for h in range(H):
                            ins = tr(bank((6, 0)[t % 2] + h // 8).bitcast(BF16)[0:KQ, (h % 8) * P:(h % 8 + 1) * P],
                                     QX[:, t % 2, h, :, :].rearrange("p r d -> p (r d)"), identb[:])
                        ins.then_inc(s["qx_transposed"], 1)
                pe.wait_ge(s["kx_ready"], CREDIT + b + 1)
                pe.wait_ge(s["kt_ready"], CREDIT + b)
                for i in range(NT):
                    ins = tr(bank(5).bitcast(BF16)[0:KM, i * P:(i + 1) * P], KX[:, i, 0:KM], identb[:])
                ins.then_inc(s["kx_transposed"], 1)
            pe.wait_ge(s["qt_ready"], CREDIT + N)
            for b in range(B):
                mm(bank(b)[0:S, :], ones1[0:1, 0:S], bqkv[0:1, D:3 * D], start=True, stop=False)
                for c in range(C):
                    ins = mm(bank(b)[0:S, :], CT[:, b, c, :], wqkv[:, c, D:3 * D], start=False, stop=c == C - 1)
                ins.then_inc(s["kv2_done"], 1)
            pe.wait_ge(s["kv2_ready"], CREDIT + B)
            pe.wait_ge(s["kt_ready"], CREDIT + B)
            pe.wait_ge(s["qh_ready"], CREDIT + N)

            for kind, n, k in order:
                b, i = items[n]
                t = b * NT + i
                r = ring_at.get((kind, n, k))
                if r is not None and r >= 2:
                    prev = ring[r - 2]
                    if prev[0] == "max":
                        pe.wait_ge(smax_free, maxima_to(r - 2))
                    else:
                        pe.wait_ge(mt_ready, prev[1] + 1)
                if kind == "max":
                    h0, nh, s0, ns, c = max_tiles(i)[k]
                    diag = s0 + ns == (i + 1) * P
                    for a in range(nh):
                        ins = mm(bank(4 + r % 2)[:, a * ns:(a + 1) * ns], QT[0:KQ, t, h0 + a, :], KT[0:KQ, b, s0:s0 + ns],
                                 start=a == 0, stop=not diag and a == nh - 1, skip_group_check=True)
                        if diag:
                            ins = mm(bank(4 + r % 2)[:, (a + 1) * ns - P:(a + 1) * ns], identb[:], mask_ts[:],
                                     start=False, stop=a == nh - 1, skip_group_check=True)
                    ins.then_inc(smax_full, 1)
                elif kind == "mt":
                    pe.wait_ge(mp_ready, n + 1)
                    tr(bank(4 + r % 2).bitcast(BF16)[0:3 * H, 0:P], MP[:, n % 2, :, :].rearrange("p k h -> p (k h)"),
                       identb[:]).then_inc(smax_full, 1)
                elif kind == "st":
                    q = pair_at[(n, k)]
                    if k == 0:
                        pe.wait_ge(mrows[n % 2], 48 * (n // 2 + 1))
                    if q >= 2:
                        pe.wait_ge(p_ready, q - 1)
                    for u, (g, j) in enumerate(pairs(i)[k]):
                        o = bank(2 * (q % 2) + u)
                        ins = mm(o, KT[0:KM, b, j * P:(j + 1) * P], QT[0:KM, t, g * HG:(g + 1) * HG, :],
                                 start=True, stop=j < i)
                        if j == i:
                            ins = mm(o, identb[:], mask_st[:].unsqueeze(1).to_broadcast([P, HG, P]), start=False, stop=True)
                    ins.then_inc(st_full, 1)
                elif kind == "pv":
                    q = pair_at[(n, k)]
                    pe.wait_ge(p_ready, q + 1)
                    if k == 0 and n >= 2:
                        pe.wait_ge(x1_ready, n - 1)
                    for u, (g, j) in enumerate(pairs(i)[k]):
                        ins = mm(bank(6 + n % 2)[32 * g:32 * g + 32, :], VX[:, b * NT + j, :], PR[:, q % 3, u, :],
                                 start=j == 0, stop=j == i)
                    ins.then_inc(pv_done, 1)
                elif kind == "ytr":
                    pe.wait_ge(yf_ready, n + 1)
                    for a in range(HG):
                        ins = tr(bank(6 + n % 2)[:, a * P:(a + 1) * P], YF[:, n % 2, a * P:(a + 1) * P], ident[:])
                    ins.then_inc(yf_turned, 1)
                elif kind == "yt":
                    pe.wait_ge(yn_ready, n + 1)
                    for c in range(C):
                        ins = tr(bank(6 + n % 2)[:, c * P:(c + 1) * P], YN[:, n % 2, c * P:(c + 1) * P], ident[:])
                    ins.then_inc(yn_transposed, 1)
                elif kind == "proj":
                    pe.wait_ge(yt_ready, n + 1)
                    for c in range(C):
                        ins = mm(bank(6 + n % 2)[:, D:2 * D], YT[:, n % 2, c, :], wproj[:, c, :], start=c == 0, stop=c == C - 1)
                    ins.then_inc(proj_done, 1)
            pe.wait_ge(x1_ready, N)
            pe.wait_ge(p_ready, len(pair_at))
            for b in range(B):
                pe.wait_ge(s["kx2_ready"], CREDIT + b + 1)
                for h in range(H):
                    ins = tr(bank(4 + 2 * b + h // 8).bitcast(BF16)[0:KM, (h % 8) * SP:(h % 8) * SP + S],
                             KX2[:, b, h, 0:KM], identb[0:S, 0:S])
                ins.then_inc(s["kx2_transposed"], 1)
            with pe.Fori(0, B) as b:
                for i in range(NT):
                    pe.wait_ge(v["xn_ready"], CREDIT + b * NT + (i + 1))
                    pe.wait_ge(v["xt_ready"], CREDIT + b * NT + max(i - 1, 0))
                    if i == 0:
                        pe.wait_ge(v["qt_ready"], CREDIT + b * NT)
                    for c in range(C):
                        ins = tr(bank(i % 2)[:, c * P:(c + 1) * P], XN[:, i, c * P:(c + 1) * P], ident[:])
                    ins.then_inc(v["xn_transposed"], 1)
                for i in range(NT + 1):
                    if i < NT:
                        pe.wait_ge(v["xt_ready"], CREDIT + b * NT + (i + 1))
                        pe.wait_ge(v["qh_ready"], CREDIT + b * NT + max(i - 1, 0))
                        mm(bank(3 + i % 2)[:, 0:D], ones1[0:1, :], bqkv[0:1, 0:D], start=True, stop=False)
                        for c in range(C):
                            ins = mm(bank(3 + i % 2)[:, 0:D], XT[:, c, i * P:(i + 1) * P], wqkv[:, c, 0:D], start=False,
                                     stop=c == C - 1)
                        ins.then_inc(v["q_done"], 1)
                    if i >= 1:
                        t = i - 1
                        pe.wait_ge(v["qx_ready"], CREDIT + b * NT + (t + 1))
                        pe.wait_ge(v["qt_ready"], CREDIT + b * NT + max(t - 1, 0))
                        if t == 1:
                            pe.wait_ge(v["xt_ready"], CREDIT + b * NT + NT)
                        for h in range(H):
                            ins = tr(bank((6, 0)[t % 2] + h // 8).bitcast(BF16)[0:KQ, (h % 8) * P:(h % 8 + 1) * P],
                                     QX[:, t % 2, h, :, :].rearrange("p r d -> p (r d)"), identb[:])
                        ins.then_inc(v["qx_transposed"], 1)
            pe.wait_ge(v["qt_ready"], CREDIT + N)
            pe.wait_ge(s["kt2_ready"], CREDIT + B)
            pe.wait_ge(v["xt_ready"], CREDIT + N)
            pe.wait_ge(v["qh_ready"], CREDIT + N)
            for i in range(N + 2):
                if i < N:
                    if i >= 2:
                        pe.wait_ge(v["smax_free"], CREDIT + i - 1)
                    for h in range(H):
                        ins = mm(bank(3 * (i % 2) + h // 6)[:, (h % 6) * S:(h % 6 + 1) * S], QT[0:KQ, i, h, :],
                                 KT2[0:KQ, i // NT, h, 0:S], start=h % 6 == 0, stop=h % 6 == 5 or h == H - 1,
                                 skip_group_check=True)
                    ins.then_inc(v["smax_full"], 1)
                if i >= 2:
                    t = i - 2
                    pe.wait_ge(v["mp_ready"], CREDIT + t + 1)
                    if t >= 2:
                        pe.wait_ge(v["mt_ready"], CREDIT + t - 1)
                    mm(bank(6 + t % 2)[0:3 * H, 0:P], MP[:, t % 2, :, :].rearrange("p k h -> p (k h)"),
                       identb[:], start=True, stop=True).then_inc(v["mt_full"], 1)
            pe.wait_ge(v["mt_ready"], CREDIT + N)
            pe.wait_ge(v["smax_free"], CREDIT + N)
            for i in range(N + 4):
                if i < N:
                    b = i // NT
                    pe.wait_ge(vrows[i % 2], CREDIT + 48 * (i // 2 + 1))
                    for q in (2 * i, 2 * i + 1):
                        if q >= 2:
                            pe.wait_ge(v["p_ready"], CREDIT + q - 1)
                        for a in range(8):
                            h = (q % 2) * 8 + a
                            ins = mm(bank(4 + 2 * (q % 2) + a // 4)[0:S, (a % 4) * P:(a % 4 + 1) * P], KT2[0:KM, b, h, 0:S],
                                     QT[0:KM, i, h, :], start=a % 4 == 0, stop=a % 4 == 3, skip_group_check=True)
                        ins.then_inc(v["st_full"], 1)
                if 1 <= i <= N:
                    t = i - 1
                    b = t // NT
                    if t >= 4:
                        pe.wait_ge(v["x2_ready"], CREDIT + t - 3)
                    for q in (2 * t, 2 * t + 1):
                        pe.wait_ge(v["p_ready"], CREDIT + q + 1)
                        for a in range(8):
                            h = (q % 2) * 8 + a
                            g, k = h % 4, h // 4
                            ins = mm(bank(t % 4)[32 * g:32 * g + 32, k * P:(k + 1) * P], V2X[:, b, h, :],
                                     PR[0:S, q % 3, a // 4, (a % 4) * P:(a % 4 + 1) * P], start=k == 0, stop=k == 3,
                                     skip_group_check=True)
                        ins.then_inc(v["pv_done"], 1)
                if 2 <= i <= N + 1:
                    t = i - 2
                    pe.wait_ge(v["yf_ready"], CREDIT + t + 1)
                    for a in range(HG):
                        ins = tr(bank(t % 4)[:, a * P:(a + 1) * P], YF[:, t % 2, a * P:(a + 1) * P], ident[:])
                    ins.then_inc(v["yf_turned"], 1)
                if 3 <= i <= N + 2:
                    t = i - 3
                    pe.wait_ge(v["yn_ready"], CREDIT + t + 1)
                    for c in range(C):
                        ins = tr(bank(t % 4)[:, c * P:(c + 1) * P], YN[:, t % 2, c * P:(c + 1) * P], ident[:])
                    ins.then_inc(v["yn_transposed"], 1)
                if i >= 4:
                    t = i - 4
                    pe.wait_ge(v["yt_ready"], CREDIT + t + 1)
                    for c in range(C):
                        ins = mm(bank(t % 4)[:, D:2 * D], YT[:, t % 2, c, :], wout[:, c, :], start=c == 0, stop=c == C - 1)
                    ins.then_inc(v["proj_done"], 1)
            pe.wait_ge(v["x2_ready"], CREDIT + N)
            LAG = 3
            for i in range(N + LAG):
                if i < N:
                    pe.wait_ge(rt["xn_ready"], CREDIT + i + 1)
                    if i >= 4:
                        pe.wait_ge(rt["xt_ready"], CREDIT + i - 3)
                    for c in range(C):
                        ins = tr(bank(4 + i % 4)[:, c * P:(c + 1) * P], XN3[:, i, c * P:(c + 1) * P], ident[:])
                    ins.then_inc(rt["xn_transposed"], 1)
                if i >= LAG:
                    t = i - LAG
                    pe.wait_ge(rt["xt_ready"], CREDIT + t + 1)
                    for c in range(C):
                        ins = mm(bank(2)[:, t * E:(t + 1) * E], XT[:, c, (t % NT) * P:(t % NT + 1) * P], gateT[:, c, :],
                                 start=t == 0 and c == 0, stop=c == C - 1, skip_group_check=True)
                    ins.then_inc(rt["lg_done"], 1)
            pe.wait_ge(rt["hot_ready"], CREDIT + 1)
            for n in range(N - 1):
                mm(bank(3)[:, (n + 1) * E:N * E].rearrange("p (n e) -> p n e", e=E), onesb[:],
                   hotb[:, n:n + 1, :].to_broadcast([P, N - 1 - n, E]), start=n == 0, stop=False, skip_group_check=True)
            mm(bank(3)[:, 0:N * E], before[:], hotb[:].rearrange("p n e -> p (n e)"), start=False, stop=True,
               skip_group_check=True)
            for n in range(N):
                ins = mm(bank(4)[:, 0:E], onesb[:], hotb[:, n, :], start=n == 0, stop=n == N - 1)
            ins.then_inc(ranked, 1)
            pe.wait_ge(inverse_ready, 1)
            for m in range(2 * N):
                ins = mm(bank(5)[:, 0:NX], is_row[:, m, :], token_at[:, m, :], start=m == 0, stop=m == 2 * N - 1)
            ins.then_inc(inverted, 1)

            def turn(u, c):
                pe.wait_ge(xg_loaded[c % 2], u * 16 + 16 * (c // 2 + 1))
                if not isinstance(u, int) or u * 2 + c >= 2:
                    pe.wait_ge(e["xl_ready"], CREDIT + u * 2 + (c - 1))
                for k in range(C):
                    ins = tr(bank(c % 2)[:, k * P:(k + 1) * P], XG[:, c % 2, k * P:(k + 1) * P], ident[:])
                ins.then_inc(e["xg_transposed"], 1)

            PARTS = ((0, 0), (0, 1), (1, 0))

            def experts(u, c):
                x4 = pe.value_load(TE4[0:1, bass.ds(u * 2 + c, 1)], min_val=0, max_val=E ** 4 - 1)
                return [x4 % E, (x4 // E) % E, (x4 // E ** 2) % E, x4 // E ** 3]

            def hidden(u, c, ex_):
                pe.wait_ge(e["xl_ready"], CREDIT + u * 2 + (c + 1))
                if not isinstance(u, int) or u * 2 + c >= 2:
                    pe.wait_ge(e["act_ready"], CREDIT + u * 2 + (c - 1))
                for f in range(FC):
                    for k in range(C):
                        for q, (a, b) in enumerate(PARTS):
                            ins = mm(bank(2 + c % 2)[:, f * P:(f + 1) * P],
                                     W16[:, bass.ds(ex_, 1), 0, a, k * F + f * P:k * F + (f + 1) * P].rearrange("p e x -> p (e x)"),
                                     X16[:, c % 2, b, k, :], start=f == 0 and q == 0 and k == 0,
                                     stop=q == 2 and k == C - 1, skip_group_check=True)
                ins.then_inc(e["up_done"], 1)

            def give(u, c, ex_):
                pe.wait_ge(e["hl_ready"], CREDIT + u * 2 + (c + 1))
                if not isinstance(u, int) or u * 2 + c >= 2:
                    pe.wait_ge(e["y_ready"], CREDIT + u * 2 + (c - 1))
                for f in range(FC):
                    for q, (a, b) in enumerate(PARTS):
                        ins = mm(bank(4 + c % 2)[:, 0:D], H16[:, c % 2, a, f * P:(f + 1) * P],
                                 W16[:, bass.ds(ex_, 1), 1, b, f * D:(f + 1) * D].rearrange("p e x -> p (e x)"),
                                 start=f == 0 and q == 0, stop=f == FC - 1 and q == 2)
                ins.then_inc(e["down_done"], 1)

            pe.wait_ge(te_ready, 1)
            pe.wait_ge(w["lo_ready"], CREDIT + E)
            turn(0, 0)
            turn(0, 1)
            hidden(0, 0, experts(0, 0)[0])
            with pe.Fori(0, (NX - 3) // 6) as turns:
                u = turns * 3
                of = experts(u, 0)
                for c in range(1, 7):
                    turn(u, c + 1)
                    if c == 4:
                        of += experts(u, 4)
                    hidden(u, c, of[c])
                    give(u, c - 1, of[c - 1])
            turn(0, NX - 1)
            of = experts(0, NX - 4)[1:]
            hidden(0, NX - 2, of[1])
            give(0, NX - 3, of[0])
            hidden(0, NX - 1, of[2])
            give(0, NX - 2, of[1])
            give(0, NX - 1, of[2])


_INS = ['x', 'ctx_1024', 'L0_attn_Wc_down', 'L0_attn_Wq_up', 'L0_attn_Wkv_up', 'L0_attn_Wc_proj', 'L0_xattn_W_qkv',
        'L0_xattn_b_qkv', 'L0_xattn_W_out', 'L0_xattn_b_out', 'L0_ffn_gate_w', 'L0_ffn_w1', 'L0_ffn_b1', 'L0_ffn_w2',
        'L0_ffn_b2']
_OUTS = [((2, 1024, 256), 'float32')]


def kernel(**inputs):
    import numpy as _np
    import concourse.bacc as _bacc
    from concourse import mybir as _mybir
    from concourse.bass_utils import run_bass_kernel_spmd as _run

    nc = _bacc.Bacc("TRN2", target_bir_lowering=False, num_devices=1)
    arrays, args = {}, []
    for name in _INS:
        a = _np.ascontiguousarray(inputs[name])
        arrays[f"in_{name}_dram"] = a
        args.append(nc.dram_tensor(f"in_{name}_dram", a.shape, _mybir.dt.from_np(a.dtype), kind="ExternalInput").ap())
    for i, (shape, dtype) in enumerate(_OUTS):
        dt = _mybir.dt.from_np(_np.dtype(dtype))
        args.append(nc.dram_tensor(f"out_{i}_dram", shape, dt, kind="ExternalOutput").ap())
    decoder_layer(nc, *args)
    r = _run(nc, [arrays], core_ids=[0])
    got = tuple(r.results[0][f"out_{i}_dram"] for i in range(len(_OUTS)))
    return got[0]
```
